# Optimizing a Trainium2 kernel written in Bass

```python
import numpy as np
import jax
import jax.numpy as jnp

def _softmax(x, axis=-1):
    return jax.nn.softmax(x, axis=axis)

def _gelu(x):
    return jax.nn.gelu(x, approximate=True)

def _silu(x):
    return jax.nn.silu(x)

def _sigmoid(x):
    return jax.nn.sigmoid(x)

def _layernorm(x, axis=-1, eps=1e-05):
    m = jnp.mean(x, axis=axis, keepdims=True)
    v = jnp.var(x, axis=axis, keepdims=True)
    return (x - m) / jnp.sqrt(v + eps)

def _scatter_add(tgt, idx, src, axis=0):
    return tgt.at[idx].add(src)

def _segment_sum(src, seg, n):
    return jax.ops.segment_sum(src, seg, n)
kernel_name = 'mk_flamingo_gated_d4_seqx_r4_754fd3'

def setup_inputs(seed: int=0):
    np.random.seed(seed)
    _w = jnp.asarray

    def _rec_inputs():
        import jax
        import jax.numpy as jnp
        _rk = jax.random.key(seed)
        x = -0.0002928 + 1 * jax.random.normal(jax.random.fold_in(_rk, 1), (2, 1024, 256), jnp.float32)
        _lenS = 1024 - jax.random.randint(jax.random.fold_in(_rk, 7), (2,), 0, max(1, 1024 // 4) + 1, jnp.int32)
        _lenS2 = 77 - jax.random.randint(jax.random.fold_in(_rk, 8), (2,), 0, max(1, 77 // 4) + 1, jnp.int32)
        _ctx_1024P = jax.random.normal(jax.random.fold_in(_rk, 11), (2, 16, 256), jnp.float32)
        _ctx_1024c = jax.random.dirichlet(jax.random.fold_in(_rk, 511), 0.3 * jnp.ones((16,), jnp.float32), (2, 77))
        _ctx_1024t = jnp.einsum('bsk,bkd->bsd', _ctx_1024c, _ctx_1024P)
        _ctx_1024t = _ctx_1024t * jax.lax.rsqrt(jnp.mean(jnp.square(_ctx_1024t)) + 1e-12) * 0.953939
        ctx_1024 = -1.39393e-06 + 0.999914 * (_ctx_1024t + 0.3 * jax.random.normal(jax.random.fold_in(_rk, 611), (2, 77, 256), jnp.float32))
        fside_BxSxS2_0 = jax.random.uniform(jax.random.fold_in(_rk, 13), (2, 1024, 77), jnp.float32, 0.0, 0.999998)
        _validS = jnp.arange(1024)[None, :] < _lenS[:, None]
        _validS2 = jnp.arange(77)[None, :] < _lenS2[:, None]
        _causal = jnp.tril(jnp.ones((1024, 1024), dtype=bool))
        mask_Bx1xSxS2_ff0 = jnp.where(jnp.ones((2, 1, 1024, 77), dtype=bool), 0.0, -1000000000.0).astype(jnp.float32)
        mask_Bx1x1xS2_ff0 = jnp.where(jnp.ones((2, 1, 1, 77), dtype=bool), 0.0, -1000000000.0).astype(jnp.float32)
        mask_Bx1xSxS2_ik1 = jnp.where(jnp.broadcast_to(_validS2[:, None, None, :], (2, 1, 1024, 77)), 1, 0).astype(jnp.int32)
        _g = jax.random.normal(jax.random.fold_in(_rk, 9001), (2, 4), jnp.float32)
        _g = jnp.sign(_g) * jnp.maximum(jnp.abs(_g), 1.0) + (_g == 0) * 1.0
        g_xattn = _g[0]
        g_ffn = _g[1]
        return (x, ctx_1024, fside_BxSxS2_0, mask_Bx1xSxS2_ff0, mask_Bx1x1xS2_ff0, mask_Bx1xSxS2_ik1, g_xattn, g_ffn)
    x, ctx_1024, fside_BxSxS2_0, mask_Bx1xSxS2_ff0, mask_Bx1x1xS2_ff0, mask_Bx1xSxS2_ik1, g_xattn, g_ffn = _rec_inputs()

    def _L0_xattn_setup():
        import jax, jax.numpy as jnp
        import numpy as np
        DEPTH = 64
        key = jax.random.key(seed)
        ks = jax.random.split(key, 7)
        B, F, T, H = (2, 512, 512, 256)
        N, D = (16, 64)
        s = 1.0 / np.sqrt(H)
        return {'query_input': jax.random.normal(ks[0], (B, F, H), jnp.float32), 'source_input': jax.random.normal(ks[1], (B, T, H), jnp.float32), 'bias': jnp.zeros((B, 1, F, T), jnp.float32), 'wq': jax.random.normal(ks[2], (H, N, D), jnp.float32) * s, 'wk': jax.random.normal(ks[3], (H, N, D), jnp.float32) * s, 'wv': jax.random.normal(ks[4], (H, N, D), jnp.float32) * s, 'wo': jax.random.normal(ks[5], (N, D, H), jnp.float32) * s}
    _L0_xattn_all = _L0_xattn_setup()
    _L0_xattn_in = {k: v for k, v in _L0_xattn_all.items() if k in ('wq', 'wk', 'wv', 'wo')}
    del _L0_xattn_all

    def _L0_ffn_setup():
        import jax, jax.numpy as jnp
        import numpy as np
        GROUP = 16
        EPS = 1e-05

        def _dequant(q, scale):
            w = q.astype(jnp.float32) / 7.5 - 1.0
            return w * jnp.repeat(scale, GROUP, axis=1)

        def _qlora_linear(x, q, scale, bias, la, lb):
            w = _dequant(q, scale)
            base = jnp.einsum('btd,od->bto', x, w) + bias
            lora = jnp.einsum('btr,or->bto', jnp.einsum('btd,rd->btr', x, la), lb)
            return base + lora

        def _layernorm(x, g, b):
            mu = jnp.mean(x, axis=-1, keepdims=True)
            var = jnp.mean(jnp.square(x - mu), axis=-1, keepdims=True)
            return (x - mu) * jax.lax.rsqrt(var + EPS) * g + b
        key = jax.random.key(seed)
        ks = jax.random.split(key, 6)
        D, R, B, T = (256, 32, 8, 1024)
        x = jax.random.normal(ks[0], (B, T, D), dtype=jnp.float32)
        qweights = jax.random.randint(ks[1], (6, D, D), 0, 16, dtype=jnp.int32)
        scales = jax.random.uniform(ks[2], (6, D, D // GROUP), dtype=jnp.float32)
        biases = jax.random.normal(ks[3], (6, D), dtype=jnp.float32) * 0.02
        lora_a = jax.random.normal(ks[4], (6, R, D), dtype=jnp.float32) * 0.02
        lora_b = jax.random.normal(ks[5], (6, D, R), dtype=jnp.float32) * 0.02
        ln_gamma = jnp.ones((3, D), dtype=jnp.float32)
        ln_beta = jnp.zeros((3, D), dtype=jnp.float32)
        return {'x': x, 'qweights': qweights, 'scales': scales, 'biases': biases, 'lora_a': lora_a, 'lora_b': lora_b, 'ln_gamma': ln_gamma, 'ln_beta': ln_beta}
    _L0_ffn_all = _L0_ffn_setup()
    _L0_ffn_in = {k: v for k, v in _L0_ffn_all.items() if k in ('qweights', 'scales', 'biases', 'lora_a', 'lora_b', 'ln_gamma', 'ln_beta')}
    del _L0_ffn_all

    def _L1_xattn_setup():
        import jax, jax.numpy as jnp
        import numpy as np
        B, F, T = (2, 128, 128)
        D, N, H = (256, 16, 64)
        K = 32
        FILT = 1024
        L = 4
        EPS = 1e-06

        def _glorot(key, shape, fan_in, fan_out):
            lim = np.sqrt(6.0 / (fan_in + fan_out)).astype(np.float32)
            return jax.random.uniform(key, shape, jnp.float32, -lim, lim)

        def _norm(x):
            m = jnp.mean(x, axis=-1, keepdims=True)
            s = jnp.sqrt(jnp.mean((x - m) ** 2, axis=-1, keepdims=True))
            return (x - m) / (s + EPS)

        def _attention(x, src, dist, bias, Wq, Wk, Wv, Wo, Wth, bth, Wto, bto):
            q = jnp.einsum('bfd,dnh->bfnh', x, Wq) * H ** (-0.5)
            k = jnp.einsum('btd,dnh->btnh', src, Wk)
            v = jnp.einsum('btd,dnh->btnh', src, Wv)
            hbias = jax.nn.relu(dist[..., None] @ Wth + bth)
            qs_bias = (hbias @ Wto + bto)[..., 0]
            logits = jnp.einsum('btnh,bfnh->bnft', k, q)
            logits = logits + bias + qs_bias[:, None]
            w = jax.nn.softmax(logits, axis=-1)
            out = jnp.einsum('bnft,btnh->bfnh', w, v)
            return jnp.einsum('bfnh,nhd->bfd', out, Wo)
        key = jax.random.key(seed)
        ks = jax.random.split(key, 18)
        inp = {'decoder_inputs': jax.random.normal(ks[0], (B, F, D), jnp.float32), 'encoder_outputs': jax.random.normal(ks[1], (B, T, D), jnp.float32), 'decoder_times_dist': jax.random.uniform(ks[2], (B, F, F), jnp.float32), 'decoder_encoder_times_dist': jax.random.uniform(ks[3], (B, F, T), jnp.float32), 'dec_self_attn_bias': jnp.zeros((B, 1, 1, F), jnp.float32), 'enc_dec_attn_bias': jnp.zeros((B, 1, 1, T), jnp.float32), 'Wq': _glorot(ks[4], (L, D, N, H), D, D), 'Wk': _glorot(ks[5], (L, D, N, H), D, D), 'Wv': _glorot(ks[6], (L, D, N, H), D, D), 'Wo': _glorot(ks[7], (L, N, H, D), D, D), 'Wth': _glorot(ks[8], (L, 1, K), 1, K), 'bth': jnp.zeros((L, K), jnp.float32), 'Wto': _glorot(ks[9], (L, K, 1), K, 1), 'bto': jnp.zeros((L, 1), jnp.float32), 'Wf1': _glorot(ks[10], (L, D, FILT), D, FILT), 'bf1': jnp.zeros((L, FILT), jnp.float32), 'Wf2': _glorot(ks[11], (L, FILT, D), FILT, D), 'bf2': jnp.zeros((L, D), jnp.float32)}
        return inp
    _L1_xattn_all = _L1_xattn_setup()
    _L1_xattn_in = {k: v for k, v in _L1_xattn_all.items() if k in ('Wq', 'Wk', 'Wv', 'Wo', 'Wth', 'bth', 'Wto', 'bto', 'Wf1', 'bf1', 'Wf2', 'bf2')}
    del _L1_xattn_all

    def _L1_ffn_setup():
        import jax, jax.numpy as jnp
        import numpy as np
        TEMPERATURE = 0.5
        CAPACITY_FACTOR = 1.25
        TOP_K = 1
        key = jax.random.key(seed)
        ks = jax.random.split(key, 5)
        B, S, D, H, E = (4, 512, 256, 512, 8)
        s = 0.02
        return {'x': jax.random.normal(ks[0], (B, S, D), jnp.float32), 'gate_w': jax.random.normal(ks[1], (E, D), jnp.float32) * s, 'gate_b': jnp.zeros((E,), jnp.float32), 'rms_w': jnp.ones((E,), jnp.float32), 'w1': jax.random.normal(ks[2], (E, D, H), jnp.float32) * s, 'b1': jnp.zeros((E, H), jnp.float32), 'w2': jax.random.normal(ks[3], (E, H, D), jnp.float32) * s, 'b2': jnp.zeros((E, D), jnp.float32)}
    _L1_ffn_all = _L1_ffn_setup()
    _L1_ffn_in = {k: v for k, v in _L1_ffn_all.items() if k in ('gate_w', 'gate_b', 'rms_w', 'w1', 'b1', 'w2', 'b2')}
    del _L1_ffn_all

    def _L2_xattn_setup():
        import jax, jax.numpy as jnp
        import numpy as np
        EMBED = 256
        HEADS = 16
        HEAD_DIM = EMBED // HEADS
        B, S = (4, 512)
        key = jax.random.key(seed)
        ks = jax.random.split(key, 9)
        inp = {'values': jax.random.normal(ks[0], (B, S, EMBED), jnp.float32), 'keys': jax.random.normal(ks[1], (B, S, EMBED), jnp.float32), 'queries': jax.random.normal(ks[2], (B, S, EMBED), jnp.float32), 'mask': jax.random.randint(ks[3], (B, 1, S, S), 0, 2, jnp.int32), 'Wv': jax.random.normal(ks[4], (HEAD_DIM, HEAD_DIM), jnp.float32) / np.sqrt(HEAD_DIM), 'Wk': jax.random.normal(ks[5], (HEAD_DIM, HEAD_DIM), jnp.float32) / np.sqrt(HEAD_DIM), 'Wq': jax.random.normal(ks[6], (HEAD_DIM, HEAD_DIM), jnp.float32) / np.sqrt(HEAD_DIM), 'Wo': jax.random.normal(ks[7], (EMBED, EMBED), jnp.float32) / np.sqrt(EMBED), 'bo': jax.random.normal(ks[8], (EMBED,), jnp.float32) * 0.01}
        return inp
    _L2_xattn_all = _L2_xattn_setup()
    _L2_xattn_in = {k: v for k, v in _L2_xattn_all.items() if k in ('Wv', 'Wk', 'Wq', 'Wo', 'bo')}
    del _L2_xattn_all

    def _L2_ffn_setup():
        import jax, jax.numpy as jnp
        import numpy as np
        H = 256
        I = 512
        E = 8
        B, S = (2, 256)

        def _swiglu(x, wg, wu, wd):
            return jax.nn.silu(x @ wg) * (x @ wu) @ wd
        key = jax.random.key(seed)
        ks = jax.random.split(key, 8)
        sc_h = 1.0 / np.sqrt(H)
        sc_i = 1.0 / np.sqrt(I)
        return {'hidden_states': jax.random.normal(ks[0], (B, S, H), jnp.float32), 'gate_w': jax.random.normal(ks[1], (H, E), jnp.float32) * sc_h, 'sh_gate': jax.random.normal(ks[2], (H, I), jnp.float32) * sc_h, 'sh_up': jax.random.normal(ks[3], (H, I), jnp.float32) * sc_h, 'sh_down': jax.random.normal(ks[4], (I, H), jnp.float32) * sc_i, 'rt_gate': jax.random.normal(ks[5], (E, H, I), jnp.float32) * sc_h, 'rt_up': jax.random.normal(ks[6], (E, H, I), jnp.float32) * sc_h, 'rt_down': jax.random.normal(ks[7], (E, I, H), jnp.float32) * sc_i}
    _L2_ffn_all = _L2_ffn_setup()
    _L2_ffn_in = {k: v for k, v in _L2_ffn_all.items() if k in ('gate_w', 'sh_gate', 'sh_up', 'sh_down', 'rt_gate', 'rt_up', 'rt_down')}
    del _L2_ffn_all

    def _L3_xattn_setup():
        import jax, jax.numpy as jnp
        import numpy as np
        import math
        EMBED_DIM = 256
        NUM_HEADS = 16
        D_K = EMBED_DIM // NUM_HEADS
        B, S_DEC, S_ENC = (4, 256, 512)
        key = jax.random.key(seed)
        ks = jax.random.split(key, 12)
        s = 1.0 / math.sqrt(EMBED_DIM)
        return {'Q_decoder': jax.random.normal(ks[0], (B, S_DEC, EMBED_DIM), jnp.float32), 'K_encoder': jax.random.normal(ks[1], (B, S_ENC, EMBED_DIM), jnp.float32), 'V_encoder': jax.random.normal(ks[2], (B, S_ENC, EMBED_DIM), jnp.float32), 'Wq': jax.random.normal(ks[3], (EMBED_DIM, EMBED_DIM), jnp.float32) * s, 'bq': jnp.zeros((EMBED_DIM,), jnp.float32), 'Wk': jax.random.normal(ks[4], (EMBED_DIM, EMBED_DIM), jnp.float32) * s, 'bk': jnp.zeros((EMBED_DIM,), jnp.float32), 'Wv': jax.random.normal(ks[5], (EMBED_DIM, EMBED_DIM), jnp.float32) * s, 'bv': jnp.zeros((EMBED_DIM,), jnp.float32), 'Wo': jax.random.normal(ks[6], (EMBED_DIM, EMBED_DIM), jnp.float32) * s, 'bo': jnp.zeros((EMBED_DIM,), jnp.float32)}
    _L3_xattn_all = _L3_xattn_setup()
    _L3_xattn_in = {k: v for k, v in _L3_xattn_all.items() if k in ('Wq', 'bq', 'Wk', 'bk', 'Wv', 'bv', 'Wo', 'bo')}
    del _L3_xattn_all

    def _L3_ffn_setup():
        import jax, jax.numpy as jnp
        import numpy as np
        B, S, D = (2, 256, 256)
        L, H = (128, 16)
        HD = L // H
        F, E, K = (512, 8, 2)
        THETA = 10000.0
        EPS = 1e-05

        def _rmsnorm(x, g):
            return x * g * jax.lax.rsqrt(jnp.mean(x * x, axis=-1, keepdims=True) + EPS)

        def _rope(t, pos):
            inv_freq = 1.0 / THETA ** (jnp.arange(0, HD, 2, dtype=jnp.float32) / HD)
            ang = pos[:, None].astype(jnp.float32) * inv_freq[None, :]
            cos, sin = (jnp.cos(ang), jnp.sin(ang))
            t1, t2 = (t[..., 0::2], t[..., 1::2])
            r1 = t1 * cos - t2 * sin
            r2 = t1 * sin + t2 * cos
            return jnp.stack([r1, r2], axis=-1).reshape(t.shape)

        def _forward(x, g1, g2, w_down, wq, wk, wv, w_up, router_w, w1, w2, w3):
            b, s, _ = x.shape
            pos = jnp.arange(s)
            h = _rmsnorm(x, g1)
            c = h @ w_down
            split = lambda t: t.reshape(b, s, H, HD).transpose(0, 2, 1, 3)
            q = _rope(split(c @ wq), pos)
            k = _rope(split(c @ wk), pos)
            v = split(c @ wv)
            scores = jnp.einsum('bhqd,bhkd->bhqk', q, k) / jnp.sqrt(jnp.float32(HD))
            causal = jnp.tril(jnp.ones((s, s), bool))
            scores = jnp.where(causal, scores, -jnp.inf)
            attn = jax.nn.softmax(scores, axis=-1)
            o = jnp.einsum('bhqk,bhkd->bhqd', attn, v).transpose(0, 2, 1, 3).reshape(b, s, L)
            x = x + o @ w_up
            res = x
            t = _rmsnorm(x, g2).reshape(-1, D)
            probs = jax.nn.softmax(t @ router_w, axis=-1)
            vals, idx = jax.lax.top_k(probs, K)
            w = vals / jnp.sum(vals, axis=-1, keepdims=True)
            gate = jnp.sum(jax.nn.one_hot(idx, E, dtype=t.dtype) * w[..., None], axis=1)
            hid = jax.nn.silu(jnp.einsum('td,edf->tef', t, w1)) * jnp.einsum('td,edf->tef', t, w3)
            y_e = jnp.einsum('tef,efd->ted', hid, w2)
            y = jnp.einsum('ted,te->td', y_e, gate)
            return res + y.reshape(b, s, D)
        key = jax.random.key(seed)
        ks = jax.random.split(key, 12)
        g = lambda k, shape, scale: jax.random.normal(k, shape, dtype=jnp.float32) * scale
        return {'x': g(ks[0], (B, S, D), 1.0), 'g1': jnp.ones((D,), jnp.float32), 'g2': jnp.ones((D,), jnp.float32), 'w_down': g(ks[1], (D, L), 0.02), 'wq': g(ks[2], (L, L), 0.02), 'wk': g(ks[3], (L, L), 0.02), 'wv': g(ks[4], (L, L), 0.02), 'w_up': g(ks[5], (L, D), 0.02), 'router_w': g(ks[6], (D, E), 0.02), 'w1': g(ks[7], (E, D, F), 0.02), 'w3': g(ks[8], (E, D, F), 0.02), 'w2': g(ks[9], (E, F, D), 0.02)}
    _L3_ffn_all = _L3_ffn_setup()
    _L3_ffn_in = {k: v for k, v in _L3_ffn_all.items() if k in ('g1', 'g2', 'w_down', 'wq', 'wk', 'wv', 'w_up', 'router_w', 'w1', 'w2', 'w3')}
    del _L3_ffn_all
    return {'x': x, 'ctx_1024': ctx_1024, 'fside_BxSxS2_0': fside_BxSxS2_0, 'mask_Bx1xSxS2_ff0': mask_Bx1xSxS2_ff0, 'mask_Bx1x1xS2_ff0': mask_Bx1x1xS2_ff0, 'mask_Bx1xSxS2_ik1': mask_Bx1xSxS2_ik1, 'g_xattn': g_xattn, 'g_ffn': g_ffn, 'L0_xattn_wq': _L0_xattn_in['wq'], 'L0_xattn_wk': _L0_xattn_in['wk'], 'L0_xattn_wv': _L0_xattn_in['wv'], 'L0_xattn_wo': _L0_xattn_in['wo'], 'L0_ffn_qweights': _L0_ffn_in['qweights'], 'L0_ffn_scales': _L0_ffn_in['scales'], 'L0_ffn_biases': _L0_ffn_in['biases'], 'L0_ffn_lora_a': _L0_ffn_in['lora_a'], 'L0_ffn_lora_b': _L0_ffn_in['lora_b'], 'L0_ffn_ln_gamma': _L0_ffn_in['ln_gamma'], 'L0_ffn_ln_beta': _L0_ffn_in['ln_beta'], 'L1_xattn_Wq': _L1_xattn_in['Wq'], 'L1_xattn_Wk': _L1_xattn_in['Wk'], 'L1_xattn_Wv': _L1_xattn_in['Wv'], 'L1_xattn_Wo': _L1_xattn_in['Wo'], 'L1_xattn_Wth': _L1_xattn_in['Wth'], 'L1_xattn_bth': _L1_xattn_in['bth'], 'L1_xattn_Wto': _L1_xattn_in['Wto'], 'L1_xattn_bto': _L1_xattn_in['bto'], 'L1_xattn_Wf1': _L1_xattn_in['Wf1'], 'L1_xattn_bf1': _L1_xattn_in['bf1'], 'L1_xattn_Wf2': _L1_xattn_in['Wf2'], 'L1_xattn_bf2': _L1_xattn_in['bf2'], 'L1_ffn_gate_w': _L1_ffn_in['gate_w'], 'L1_ffn_gate_b': _L1_ffn_in['gate_b'], 'L1_ffn_rms_w': _L1_ffn_in['rms_w'], 'L1_ffn_w1': _L1_ffn_in['w1'], 'L1_ffn_b1': _L1_ffn_in['b1'], 'L1_ffn_w2': _L1_ffn_in['w2'], 'L1_ffn_b2': _L1_ffn_in['b2'], 'L2_xattn_Wv': _L2_xattn_in['Wv'], 'L2_xattn_Wk': _L2_xattn_in['Wk'], 'L2_xattn_Wq': _L2_xattn_in['Wq'], 'L2_xattn_Wo': _L2_xattn_in['Wo'], 'L2_xattn_bo': _L2_xattn_in['bo'], 'L2_ffn_gate_w': _L2_ffn_in['gate_w'], 'L2_ffn_sh_gate': _L2_ffn_in['sh_gate'], 'L2_ffn_sh_up': _L2_ffn_in['sh_up'], 'L2_ffn_sh_down': _L2_ffn_in['sh_down'], 'L2_ffn_rt_gate': _L2_ffn_in['rt_gate'], 'L2_ffn_rt_up': _L2_ffn_in['rt_up'], 'L2_ffn_rt_down': _L2_ffn_in['rt_down'], 'L3_xattn_Wq': _L3_xattn_in['Wq'], 'L3_xattn_bq': _L3_xattn_in['bq'], 'L3_xattn_Wk': _L3_xattn_in['Wk'], 'L3_xattn_bk': _L3_xattn_in['bk'], 'L3_xattn_Wv': _L3_xattn_in['Wv'], 'L3_xattn_bv': _L3_xattn_in['bv'], 'L3_xattn_Wo': _L3_xattn_in['Wo'], 'L3_xattn_bo': _L3_xattn_in['bo'], 'L3_ffn_g1': _L3_ffn_in['g1'], 'L3_ffn_g2': _L3_ffn_in['g2'], 'L3_ffn_w_down': _L3_ffn_in['w_down'], 'L3_ffn_wq': _L3_ffn_in['wq'], 'L3_ffn_wk': _L3_ffn_in['wk'], 'L3_ffn_wv': _L3_ffn_in['wv'], 'L3_ffn_w_up': _L3_ffn_in['w_up'], 'L3_ffn_router_w': _L3_ffn_in['router_w'], 'L3_ffn_w1': _L3_ffn_in['w1'], 'L3_ffn_w2': _L3_ffn_in['w2'], 'L3_ffn_w3': _L3_ffn_in['w3']}

def reference(x, ctx_1024, fside_BxSxS2_0, mask_Bx1xSxS2_ff0, mask_Bx1x1xS2_ff0, mask_Bx1xSxS2_ik1, g_xattn, g_ffn, L0_xattn_wq, L0_xattn_wk, L0_xattn_wv, L0_xattn_wo, L0_ffn_qweights, L0_ffn_scales, L0_ffn_biases, L0_ffn_lora_a, L0_ffn_lora_b, L0_ffn_ln_gamma, L0_ffn_ln_beta, L1_xattn_Wq, L1_xattn_Wk, L1_xattn_Wv, L1_xattn_Wo, L1_xattn_Wth, L1_xattn_bth, L1_xattn_Wto, L1_xattn_bto, L1_xattn_Wf1, L1_xattn_bf1, L1_xattn_Wf2, L1_xattn_bf2, L1_ffn_gate_w, L1_ffn_gate_b, L1_ffn_rms_w, L1_ffn_w1, L1_ffn_b1, L1_ffn_w2, L1_ffn_b2, L2_xattn_Wv, L2_xattn_Wk, L2_xattn_Wq, L2_xattn_Wo, L2_xattn_bo, L2_ffn_gate_w, L2_ffn_sh_gate, L2_ffn_sh_up, L2_ffn_sh_down, L2_ffn_rt_gate, L2_ffn_rt_up, L2_ffn_rt_down, L3_xattn_Wq, L3_xattn_bq, L3_xattn_Wk, L3_xattn_bk, L3_xattn_Wv, L3_xattn_bv, L3_xattn_Wo, L3_xattn_bo, L3_ffn_g1, L3_ffn_g2, L3_ffn_w_down, L3_ffn_wq, L3_ffn_wk, L3_ffn_wv, L3_ffn_w_up, L3_ffn_router_w, L3_ffn_w1, L3_ffn_w2, L3_ffn_w3):
    import jax
    import jax.numpy as jnp

    def _L0_xattn_ref(query_input, source_input, bias, wq, wk, wv, wo):
        import jax, jax.numpy as jnp
        import numpy as np
        DEPTH = 64
        q = jnp.einsum('bfd,dnh->bfnh', query_input, wq)
        k = jnp.einsum('btd,dnh->btnh', source_input, wk)
        v = jnp.einsum('btd,dnh->btnh', source_input, wv)
        q = q * DEPTH ** (-0.5)
        logits = jnp.einsum('btnh,bfnh->bnft', k, q) + bias
        weights = jax.nn.softmax(logits, axis=-1)
        ctx = jnp.einsum('bnft,btnh->bfnh', weights, v)
        return jnp.einsum('bfnh,nhd->bfd', ctx, wo)

    def _L0_ffn_ref(x, qweights, scales, biases, lora_a, lora_b, ln_gamma, ln_beta):
        import jax, jax.numpy as jnp
        import numpy as np
        GROUP = 16
        EPS = 1e-05

        def _dequant(q, scale):
            w = q.astype(jnp.float32) / 7.5 - 1.0
            return w * jnp.repeat(scale, GROUP, axis=1)

        def _qlora_linear(x, q, scale, bias, la, lb):
            w = _dequant(q, scale)
            base = jnp.einsum('btd,od->bto', x, w) + bias
            lora = jnp.einsum('btr,or->bto', jnp.einsum('btd,rd->btr', x, la), lb)
            return base + lora

        def _layernorm(x, g, b):
            mu = jnp.mean(x, axis=-1, keepdims=True)
            var = jnp.mean(jnp.square(x - mu), axis=-1, keepdims=True)
            return (x - mu) * jax.lax.rsqrt(var + EPS) * g + b
        h = x
        for blk in range(3):
            i0, i1 = (2 * blk, 2 * blk + 1)
            y = _qlora_linear(h, qweights[i0], scales[i0], biases[i0], lora_a[i0], lora_b[i0])
            y = _layernorm(y, ln_gamma[blk], ln_beta[blk])
            y = jax.nn.gelu(y, approximate=False)
            y = _qlora_linear(y, qweights[i1], scales[i1], biases[i1], lora_a[i1], lora_b[i1])
            h = y + h
        return h

    def _L1_xattn_ref(decoder_inputs, encoder_outputs, decoder_times_dist, decoder_encoder_times_dist, dec_self_attn_bias, enc_dec_attn_bias, Wq, Wk, Wv, Wo, Wth, bth, Wto, bto, Wf1, bf1, Wf2, bf2):
        import jax, jax.numpy as jnp
        import numpy as np
        B, F, T = (2, 128, 128)
        D, N, H = (256, 16, 64)
        K = 32
        FILT = 1024
        L = 4
        EPS = 1e-06

        def _glorot(key, shape, fan_in, fan_out):
            lim = np.sqrt(6.0 / (fan_in + fan_out)).astype(np.float32)
            return jax.random.uniform(key, shape, jnp.float32, -lim, lim)

        def _norm(x):
            m = jnp.mean(x, axis=-1, keepdims=True)
            s = jnp.sqrt(jnp.mean((x - m) ** 2, axis=-1, keepdims=True))
            return (x - m) / (s + EPS)

        def _attention(x, src, dist, bias, Wq, Wk, Wv, Wo, Wth, bth, Wto, bto):
            q = jnp.einsum('bfd,dnh->bfnh', x, Wq) * H ** (-0.5)
            k = jnp.einsum('btd,dnh->btnh', src, Wk)
            v = jnp.einsum('btd,dnh->btnh', src, Wv)
            hbias = jax.nn.relu(dist[..., None] @ Wth + bth)
            qs_bias = (hbias @ Wto + bto)[..., 0]
            logits = jnp.einsum('btnh,bfnh->bnft', k, q)
            logits = logits + bias + qs_bias[:, None]
            w = jax.nn.softmax(logits, axis=-1)
            out = jnp.einsum('bnft,btnh->bfnh', w, v)
            return jnp.einsum('bfnh,nhd->bfd', out, Wo)
        x = decoder_inputs
        for i in range(L):
            y = _attention(_norm(x), encoder_outputs, decoder_encoder_times_dist, enc_dec_attn_bias, Wq[i], Wk[i], Wv[i], Wo[i], Wth[i], bth[i], Wto[i], bto[i])
            x = x + y
            y = jax.nn.relu(_norm(x) @ Wf1[i] + bf1[i]) @ Wf2[i] + bf2[i]
            x = x + y
        return _norm(x)

    def _L1_ffn_ref(x, gate_w, gate_b, rms_w, w1, b1, w2, b2):
        import jax, jax.numpy as jnp
        import numpy as np
        TEMPERATURE = 0.5
        CAPACITY_FACTOR = 1.25
        TOP_K = 1
        B, S, D = x.shape
        E = gate_w.shape[0]
        xf = x.reshape(-1, D)
        N = xf.shape[0]
        logits = xf @ gate_w.T + gate_b
        eps = jnp.finfo(logits.dtype).eps
        ms = jnp.mean(logits * logits, axis=-1, keepdims=True)
        logits = logits * jax.lax.rsqrt(ms + eps) * rms_w
        gates = jax.nn.softmax(logits / TEMPERATURE, axis=-1)
        g, idx = jax.lax.top_k(gates, TOP_K)
        g, idx = (g[:, 0], idx[:, 0])
        capacity = min(int(np.ceil(N * TOP_K / E * CAPACITY_FACTOR)), N)
        counts = jnp.zeros((E,), jnp.int32).at[idx].add(1)
        active = (counts > 0) & (capacity >= 1)
        mask = active[idx].astype(gates.dtype)
        masked = g * mask
        norm_g = masked / (masked + 1e-06)
        h = jax.nn.gelu(jnp.einsum('nd,edh->neh', xf, w1) + b1, approximate=False)
        y = jnp.einsum('neh,ehd->ned', h, w2) + b2
        out = (y * norm_g[:, None, None]).sum(axis=1)
        return out.reshape(B, S, D)

    def _L2_xattn_ref(values, keys, queries, mask, Wv, Wk, Wq, Wo, bo):
        import jax, jax.numpy as jnp
        import numpy as np
        EMBED = 256
        HEADS = 16
        HEAD_DIM = EMBED // HEADS
        B, S = (4, 512)
        N, q_len = (queries.shape[0], queries.shape[1])
        v_len, k_len = (values.shape[1], keys.shape[1])
        v = values.reshape(N, v_len, HEADS, HEAD_DIM)
        k = keys.reshape(N, k_len, HEADS, HEAD_DIM)
        q = queries.reshape(N, q_len, HEADS, HEAD_DIM)
        v = jnp.einsum('nlhd,ed->nlhe', v, Wv)
        k = jnp.einsum('nlhd,ed->nlhe', k, Wk)
        q = jnp.einsum('nlhd,ed->nlhe', q, Wq)
        energy = jnp.einsum('nqhd,nkhd->nhqk', q, k)
        energy = jnp.where(mask == 0, jnp.float32(-1e+20), energy)
        attention = jax.nn.softmax(energy / np.sqrt(EMBED).astype(np.float32), axis=3)
        out = jnp.einsum('nhql,nlhd->nqhd', attention, v).reshape(N, q_len, EMBED)
        return out @ Wo.T + bo

    def _L2_ffn_ref(hidden_states, gate_w, sh_gate, sh_up, sh_down, rt_gate, rt_up, rt_down):
        import jax, jax.numpy as jnp
        import numpy as np
        H = 256
        I = 512
        E = 8
        B, S = (2, 256)

        def _swiglu(x, wg, wu, wd):
            return jax.nn.silu(x @ wg) * (x @ wu) @ wd
        b, s, h = hidden_states.shape
        x = hidden_states.reshape(-1, h)
        logits = x @ gate_w
        top_val = jnp.max(logits, axis=-1, keepdims=True)
        top_id = jnp.argmax(logits, axis=-1)
        score = jax.nn.sigmoid(top_val)
        xs = x * score
        g = jnp.einsum('th,ehi->eti', xs, rt_gate)
        u = jnp.einsum('th,ehi->eti', xs, rt_up)
        act = jax.nn.silu(g) * u
        y = jnp.einsum('eti,eih->eth', act, rt_down)
        onehot = jax.nn.one_hot(top_id, E, dtype=x.dtype)
        routed = jnp.einsum('eth,te->th', y, onehot)
        shared = _swiglu(x, sh_gate, sh_up, sh_down)
        return (shared + routed).reshape(b, s, h)

    def _L3_xattn_ref(Q_decoder, K_encoder, V_encoder, Wq, bq, Wk, bk, Wv, bv, Wo, bo):
        import jax, jax.numpy as jnp
        import numpy as np
        import math
        EMBED_DIM = 256
        NUM_HEADS = 16
        D_K = EMBED_DIM // NUM_HEADS
        B, S_DEC, S_ENC = (4, 256, 512)
        b, sd, d = Q_decoder.shape
        se = K_encoder.shape[1]
        Q = (Q_decoder @ Wq + bq).reshape(b, sd, NUM_HEADS, D_K).transpose(0, 2, 1, 3)
        K = (K_encoder @ Wk + bk).reshape(b, se, NUM_HEADS, D_K).transpose(0, 2, 1, 3)
        V = (V_encoder @ Wv + bv).reshape(b, se, NUM_HEADS, D_K).transpose(0, 2, 1, 3)
        scores = jnp.einsum('bhqd,bhkd->bhqk', Q, K) / math.sqrt(D_K)
        attn = jax.nn.softmax(scores, axis=-1)
        out = jnp.einsum('bhqk,bhkd->bhqd', attn, V)
        out = out.transpose(0, 2, 1, 3).reshape(b, sd, d)
        return out @ Wo + bo

    def _L3_ffn_ref(x, g1, g2, w_down, wq, wk, wv, w_up, router_w, w1, w2, w3):
        import jax, jax.numpy as jnp
        import numpy as np
        B, S, D = (2, 256, 256)
        L, H = (128, 16)
        HD = L // H
        F, E, K = (512, 8, 2)
        THETA = 10000.0
        EPS = 1e-05

        def _rmsnorm(x, g):
            return x * g * jax.lax.rsqrt(jnp.mean(x * x, axis=-1, keepdims=True) + EPS)

        def _rope(t, pos):
            inv_freq = 1.0 / THETA ** (jnp.arange(0, HD, 2, dtype=jnp.float32) / HD)
            ang = pos[:, None].astype(jnp.float32) * inv_freq[None, :]
            cos, sin = (jnp.cos(ang), jnp.sin(ang))
            t1, t2 = (t[..., 0::2], t[..., 1::2])
            r1 = t1 * cos - t2 * sin
            r2 = t1 * sin + t2 * cos
            return jnp.stack([r1, r2], axis=-1).reshape(t.shape)

        def _forward(x, g1, g2, w_down, wq, wk, wv, w_up, router_w, w1, w2, w3):
            b, s, _ = x.shape
            pos = jnp.arange(s)
            h = _rmsnorm(x, g1)
            c = h @ w_down
            split = lambda t: t.reshape(b, s, H, HD).transpose(0, 2, 1, 3)
            q = _rope(split(c @ wq), pos)
            k = _rope(split(c @ wk), pos)
            v = split(c @ wv)
            scores = jnp.einsum('bhqd,bhkd->bhqk', q, k) / jnp.sqrt(jnp.float32(HD))
            causal = jnp.tril(jnp.ones((s, s), bool))
            scores = jnp.where(causal, scores, -jnp.inf)
            attn = jax.nn.softmax(scores, axis=-1)
            o = jnp.einsum('bhqk,bhkd->bhqd', attn, v).transpose(0, 2, 1, 3).reshape(b, s, L)
            x = x + o @ w_up
            res = x
            t = _rmsnorm(x, g2).reshape(-1, D)
            probs = jax.nn.softmax(t @ router_w, axis=-1)
            vals, idx = jax.lax.top_k(probs, K)
            w = vals / jnp.sum(vals, axis=-1, keepdims=True)
            gate = jnp.sum(jax.nn.one_hot(idx, E, dtype=t.dtype) * w[..., None], axis=1)
            hid = jax.nn.silu(jnp.einsum('td,edf->tef', t, w1)) * jnp.einsum('td,edf->tef', t, w3)
            y_e = jnp.einsum('tef,efd->ted', hid, w2)
            y = jnp.einsum('ted,te->td', y_e, gate)
            return res + y.reshape(b, s, D)
        return _forward(x, g1, g2, w_down, wq, wk, wv, w_up, router_w, w1, w2, w3)
    x = x + jnp.tanh(g_xattn[0]) * _L0_xattn_ref(_layernorm(x, axis=-1), ctx_1024, mask_Bx1xSxS2_ff0, L0_xattn_wq, L0_xattn_wk, L0_xattn_wv, L0_xattn_wo)
    x = x + jnp.tanh(g_ffn[0]) * _L0_ffn_ref(_layernorm(x, axis=-1), L0_ffn_qweights, L0_ffn_scales, L0_ffn_biases, L0_ffn_lora_a, L0_ffn_lora_b, L0_ffn_ln_gamma, L0_ffn_ln_beta)
    x = x + jnp.tanh(g_xattn[1]) * _L1_xattn_ref(_layernorm(x, axis=-1), ctx_1024, fside_BxSxS2_0, fside_BxSxS2_0, mask_Bx1x1xS2_ff0, mask_Bx1x1xS2_ff0, L1_xattn_Wq, L1_xattn_Wk, L1_xattn_Wv, L1_xattn_Wo, L1_xattn_Wth, L1_xattn_bth, L1_xattn_Wto, L1_xattn_bto, L1_xattn_Wf1, L1_xattn_bf1, L1_xattn_Wf2, L1_xattn_bf2)
    x = x + jnp.tanh(g_ffn[1]) * _L1_ffn_ref(_layernorm(x, axis=-1), L1_ffn_gate_w, L1_ffn_gate_b, L1_ffn_rms_w, L1_ffn_w1, L1_ffn_b1, L1_ffn_w2, L1_ffn_b2)
    x = x + jnp.tanh(g_xattn[2]) * _L2_xattn_ref(ctx_1024, ctx_1024, _layernorm(x, axis=-1), mask_Bx1xSxS2_ik1, L2_xattn_Wv, L2_xattn_Wk, L2_xattn_Wq, L2_xattn_Wo, L2_xattn_bo)
    x = x + jnp.tanh(g_ffn[2]) * _L2_ffn_ref(_layernorm(x, axis=-1), L2_ffn_gate_w, L2_ffn_sh_gate, L2_ffn_sh_up, L2_ffn_sh_down, L2_ffn_rt_gate, L2_ffn_rt_up, L2_ffn_rt_down)
    x = x + jnp.tanh(g_xattn[3]) * _L3_xattn_ref(_layernorm(x, axis=-1), ctx_1024, ctx_1024, L3_xattn_Wq, L3_xattn_bq, L3_xattn_Wk, L3_xattn_bk, L3_xattn_Wv, L3_xattn_bv, L3_xattn_Wo, L3_xattn_bo)
    x = x + jnp.tanh(g_ffn[3]) * _L3_ffn_ref(_layernorm(x, axis=-1), L3_ffn_g1, L3_ffn_g2, L3_ffn_w_down, L3_ffn_wq, L3_ffn_wk, L3_ffn_wv, L3_ffn_w_up, L3_ffn_router_w, L3_ffn_w1, L3_ffn_w2, L3_ffn_w3)
    return x

_drawn_inputs = setup_inputs


def setup_inputs(seed=0):
    import zlib

    import numpy as np

    out = dict(_drawn_inputs(seed))
    spreads = {'L0_ffn_ln_gamma': (1.0, 0.2),
     'L0_ffn_ln_beta': (0.0, 0.1),
     'L1_xattn_bth': (0.0, 0.8),
     'L1_xattn_bto': (0.0, 0.8),
     'L1_xattn_bf1': (0.0, 0.523),
     'L1_xattn_bf2': (0.0, 0.459),
     'L1_ffn_gate_b': (0.0, 0.8),
     'L1_ffn_rms_w': (1.0, 0.6),
     'L1_ffn_b1': (0.0, 0.572),
     'L1_ffn_b2': (0.0, 0.1),
     'L3_xattn_bq': (0.0, 0.8),
     'L3_xattn_bk': (0.0, 0.8),
     'L3_xattn_bv': (0.0, 0.558),
     'L3_xattn_bo': (0.0, 0.53),
     'L3_ffn_g1': (1.0, 0.6),
     'L3_ffn_g2': (1.0, 0.6)}
    factors = {'fside_BxSxS2_0': 8.0,
     'g_ffn': 7.717,
     'L0_ffn_biases': 6.682,
     'L0_ffn_lora_a': 4.186,
     'L0_ffn_lora_b': 4.099,
     'L1_xattn_Wth': 8.0,
     'L1_xattn_Wto': 8.0,
     'L1_ffn_gate_w': 8.0,
     'L2_xattn_Wk': 4.089,
     'L2_xattn_Wq': 4.785,
     'L2_xattn_bo': 8.0,
     'L3_ffn_w_down': 8.0,
     'L3_ffn_wq': 8.0,
     'L3_ffn_wk': 8.0,
     'L3_ffn_wv': 8.0,
     'L3_ffn_w_up': 8.0,
     'L3_ffn_router_w': 8.0,
     'L3_ffn_w1': 8.0,
     'L3_ffn_w2': 8.0,
     'L3_ffn_w3': 8.0}
    for name, (base, spread) in spreads.items():
        noise = np.random.default_rng([zlib.crc32(name.encode()), seed]).standard_normal(out[name].shape)
        drawn = base * np.exp(spread * noise) if base else spread * noise
        out[name] = jnp.asarray(drawn.astype(out[name].dtype))
    for name, factor in factors.items():
        out[name] = (out[name] * factor).astype(out[name].dtype)
    return out
```

```python
from contextlib import ExitStack

import numpy as np

import concourse.bass as bass
from concourse import mybir
from concourse.alu_op_type import AluOpType as ALU

F32 = mybir.dt.float32
I32 = mybir.dt.int32
BF16 = mybir.dt.bfloat16
ACT = mybir.ActivationFunctionType
AX = mybir.AxisListType

P = 128
B, S, D = 2, 1024, 256
KD = D // P
TB = S // P
NT = B * TB
H, S2 = 16, 77
HK = H * S2
CH = -(-HK // P)
LASTROWS = HK - (CH - 1) * P
HE = H * 64
NTE = HE // P
PAIR = 2 * S2
VPAD = P + PAIR + P
CTX = B * S2
E, F = 8, 512
FC = F // P
GRP = 512
TG = GRP // P
NG = NT // TG
NEG = -1.0e30
BANK = 512
HD3 = 8
STOP = None


class Queue:

    def __init__(self, eng, sem, step=1):
        self.eng, self.sem, self.step, self.count, self.seen = eng, sem, step, 0, {}

    def wait(self, *marks):
        for mark in marks:
            if mark is None:
                continue
            queue, value = mark
            if self.seen.get(id(queue), 0) < value:
                self.eng.wait_ge(queue.sem, value)
                self.seen[id(queue)] = value

    def mark(self, ins):
        ins.then_inc(self.sem, self.step)
        self.count += self.step
        return (self, self.count)

    def last(self):
        return (self, self.count) if self.count else None

    def __call__(self, build, *after):
        self.wait(self.last(), *after)
        return self.mark(build(self.eng))


class Lane(Queue):

    def __init__(self, sem):
        super().__init__(None, sem, 16)


def program(nc, a, out):
    with ExitStack() as ctx:
        build(nc, ctx, a, out)


def build(nc, ctx, a, out):
    def sb(name, shape, dt=F32):
        return ctx.enter_context(nc.sbuf_tensor(name, shape, dt))

    def sem(name):
        return ctx.enter_context(nc.semaphore(name))

    def scratch(name, shape, dt=F32):
        return nc.dram_tensor(name, shape, dt, kind="Internal").ap()

    PE = Queue(nc.tensor, sem("pe_done"))
    V = Queue(nc.vector, sem("vector_done"))
    A = Queue(nc.scalar, sem("scalar_done"))
    G = Queue(nc.gpsimd, sem("gpsimd_done"))
    SP = Queue(nc.sync, sem("sync_unused"))
    dma_lanes = [Lane(sem(f"dma_{n}_landed")) for n in "abcdefghij"]
    dma_a, dma_b, dma_c, dma_d, dma_e, dma_f, *more_lanes = dma_lanes
    lanes = [PE, V, A, G, *dma_lanes]

    def load(lane, dst, src, *after, columns=False):
        SP.wait(*after)
        return lane.mark(SP.eng.dma_start(dst, src, allow_slow_non_contiguous=columns))

    ahead = dma_f

    def fence(spare=None):
        for lane in dma_lanes:
            if lane is not spare:
                SP.wait(lane.last())
        for q in (PE, V, A, G):
            q.wait(q.last())
        nc.all_engine_barrier()
        for q in lanes:
            if q.count and q is not spare:
                nc.vector.sem_clear(q.sem)
        nc.all_engine_barrier()
        for q in lanes:
            if q is not spare:
                q.count = 0
        for q in (PE, V, A, G, SP):
            q.seen = {}

    x = sb("x", [P, NT, D])
    inner = sb("inner", [P, NT, D])
    Kt = sb("Kt", [P, B, KD, HK])
    Vt = sb("Vt", [P, B, CH, D])
    weights = sb("weights", [P, 4 * 2048])
    prep = sb("prep", [P, 2048 + NTE * B * PAIR + B * NTE * VPAD])
    shared = sb("shared", [P, 2 * HK + 2 * CH * P])
    prob = shared[:, 0:2 * HK].rearrange("p (n c) -> p n c", n=2)
    probT = shared[:, 2 * HK:].rearrange("p (n c m) -> p n c m", n=2, c=CH)
    xnT = shared[:, 0:KD * NT * P].rearrange("p (k n) -> p k n", k=KD)
    bias = sb("bias", [P, NT, S2])
    ctxT = sb("ctxT", [P, KD, CTX])
    ident = sb("ident", [P, P])
    block = sb("block", [P, 8])
    ones = sb("ones", [P, P])
    small = sb("small", [P, 1024])
    bn6 = sb("bn6", [P, NT, 6])
    meanvar = sb("meanvar", [P, NT, 2])
    rstd = sb("rstd", [P, NT])
    gates = sb("gates", [P, NT, E])
    tanh_g = sb("tanh_g", [P, 8])
    xn = sb("xn", [P, 2, D])
    xnTt = sb("xnTt", [P, 2, KD, P])
    qTt = sb("qTt", [P, 2, KD, P])
    row = sb("row", [P, 2, 64])
    tmp = sb("tmp", [P, 2, D])
    psum = ctx.enter_context(nc.psum_tensor("psum", [P, 8, BANK], F32))
    flat = psum[:, :, :].rearrange("p b c -> p (b c)")

    sT = inner[:, :, :].rearrange("p t d -> p (t d)").rearrange("p (k n) -> p k n", k=KD)

    def bcast(src, n):
        return src.rearrange("(o n) -> o n", o=1).to_broadcast([P, n])

    fside = sb("fside", [P, NT, S2])
    for bt in range(B):
        load(dma_a, x[:, bt * TB:(bt + 1) * TB, :], a["x"][bt].rearrange("(t p) d -> p t d", p=P))
    graw = small[:, 0:8]
    load(dma_b, graw[:, 0:4], bcast(a["g_xattn"], 4))
    load(dma_b, graw[:, 4:8], bcast(a["g_ffn"], 4))
    ctx_rows = prep[:, 0:2 * D].rearrange("p (k d) -> p k d", k=2)
    ctx_flat = a["ctx_1024"].rearrange("b s d -> (b s) d")
    load(dma_b, ctx_rows[:, 0, :], ctx_flat[0:P])
    load(dma_b, ctx_rows[0:CTX - P, 1, :], ctx_flat[P:CTX])
    load(dma_c, fside[:, :, :], a["fside_BxSxS2_0"].rearrange("b (t p) s -> p (b t) s", p=P))
    G(lambda e: e.memset(ones[:, :], 1.0))
    G(lambda e: e.affine_select(out=ident[:, :], in_=ones[:, :], compare_op=ALU.is_equal, fill=0.0,
                                base=0, pattern=[[-1, P]], channel_multiplier=1))
    G(lambda e: e.affine_select(out=block[:, :], in_=ones[:, 0:8], compare_op=ALU.is_ge, fill=0.0,
                                base=0, pattern=[[-16, 8]], channel_multiplier=1))
    const = G(lambda e: e.affine_select(out=block[:, :], in_=block[:, :], compare_op=ALU.is_ge,
                                        fill=0.0, base=15, pattern=[[16, 8]], channel_multiplier=-1))
    A(lambda e: e.activation(tanh_g[:, :], graw, ACT.Tanh), dma_b.last())
    PE.wait(const, dma_b.last())
    for k in range(KD):
        nc.tensor.transpose(psum[:, k, 0:P], ctx_rows[:, 0, k * P:(k + 1) * P], ident[:, :])
        t = PE.mark(nc.tensor.transpose(psum[:, k, P:CTX], ctx_rows[0:CTX - P, 1, k * P:(k + 1) * P],
                                        ident[0:CTX - P, 0:CTX - P]))
        V(lambda e: e.tensor_copy(ctxT[:, k, :], psum[:, k, 0:CTX]), t)
    fence()


    def statistics(src, inside=None, outside=None):
        for t in range(NT):
            V.wait(V.last())
            V.mark(nc.vector.bn_stats(bn6[:, t, :], src[:, t, :]))
        V.wait(V.last())
        for t in range(NT):
            V.mark(nc.vector.bn_aggr(meanvar[:, t, :], bn6[:, t, :]))
        reciprocal_root(meanvar[:, :, 1], inside, outside)

    def reciprocal_root(var, inside, outside):
        V(lambda e: e.tensor_scalar(rstd[:, :], var, inside or 0.0, None, ALU.add))
        r = A(lambda e: e.activation(rstd[:, :], rstd[:, :], ACT.Sqrt), V.last())
        V.wait(r)
        if outside:
            V(lambda e: e.tensor_scalar(rstd[:, :], rstd[:, :], outside, None, ALU.add))
        V(lambda e: e.reciprocal(rstd[:, :], rstd[:, :]))

    def normalise(dst, src, t, *after):
        return V(lambda e: e.tensor_scalar(dst, src[:, t, :], meanvar[:, t, 0:1], rstd[:, bass.ds(t, 1)],
                                           ALU.subtract, ALU.mult), *after)

    def turn(src, dst_psum, *after):
        PE.wait(*after)
        for k in range(KD):
            ins = nc.tensor.transpose(dst_psum[:, k * P:(k + 1) * P], src[:, k * P:(k + 1) * P],
                                      ident[:, :])
        return PE.mark(ins)

    class Ring:

        def __init__(self, banks):
            self.banks, self.free, self.n = banks, [None] * len(banks), -1

        def take(self):
            self.n = (self.n + 1) % len(self.banks)
            return self.banks[self.n], self.free[self.n]

        def give(self, mark):
            self.free[self.n] = mark


    WqT = prep[:, 0:2048].rearrange("p (t d) -> p t d", t=NTE)
    kexp = prep[:, 2048:2048 + NTE * B * PAIR].rearrange("p (t b c) -> p t b c", t=NTE, b=B)
    vexp = prep[:, 2048 + NTE * B * PAIR:].rearrange("p (b t c) -> p b t c", b=B, t=NTE)
    vexp16 = prep[:, 2048:2048 + B * KD * HK].rearrange("p (b g c) -> p b g c", b=B, g=KD)

    def clear_expanded():
        half = prep.shape[1] // 2
        G(lambda e: e.memset(prep[:, 0:half], 0.0))
        V(lambda e: e.memset(prep[:, half:], 0.0))
        fence()

    def prepare_wide(wq, wk, wv, wo, filler):
        Wq = weights[:, 0:2048].rearrange("p (k n) -> p k n", k=KD)
        Wk = weights[:, 2048:4096].rearrange("p (k n) -> p k n", k=KD)
        Wv = weights[:, 4096:6144].rearrange("p (k n) -> p k n", k=KD)
        Wo = weights[:, 6144:8192].rearrange("p (t d) -> p t d", t=NTE)
        lk = load(dma_a, Wk, wk)
        lv = load(dma_b, Wv, wv)
        lq = load(dma_c, Wq, wq)
        lo = load(dma_d, Wo, wo)
        ring = Ring(list(range(8)))
        for w, landed, scale, dst in ((Wk, lk, 0.125, lambda t, i: kexp[64 * i:64 * i + 64, t, :, S2 * i:S2 * i + S2]),
                                      (Wv, lv, 1.0, lambda t, i: vexp[64 * i:64 * i + 64, :, t, P + S2 * i:P + S2 * i + S2])):
            for t in range(NTE):
                bank, free = ring.take()
                PE.wait(landed, free)
                for k in range(KD):
                    ins = nc.tensor.matmul(psum[:, bank, 0:CTX], w[:, k, t * P:(t + 1) * P], ctxT[:, k, :],
                                           start=(k == 0), stop=(k == KD - 1))
                m = PE.mark(ins)
                for i in range(2):
                    src = psum[64 * i:64 * i + 64, bank, 0:CTX].rearrange("p (b c) -> p b c", b=B)
                    r = A(lambda e: e.mul(dst(t, i), src, scale), m)
                ring.give(r)
                filler()
        for t in range(0, NTE, 2):
            bank, free = ring.take()
            PE.wait(lq, free)
            for i in range(2):
                for k in range(KD):
                    ins = nc.tensor.transpose(psum[:, bank, (2 * i + k) * P:(2 * i + k + 1) * P],
                                              Wq[:, k, (t + i) * P:(t + i + 1) * P], ident[:, :])
            m = PE.mark(ins)
            turned = V(lambda e: e.tensor_copy(WqT[:, t:t + 2, :].rearrange("p t d -> p (t d)"), psum[:, bank, :]), m)
            ring.give(turned)
            filler()
        kv_done = A.last()
        for t in range(NTE):
            for k in range(KD):
                bank, free = ring.take()
                PE.wait(turned, kv_done, free)
                m = PE.mark(nc.tensor.matmul(psum[:, bank, 0:B * PAIR], WqT[:, t, k * P:(k + 1) * P],
                                             kexp[:, t, :, :].rearrange("p b c -> p (b c)"), start=True, stop=True))
                ring.give(A(lambda e: e.copy(Kt[:, :, k, t * PAIR:(t + 1) * PAIR],
                                             psum[:, bank, 0:B * PAIR].rearrange("p (b c) -> p b c", b=B)), m))
                filler()
        for bt in range(B):
            for c in range(0, CH, 2):
                bank, free = ring.take()
                PE.wait(lo, free)
                for i in range(2):
                    pairs = [t for t in range(NTE) if t * PAIR < (c + i + 1) * P and (t + 1) * PAIR > (c + i) * P]
                    for t in pairs:
                        at = (c + i) * P - t * PAIR + P
                        ins = nc.tensor.matmul(psum[:, bank, i * D:(i + 1) * D], vexp[:, bt, t, at:at + P], Wo[:, t, :],
                                               start=(t == pairs[0]), stop=(t == pairs[-1]))
                m = PE.mark(ins)
                ring.give(V(lambda e: e.tensor_copy(Vt[:, bt, c:c + 2, :].rearrange("p c d -> p (c d)"), psum[:, bank, :]), m))
                filler()

    def prepare_narrow(kT_of, vT_of, wo_turned, wo_after, kv_bias):
        kc = small[:, 0:KD * CTX].rearrange("p (g c) -> p g c", g=KD)
        vc = small[:, KD * CTX:2 * KD * CTX].rearrange("p (g c) -> p g c", g=KD)
        zeroed = G(lambda e: e.memset(vexp16[:, :, :, :].rearrange("p b g c -> p (b g c)"), 0.0))
        ring = Ring([4, 5, 6, 7])
        for g in range(KD):
            for n, (of, dst) in enumerate(((kT_of, kc), (vT_of, vc))):
                bank, free = ring.take()
                PE.wait(free)
                m = of(psum[:, bank, 0:CTX], g)
                add = kv_bias[:, 2 * g + n:2 * g + n + 1] if kv_bias is not None else 0.0
                r = V(lambda e: e.tensor_scalar(dst[:, g, :], psum[:, bank, 0:CTX], add, None, ALU.add), m)
                ring.give(r)
            for h in range(8):
                V(lambda e: e.tensor_scalar(Kt[:, :, g, h * S2:(h + 1) * S2],
                                            kc[:, g, :].rearrange("p (b c) -> p b c", b=B),
                                            block[:, h:h + 1], None, ALU.mult))
                at = (g * 8 + h) * S2
                V(lambda e: e.tensor_scalar(vexp16[:, :, g, at:at + S2],
                                            vc[:, g, :].rearrange("p (b c) -> p b c", b=B),
                                            block[:, h:h + 1], None, ALU.mult), zeroed)
        expanded = V.last()
        for bt in range(B):
            for c in range(CH):
                bank, free = ring.take()
                PE.wait(expanded, free, wo_after)
                rows = min(P, HK - c * P)
                halves = [g for g in range(KD) if g * 8 * S2 < (c + 1) * P and (g + 1) * 8 * S2 > c * P]
                for g in halves:
                    ins = nc.tensor.matmul(psum[0:rows, bank, 0:D], vexp16[:, bt, g, c * P:c * P + rows],
                                           wo_turned[:, g, :], start=(g == halves[0]), stop=(g == halves[-1]))
                m = PE.mark(ins)
                ring.give(A(lambda e: e.copy(Vt[0:rows, bt, c, :], psum[0:rows, bank, 0:D]), m))


    WIDE = [[(n * BANK, min(BANK, HK - n * BANK), [(0, n * BANK), (1, n * BANK)])] for n in range(3)]
    HALF = 8 * S2
    NARROW = [[(0, BANK, [(0, 0)])],
              [(BANK, HALF - BANK, [(0, BANK)]), (HALF, 2 * BANK - HALF, [(1, 0)])],
              [(2 * BANK, HK - 2 * BANK, [(1, 2 * BANK - HALF)])]]

    def attention(stream, pieces, scale, biased, gate, project=None, out_bias=None):
        with nc.Fori(0, B) as bt:
            free_s = [None, None]
            free_o = [None, None]
            free_p = [None, None]
            xn_read = [None, None]
            xt_read = [None, None]
            probT_read = [None, None]
            lhs_read = [None, None]

            def normal(t):
                return normalise(xn[:, t % 2, :], stream, bt * TB + t, xn_read[t % 2])

            def turned(t, n):
                par = t % 2
                so = flat[:, (6 + par) * BANK:(6 + par) * BANK + D]
                tr = turn(xn[:, par, :], so, n, xt_read[par])
                xn_read[par] = tr
                cp = A(lambda e: e.copy(xnTt[:, par, :, :].rearrange("p k c -> p (k c)"), so), tr, lhs_read[par])
                if project is not None:
                    cp = project(par, so, cp)
                xt_read[par] = cp
                return cp

            def scores(t, cp):
                par = t % 2
                lhs = xnTt if project is None else qTt
                PE.wait(cp, free_s[par])
                for bank in pieces:
                    for at, cols, parts in bank:
                        for k, src in parts:
                            ins = nc.tensor.matmul(flat[:, par * 3 * BANK + at:par * 3 * BANK + at + cols],
                                                   lhs[:, par, k, :], Kt[:, bt, k, src:src + cols],
                                                   start=(k == parts[0][0]), stop=(k == parts[-1][0]))
                lhs_read[par] = PE.mark(ins)
                return lhs_read[par]

            def softmax(t, m):
                par = t % 2
                S_ps = flat[:, par * 3 * BANK:par * 3 * BANK + HK].rearrange("p (h c) -> p h c", h=H)
                Pb = prob[:, par, :].rearrange("p (h c) -> p h c", h=H)
                negmax, total = row[:, par, 0:H], row[:, par, H:2 * H]
                V.wait(free_p[par], m)
                src = S_ps
                if biased:
                    V(lambda e: e.tensor_tensor(Pb, S_ps, bias[:, bt * TB + t, :].unsqueeze(1).to_broadcast([P, H, S2]),
                                                ALU.add))
                    src = Pb
                V(lambda e: e.tensor_reduce(negmax, src, AX.X, ALU.max, negate=True))
                V(lambda e: e.tensor_tensor(Pb, src, negmax.unsqueeze(2).to_broadcast([P, H, S2]), ALU.add))
                ex = A(lambda e: e.activation(prob[:, par, :], prob[:, par, :], ACT.Exp, scale=scale), V.last())
                return ex

            def share(t, ex):
                par = t % 2
                Pb = prob[:, par, :].rearrange("p (h c) -> p h c", h=H)
                total = row[:, par, H:2 * H]
                V(lambda e: e.tensor_reduce(total, Pb, AX.X, ALU.add), ex)
                V(lambda e: e.reciprocal(total, total))
                return V(lambda e: e.tensor_tensor(Pb, Pb, total.unsqueeze(2).to_broadcast([P, H, S2]), ALU.mult))

            def outputs(t, ready):
                par = t % 2
                base = par * 3 * BANK
                PE.wait(ready)
                for c in range(CH):
                    rows = min(P, HK - c * P)
                    ins = nc.tensor.transpose(flat[0:rows, base + c * P:base + (c + 1) * P],
                                              prob[:, par, c * P:c * P + rows], ident[:, :])
                m = PE.mark(ins)
                free_p[par] = m
                full = (CH - 1) * P
                A(lambda e: e.copy(probT[:, par, 0:CH - 1, :].rearrange("p c n -> p (c n)"),
                                   flat[:, base:base + full]), m, probT_read[par])
                cp = A(lambda e: e.copy(probT[0:LASTROWS, par, CH - 1, :],
                                        flat[0:LASTROWS, base + full:base + full + P]))
                free_s[par] = cp
                PE.wait(cp, free_o[par])
                o = flat[:, (6 + par) * BANK + D:(6 + par) * BANK + 2 * D]
                for c in range(CH):
                    rows = min(P, HK - c * P)
                    ins = nc.tensor.matmul(o, probT[0:rows, par, c, :], Vt[0:rows, bt, c, :],
                                           start=(c == 0), stop=(c == CH - 1 and out_bias is None))
                if out_bias is not None:
                    ins = nc.tensor.matmul(o, ones[0:1, :], out_bias, start=False, stop=True)
                probT_read[par] = PE.mark(ins)
                return probT_read[par]

            def residual(t, m):
                o = flat[:, (6 + t % 2) * BANK + D:(6 + t % 2) * BANK + 2 * D]
                tile = bt * TB + t
                free_o[t % 2] = V(lambda e: e.scalar_tensor_tensor(stream[:, tile, :], o, gate, stream[:, tile, :],
                                                                   ALU.mult, ALU.add), m)

            cp = turned(0, normal(0))
            scored = scores(0, cp)
            cp = turned(1, normal(1))
            done = None
            for t in range(TB):
                ex = softmax(t, scored)
                n = normal(t + 2) if t + 2 < TB else None
                if done is not None:
                    residual(t - 1, done)
                ready = share(t, ex)
                if t + 1 < TB:
                    scored = scores(t + 1, cp)
                if t + 2 < TB:
                    cp = turned(t + 2, n)
                done = outputs(t, ready)
            residual(TB - 1, done)
            fence(spare=ahead)


    def slot(s):
        w = weights[:, s * 3072:(s + 1) * 3072]
        return (w[:, 0:1024].rearrange("p (k f) -> p k f", k=KD), w[:, 1024:2048].rearrange("p (k f) -> p k f", k=KD),
                w[:, 2048:3072].rearrange("p (f d) -> p f d", f=FC))

    bias1 = sb("bias1", [P, 2, FC])
    hidden = prep[:, 0:4 * GRP].rearrange("p (n c) -> p n c", n=4)
    gated_tmp = prep[:, 4 * GRP:6 * GRP].rearrange("p (n c) -> p n c", n=2)

    def fresh_state():
        return {"ring": Ring([0, 1, 2, 3]), "hid": [None] * 4, "y": [None, None], "n": 0, "tmp": [None, None]}

    def experts(acc, slots, func, gated, xT, gate_of, state=None):
        state = state or fresh_state()
        hring = state["ring"]

        def first(s, landed, g, f):
            w1, w3, _ = slot(s)
            n = state["n"]
            state["n"] += 1
            outs = []
            for w in ((w1, w3) if gated else (w1,)):
                bank, free = hring.take()
                i = hring.n
                PE.wait(free, landed)
                for k in range(KD):
                    ins = nc.tensor.matmul(psum[:, bank, :], w[:, k, f * P:(f + 1) * P],
                                           xT(s)[:, k, g * GRP:(g + 1) * GRP], start=(k == 0), stop=(k == KD - 1))
                outs.append((bank, i, PE.mark(ins)))
            h = hidden[:, n % 4, :]
            if gated:
                (b0, i0, m0), (b1, i1, m1) = outs
                tm = gated_tmp[:, n % 2, :]
                r = A(lambda e: e.activation(tm, psum[:, b0, :], func), m0, state["tmp"][n % 2])
                hring.free[i0] = r
                r = V(lambda e: e.tensor_tensor(h, psum[:, b1, :], tm, ALU.mult), m1, r, state["hid"][n % 4])
                hring.free[i1] = r
                state["tmp"][n % 2] = r
            else:
                b0, i0, m0 = outs[0]
                r = A(lambda e: e.activation(h, psum[:, b0, :], func, bias=bias1[:, s, f:f + 1]),
                      m0, state["hid"][n % 4], landed)
                hring.free[i0] = r
            return n, r

        def second(s, g, f, n, ready):
            _, _, w2 = slot(s)
            y = flat[:, (4 + 2 * (g % 2)) * BANK:(6 + 2 * (g % 2)) * BANK]
            PE.wait(ready, state["y"][g % 2] if f == 0 else None)
            for t in range(TG):
                ins = nc.tensor.matmul(y[:, t * D:(t + 1) * D], hidden[:, n % 4, t * P:(t + 1) * P], w2[:, f, :],
                                       start=(f == 0 and t % 2 == 0), stop=(f == FC - 1), skip_group_check=True)
            m = PE.mark(ins)
            state["hid"][n % 4] = m
            if f == FC - 1:
                for t in range(TG):
                    tile = g * TG + t
                    state["y"][g % 2] = V(lambda e: e.scalar_tensor_tensor(
                        acc[:, tile, :], y[:, t * D:(t + 1) * D], gate_of(s, tile), acc[:, tile, :],
                        ALU.mult, ALU.add), m)

        behind = None
        for s, landed in slots:
            for g in range(NG):
                for f in range(FC):
                    n, ready = first(s, landed, g, f)
                    if behind is not None:
                        second(*behind)
                    behind = (s, g, f, n, ready)
        second(*behind)

    def fetch_expert(lane, s, w1, w3, w2, b1, *after):
        to1, to3, to2 = slot(s)
        load(lane, to1, w1.rearrange("(k p) f -> p k f", p=P), *after)
        if w3 is not None:
            load(lane, to3, w3.rearrange("(k p) f -> p k f", p=P))
        if b1 is not None:
            load(lane, bias1[:, s, :], b1.rearrange("(f p) -> p f", p=P), columns=True)
        return load(lane, to2, w2.rearrange("(f p) d -> p f d", p=P))

    def expert_pairs(acc, fetch, func, gated, xT, gate_of):
        with nc.Fori(0, E // 2) as i:
            state = fresh_state()
            got1 = fetch(dma_b, 1, 2 * i + 1)
            experts(acc, [(0, None)], func, gated, xT, lambda s, tile: gate_of(2 * i, tile), state)
            fetch(dma_a, 0, (2 * i + 2) % E, PE.last(), A.last())
            experts(acc, [(1, got1)], func, gated, xT, lambda s, tile: gate_of(2 * i + 1, tile), state)
            fence()


    def feed_input(src, dst, per_tile=None, gain=None):
        with nc.Fori(0, B) as bt:
            xn_read = [None, None]
            read = [None, None]
            for t in range(TB):
                par = t % 2
                tile = bt * TB + t
                bank = flat[:, par * BANK:(par + 1) * BANK]
                n = normalise(xn[:, par, :], src, tile, xn_read[par])
                tr = turn(xn[:, par, :], bank[:, 0:D], n, read[par])
                xn_read[par] = tr
                A.wait(tr)
                if gain is None:
                    read[par] = A(lambda e: e.copy(dst[:, :, bass.ds(tile * P, P)],
                                                   bank[:, 0:D].rearrange("p (k c) -> p k c", k=KD)))
                else:
                    for k in range(KD):
                        read[par] = A(lambda e: e.mul(dst[:, k, bass.ds(tile * P, P)], bank[:, k * P:(k + 1) * P],
                                                      gain[:, k:k + 1]))
                if per_tile:
                    read[par] = per_tile(tile, par, bank, read[par])
            fence(spare=ahead)

    logits = sb("logits", [P, NT, E])
    wide = small[:, 0:4 * NT * E].rearrange("p (n t e) -> p n t e", n=4, e=E)
    w_gate = small[:, 4 * NT * E:4 * NT * E + KD * E].rearrange("p (k e) -> p k e", k=KD)
    b_gate = small[0:1, 4 * NT * E + KD * E:4 * NT * E + KD * E + E]

    def router(with_bias, gain=None):
        def work(tile, par, bank, after):
            A.wait(after)
            if gain is None:
                A(lambda e: e.copy(xnTt[:, par, :, :].rearrange("p k c -> p (k c)"), bank[:, 0:D]))
            else:
                for k in range(KD):
                    A(lambda e: e.mul(xnTt[:, par, k, :], bank[:, k * P:(k + 1) * P], gain[:, k:k + 1]))
            PE.wait(A.last())
            o = bank[:, D:D + E]
            if with_bias:
                nc.tensor.matmul(o, ones[0:1, :], b_gate, start=True, stop=False)
            for k in range(KD):
                ins = nc.tensor.matmul(o, xnTt[:, par, k, :], w_gate[:, k, :], start=(k == 0 and not with_bias),
                                       stop=(k == KD - 1))
            return A(lambda e: e.copy(logits[:, tile, :], o), PE.mark(ins))
        return work

    def over(v):
        return v.unsqueeze(2).to_broadcast([P, NT, E])

    def first_best(best, scores_, top, order):
        V(lambda e: e.tensor_reduce(top, scores_, AX.X, ALU.max))
        V(lambda e: e.tensor_tensor(best, scores_, over(top), ALU.is_equal))
        V(lambda e: e.tensor_tensor(best, best, order.unsqueeze(1).to_broadcast([P, NT, E]), ALU.mult))
        V(lambda e: e.tensor_reduce(rank[:, :], best, AX.X, ALU.max))
        V(lambda e: e.tensor_tensor(best, best, over(rank[:, :]), ALU.is_equal))

    rank = sb("rank", [P, NT])
    top_a = sb("top_a", [P, NT])
    top_b = sb("top_b", [P, NT])
    order = sb("order", [P, E])

    def descending():
        for e_ in range(E):
            G(lambda e: e.memset(order[:, e_:e_ + 1], float(E - e_)))

    def finish():
        o = None
        for bt in range(B):
            o = load(dma_a, out[bt].rearrange("(t p) d -> p t d", p=P), x[:, bt * TB:(bt + 1) * TB, :])
        SP.wait(o)

    def head64(ap):
        return ap.rearrange("(k p) n h -> p k (n h)", p=P)

    def begins(stage):
        return STOP is None or (STOP[1] < stage <= STOP[0])

    if begins(0):
        load(dma_c, bias[:, :, :], a["mask_Bx1xSxS2_ff0"][:, 0].rearrange("b (t p) s -> p (b t) s", p=P))
        clear_expanded()
        prepare_wide(head64(a["L0_xattn_wq"]), head64(a["L0_xattn_wk"]), head64(a["L0_xattn_wv"]),
                     a["L0_xattn_wo"].rearrange("n h d -> (n h) d").rearrange("(t p) d -> p t d", p=P), lambda: None)
        statistics(x, 1e-5)
        fence()
        attention(x, WIDE, 1.0, True, tanh_g[:, 0:1])

    def quantised_ffn():
        NL, R = 6, 32
        WT = weights[:, 0:NL * 2 * D].rearrange("p (j k o) -> p j k o", j=NL, k=KD)
        q = weights[:, NL * 2 * D:2 * NL * 2 * D].bitcast(I32).rearrange("p (j h d) -> p j h d", j=NL, h=2)
        z = prep[:, 0:NT * D].rearrange("p (t d) -> p t d", t=NT)
        rest = prep[:, NT * D:]
        sc = rest[:, 0:192].rearrange("p (j h g) -> p j h g", j=NL, h=2)
        lb = rest[:, 192:576].rearrange("p (j h r) -> p j h r", j=NL, h=2)
        la = rest[0:R, 576:2112].rearrange("p (j d) -> p j d", j=NL)
        brow = rest[0:1, 2112:3648].rearrange("p (j o) -> p j o", j=NL)
        gamma = rest[:, 3648:3654].rearrange("p (b k) -> p b k", b=3)
        beta = rest[:, 3654:3660].rearrange("p (b k) -> p b k", b=3)
        wf = rest[:, 3660:3660 + 2 * D].rearrange("p (n d) -> p n d", n=2)
        lbT = rest[0:R, 3660 + 2 * D:3660 + 2 * D + 2 * P].rearrange("p (n c) -> p n c", n=2)
        l_q = load(dma_a, q, a["L0_ffn_qweights"].rearrange("j (h p) d -> p j h d", p=P))
        load(dma_b, sc, a["L0_ffn_scales"].rearrange("j (h p) g -> p j h g", p=P))
        load(dma_b, lb, a["L0_ffn_lora_b"].rearrange("j (h p) r -> p j h r", p=P))
        load(dma_b, la, a["L0_ffn_lora_a"].rearrange("j r d -> r j d"))
        load(dma_b, brow, a["L0_ffn_biases"].rearrange("(o j) d -> o j d", o=1))
        for blk in range(3):
            load(dma_b, gamma[:, blk, :], a["L0_ffn_ln_gamma"][blk].rearrange("(k p) -> p k", p=P), columns=True)
            l_s = load(dma_b, beta[:, blk, :], a["L0_ffn_ln_beta"][blk].rearrange("(k p) -> p k", p=P), columns=True)
        statistics(x, 1e-5)
        for t in range(NT):
            normalise(inner[:, t, :], x, t)
        ring = Ring([0, 1, 2, 3, 4, 5, 6, 7])
        V.wait(l_q, l_s)
        PE.wait(l_s)
        lb_read, wf_read = [None, None], [None, None]
        for n in range(2 * NL):
            j, h, i = n // 2, n % 2, n % 2
            bank, free = ring.take()
            PE.wait(free)
            m = PE.mark(nc.tensor.transpose(psum[0:R, bank, 0:P], lb[:, j, h, :], ident[:, :]))
            cp = A(lambda e: e.copy(lbT[:, i, :], psum[0:R, bank, 0:P]), m, lb_read[i])
            PE.wait(cp)
            lora = PE.mark(nc.tensor.matmul(psum[:, bank, D:2 * D], lbT[:, i, :], la[:, j, :], start=True, stop=True))
            lb_read[i] = lora
            V(lambda e: e.tensor_scalar(wf[:, i, :], q[:, j, h, :], 1.0 / 7.5, -1.0, ALU.mult, ALU.add), wf_read[i])
            w3d = wf[:, i, :].rearrange("p (g c) -> p g c", g=16)
            V(lambda e: e.tensor_tensor(w3d, w3d, sc[:, j, h, :].unsqueeze(2).to_broadcast([P, 16, 16]), ALU.mult))
            w = V(lambda e: e.tensor_tensor(wf[:, i, :], psum[:, bank, D:2 * D], wf[:, i, :], ALU.add), lora)
            tr = turn(wf[:, i, :], psum[:, bank, 0:D], w)
            wf_read[i] = tr
            ring.give(A(lambda e: e.copy(WT[:, j, :, h * P:(h + 1) * P],
                                         psum[:, bank, 0:D].rearrange("p (k c) -> p k c", k=KD)), tr))
        fence()
        with nc.Fori(0, 3) as blk:
            turned_tile = [xnTt[:, 0], xnTt[:, 1], qTt[:, 0], qTt[:, 1]]
            for layer in range(2):
                ring = Ring([0, 1, 2, 3, 4, 5, 6, 7])
                lhs_read = [None] * 4
                waiting = []

                def product(t, bank, cp):
                    PE.wait(cp)
                    y = psum[:, bank, D:2 * D]
                    nc.tensor.matmul(y, ones[0:1, :], brow[:, 2 * blk + layer, :], start=True, stop=False)
                    for k in range(KD):
                        ins = nc.tensor.matmul(y, turned_tile[t % 4][:, k, :], WT[:, 2 * blk + layer, k, :],
                                               start=False, stop=(k == KD - 1))
                    m = PE.mark(ins)
                    lhs_read[t % 4] = m
                    if layer == 0:
                        ring.free[bank] = A(lambda e: e.copy(z[:, t, :], y), m)
                        V(lambda e: e.bn_stats(bn6[:, t, :], z[:, t, :]), A.last())
                        V(lambda e: e.bn_aggr(meanvar[:, t, :], bn6[:, t, :]))
                    else:
                        ring.free[bank] = V(lambda e: e.tensor_tensor(inner[:, t, :], y, inner[:, t, :], ALU.add), m)

                for t in range(NT):
                    bank, free = ring.take()
                    if layer == 0:
                        tr = turn(inner[:, t, :], psum[:, bank, 0:D], free)
                        cp = A(lambda e: e.copy(turned_tile[t % 4].rearrange("p k c -> p (k c)"), psum[:, bank, 0:D]),
                               tr, lhs_read[t % 4])
                    else:
                        n = V(lambda e: e.tensor_scalar(z[:, t, :], z[:, t, :], meanvar[:, t, 0:1], rstd[:, t:t + 1],
                                                        ALU.subtract, ALU.mult))
                        tr = turn(z[:, t, :], psum[:, bank, 0:D], n, free)
                        for k in range(KD):
                            cp = A(lambda e: e.activation(turned_tile[t % 4][:, k, :], psum[:, bank, k * P:(k + 1) * P],
                                                          ACT.Gelu, bias=beta[:, bass.ds(blk, 1), k],
                                                          scale=gamma[:, bass.ds(blk, 1), k]), tr, lhs_read[t % 4])
                    waiting.append((t, bank, cp))
                    if len(waiting) > 2:
                        product(*waiting.pop(0))
                for w in waiting:
                    product(*w)
                if layer == 0:
                    reciprocal_root(meanvar[:, :, 1], 1e-5, None)
            fence()
        for t in range(NT):
            V(lambda e: e.scalar_tensor_tensor(x[:, t, :], inner[:, t, :], tanh_g[:, 4:5], x[:, t, :],
                                               ALU.mult, ALU.add))
        fence()

    if begins(1):
        quantised_ffn()

    def decoder():
        K = 32
        mask = small[:, 0:B * S2].rearrange("p (b s) -> p b s", b=B)
        wth, bth, wto, bto = (small[:, 160 + 32 * n:192 + 32 * n] for n in range(4))
        b2 = small[:, 320:320 + D]
        load(dma_a, mask, a["mask_Bx1x1xS2_ff0"].rearrange("b x y s -> (x y) b s").to_broadcast([P, B, S2]))
        statistics(x, 1e-5)
        for t in range(NT):
            normalise(inner[:, t, :], x, t)
        clear_expanded()
        wq4, wk4, wv4 = (a["L1_xattn_" + n].rearrange("l (k p) n h -> l p k (n h)", p=P) for n in ("Wq", "Wk", "Wv"))
        wo4 = a["L1_xattn_Wo"].rearrange("l n h d -> l (n h) d").rearrange("l (t p) d -> l p t d", p=P)
        with nc.Fori(0, 4) as layer:
            def vector_of(name, n):
                return a[name][layer].rearrange("(o n) -> o n", o=1).to_broadcast([P, n])

            load(dma_e, wth, a["L1_xattn_Wth"][layer].to_broadcast([P, K]))
            load(dma_e, bth, vector_of("L1_xattn_bth", K))
            load(dma_e, wto, a["L1_xattn_Wto"][layer].rearrange("k o -> o k").to_broadcast([P, K]), columns=True)
            load(dma_e, b2, vector_of("L1_xattn_bf2", D))
            got = load(dma_e, bto[:, 0:1], vector_of("L1_xattn_bto", 1), columns=True)
            flat_bias = bias[:, :, :].rearrange("p t s -> p (t s)")
            flat_side = fside[:, :, :].rearrange("p t s -> p (t s)")
            for bt in range(B):
                V(lambda e: e.tensor_scalar(bias[:, bt * TB:(bt + 1) * TB, :],
                                            mask[:, bt, :].unsqueeze(1).to_broadcast([P, TB, S2]),
                                            bto[:, 0:1], None, ALU.add), got)
            used = [None, None]
            steps = []

            def distance_step():
                if len(steps) == K:
                    return
                j = len(steps)
                steps.append(j)
                r = prob[:, j % 2, :]
                m = A(lambda e: e.activation(r, flat_side, ACT.Relu, scale=wth[:, j:j + 1], bias=bth[:, j:j + 1]),
                      got, used[j % 2])
                used[j % 2] = V(lambda e: e.scalar_tensor_tensor(flat_bias, r, wto[:, j:j + 1], flat_bias,
                                                                 ALU.mult, ALU.add), m)

            prepare_wide(wq4[layer], wk4[layer], wv4[layer], wo4[layer], distance_step)
            while len(steps) < K:
                distance_step()
            statistics(inner, None, 1e-6)
            fence()
            for h in range(2):
                fetch_expert(ahead, h, a["L1_xattn_Wf1"][layer][:, h * F:(h + 1) * F], None,
                             a["L1_xattn_Wf2"][layer][h * F:(h + 1) * F, :], a["L1_xattn_bf1"][layer][h * F:(h + 1) * F])
            attention(inner, WIDE, 1.0, True, 1.0)
            statistics(inner, None, 1e-6)
            fence()
            feed_input(inner, xnT)
            fence()
            for t in range(NT):
                V(lambda e: e.tensor_tensor(inner[:, t, :], inner[:, t, :], b2, ALU.add))
            experts(inner, [(0, None), (1, None)], ACT.Relu, False, lambda s: xnT, lambda s, tile: 1.0)
            fence()
        statistics(inner, None, 1e-6)
        for t in range(NT):
            par = t % 2
            normalise(xn[:, par, :], inner, t)
            V(lambda e: e.scalar_tensor_tensor(x[:, t, :], xn[:, par, :], tanh_g[:, 1:2], x[:, t, :], ALU.mult, ALU.add))
        fence()

    if begins(2):
        decoder()

    def one_gate_experts():
        gw = small[0:E, 600:600 + D]
        b2 = small[0:E, 600:600 + D]
        def fetch(lane, s, e, *after):
            return fetch_expert(lane, s, a["L1_ffn_w1"][e], None, a["L1_ffn_w2"][e], a["L1_ffn_b1"][e], *after)
        fetch(ahead, 0, 0)
        got = load(dma_b, gw, a["L1_ffn_gate_w"])
        load(dma_b, rms_w[:, :], bcast(a["L1_ffn_rms_w"], E))
        got = load(dma_b, b_gate, a["L1_ffn_gate_b"].rearrange("(o e) -> o e", o=1))
        for k in range(KD):
            PE.wait(got)
            m = PE.mark(nc.tensor.transpose(psum[:, k, 0:E], gw[:, k * P:(k + 1) * P], ident[0:E, 0:E]))
            A(lambda e: e.copy(w_gate[:, k, :], psum[:, k, 0:E]), m)
        statistics(x, 1e-5)
        fence()
        feed_input(x, xnT, router(True))
        got = load(dma_b, b2, a["L1_ffn_b2"])
        sq = wide[:, 0]
        V(lambda e: e.tensor_tensor(sq, logits[:, :, :], logits[:, :, :], ALU.mult))
        V(lambda e: e.tensor_reduce(top_a[:, :], sq, AX.X, ALU.add))
        V(lambda e: e.tensor_scalar(top_a[:, :], top_a[:, :], 1.0 / E, float(np.finfo(np.float32).eps), ALU.mult, ALU.add))
        A(lambda e: e.activation(top_a[:, :], top_a[:, :], ACT.Sqrt), V.last())
        V(lambda e: e.reciprocal(top_a[:, :], top_a[:, :]), A.last())
        V(lambda e: e.tensor_tensor(sq, logits[:, :, :], over(top_a[:, :]), ALU.mult))
        V(lambda e: e.tensor_tensor(sq, sq, rms_w[:, :].unsqueeze(1).to_broadcast([P, NT, E]), ALU.mult))
        V(lambda e: e.tensor_reduce(top_b[:, :], sq, AX.X, ALU.max))
        V(lambda e: e.tensor_tensor(sq, sq, over(top_b[:, :]), ALU.subtract))
        A(lambda e: e.activation(sq, sq, ACT.Exp, scale=2.0), V.last())
        V(lambda e: e.tensor_reduce(top_a[:, :], sq, AX.X, ALU.add), A.last())
        V(lambda e: e.reciprocal(top_a[:, :], top_a[:, :]))
        V(lambda e: e.tensor_scalar(top_b[:, :], top_a[:, :], 1e-6, None, ALU.add))
        V(lambda e: e.reciprocal(top_b[:, :], top_b[:, :]))
        V(lambda e: e.tensor_tensor(top_a[:, :], top_a[:, :], top_b[:, :], ALU.mult))
        V(lambda e: e.tensor_scalar(gates[:, :, 0], top_a[:, :], tanh_g[:, 5:6], None, ALU.mult))
        PE.wait(got)
        m = PE.mark(nc.tensor.matmul(psum[:, 0, 0:D], ones[0:E, :], b2, start=True, stop=True))
        for t in range(NT):
            V(lambda e: e.scalar_tensor_tensor(x[:, t, :], psum[:, 0, 0:D], gates[:, t, 0:1], x[:, t, :],
                                               ALU.mult, ALU.add), m)
        fence()
        expert_pairs(x, fetch, ACT.Gelu, False, lambda s: xnT, lambda e, tile: gates[:, tile, 0:1])

    rms_w = sb("rms_w", [P, E])
    if begins(3):
        one_gate_experts()

    def block_diagonal(dst, lhs, rhs, bank, landed):
        PE.wait(landed)
        m = PE.mark(nc.tensor.matmul(psum[:, bank, 0:P], lhs, rhs, start=True, stop=True))
        b3 = block[:, :].unsqueeze(2).to_broadcast([P, 8, 16])
        V(lambda e: e.tensor_tensor(dst.rearrange("p (h c) -> p h c", h=8),
                                    psum[:, bank, 0:P].rearrange("p (h c) -> p h c", h=8), b3, ALU.mult), m)

    def shared_head_attention():
        rep = weights[0:16, 0:3 * P].rearrange("p (n h c) -> p n h c", n=3, h=8)
        raw = weights[0:16, 3 * P:3 * P + 48].rearrange("p (n c) -> p n c", n=3)
        bd = weights[:, 512:512 + 2 * P].rearrange("p (n c) -> p n c", n=2)
        wo_rows = weights[:, 1024:1024 + KD * D].rearrange("p (k d) -> p k d", k=KD)
        woT = weights[:, 2048:2048 + KD * D].rearrange("p (k d) -> p k d", k=KD)
        bo = weights[0:1, 3072:3072 + D]
        mask_i = prep[:, 7000:7000 + NT * S2].bitcast(I32).rearrange("p (t s) -> p t s", t=NT)
        for n, name in enumerate(("Wk", "Wq", "Wv")):
            got = load(dma_a, raw[:, n, :], a["L2_xattn_" + name])
        got_o = load(dma_b, wo_rows, a["L2_xattn_Wo"].rearrange("(k p) d -> p k d", p=P))
        load(dma_b, bo, a["L2_xattn_bo"].rearrange("(o d) -> o d", o=1))
        got_m = load(dma_c, mask_i, a["mask_Bx1xSxS2_ik1"][:, 0].rearrange("b (t p) s -> p (b t) s", p=P))
        statistics(x, 1e-5)
        V(lambda e: e.tensor_scalar(bias[:, :, :], mask_i, 0.0, -1e20, ALU.is_equal, ALU.mult), got_m)
        for n in range(3):
            V(lambda e: e.tensor_copy(rep[:, n, :, :], raw[:, n, :].unsqueeze(1).to_broadcast([16, 8, 16])), got)
        wide_rep = rep[:, :, :, :].rearrange("p n h c -> p n (h c)")
        block_diagonal(bd[:, 0, :], wide_rep[:, 0, :], wide_rep[:, 1, :], 0, V.last())
        eye = weights[0:16, 3400:3400 + P].rearrange("p (h c) -> p h c", h=8)
        V(lambda e: e.tensor_copy(eye, ident[0:16, 0:16].unsqueeze(1).to_broadcast([16, 8, 16])))
        block_diagonal(bd[:, 1, :], wide_rep[:, 2, :], eye.rearrange("p h c -> p (h c)"), 1, V.last())
        for k in range(KD):
            PE.wait(got_o)
            for o in range(KD):
                ins = nc.tensor.transpose(psum[:, 2 + k, o * P:(o + 1) * P], wo_rows[:, o, k * P:(k + 1) * P], ident[:, :])
            turned_ = V(lambda e: e.tensor_copy(woT[:, k, :], psum[:, 2 + k, 0:D]), PE.mark(ins))

        def projection(n):
            def of(dst, g):
                PE.wait(V.last())
                return PE.mark(nc.tensor.matmul(dst, bd[:, n, :], ctxT[:, g, :], start=True, stop=True))
            return of
        prepare_narrow(projection(0), projection(1), woT, turned_, None)
        fence()
        attention(x, NARROW, 1.0 / 16.0, True, tanh_g[:, 2:3], out_bias=bo)

    if begins(4):
        shared_head_attention()

    def best_expert():
        def fetch(lane, s, e, *after):
            return fetch_expert(lane, s, a["L2_ffn_rt_gate"][e], a["L2_ffn_rt_up"][e], a["L2_ffn_rt_down"][e], None, *after)
        fetch(ahead, 0, 0)
        fetch_expert(ahead, 1, a["L2_ffn_sh_gate"], a["L2_ffn_sh_up"], a["L2_ffn_sh_down"], None)
        descending()
        load(dma_b, w_gate, a["L2_ffn_gate_w"].rearrange("(k p) e -> p k e", p=P))
        statistics(x, 1e-5)
        fence()
        feed_input(x, xnT, router(False))
        best = wide[:, 0]
        first_best(best, logits[:, :, :], top_a[:, :], order[:, :])
        V(lambda e: e.tensor_scalar(gates[:, :, :], best, tanh_g[:, 6:7], None, ALU.mult))
        A(lambda e: e.activation(top_a[:, :], top_a[:, :], ACT.Exp, scale=-1.0), V.last())
        V(lambda e: e.tensor_scalar(top_a[:, :], top_a[:, :], 1.0, None, ALU.add), A.last())
        V(lambda e: e.reciprocal(top_a[:, :], top_a[:, :]))
        V(lambda e: e.tensor_tensor(rstd[:, :], rstd[:, :], top_a[:, :], ALU.mult))
        fence()
        feed_input(x, sT)
        experts(x, [(1, None)], ACT.Silu, True, lambda s: xnT, lambda s, tile: tanh_g[:, 6:7])
        fence()
        expert_pairs(x, fetch, ACT.Silu, True, lambda s: sT, lambda e, tile: gates[:, tile, bass.ds(e, 1)])

    if begins(5):
        best_expert()

    def biased_attention():
        w = [weights[:, n * KD * D:(n + 1) * KD * D].rearrange("p (k d) -> p k d", k=KD) for n in range(4)]
        kv_bias = weights[:, 2400:2404]
        bq = weights[:, 2404:2406]
        bo = weights[0:1, 2410:2410 + D]
        for n, name in enumerate(("Wq", "Wk", "Wv", "Wo")):
            got = load(dma_a, w[n], a["L3_xattn_" + name].rearrange("(k p) d -> p k d", p=P))
        for g in range(KD):
            for n, name in enumerate(("bk", "bv")):
                load(dma_b, kv_bias[:, 2 * g + n:2 * g + n + 1],
                     a["L3_xattn_" + name][g * P:(g + 1) * P].rearrange("(p o) -> p o", o=1), columns=True)
            load(dma_b, bq[:, g:g + 1], a["L3_xattn_bq"][g * P:(g + 1) * P].rearrange("(p o) -> p o", o=1), columns=True)
        got_b = load(dma_b, bo, a["L3_xattn_bo"].rearrange("(o d) -> o d", o=1))
        statistics(x, 1e-5)
        V.wait(got_b)

        def projection(n):
            def of(dst, g):
                PE.wait(got)
                for k in range(KD):
                    ins = nc.tensor.matmul(dst, w[n][:, k, g * P:(g + 1) * P], ctxT[:, k, :], start=(k == 0), stop=(k == KD - 1))
                return PE.mark(ins)
            return of
        prepare_narrow(projection(1), projection(2), w[3], got, kv_bias)
        fence()
        q_read = [None, None]

        def project(par, so, after):
            PE.wait(after)
            for g in range(KD):
                for k in range(KD):
                    ins = nc.tensor.matmul(so[:, g * P:(g + 1) * P], w[0][:, k, g * P:(g + 1) * P], xnTt[:, par, k, :],
                                           start=(k == 0), stop=(k == KD - 1))
            m = PE.mark(ins)
            for g in range(KD):
                r = A(lambda e: e.activation(qTt[:, par, g, :], so[:, g * P:(g + 1) * P], ACT.Identity,
                                             bias=bq[:, g:g + 1]), m)
            return r
        attention(x, NARROW, 0.25, False, tanh_g[:, 3:4], project=project, out_bias=bo)

    if begins(6):
        biased_attention()

    def latent_block():
        L = H * HD3
        EPS = 1e-5
        PARTS = 3
        STACK = PARTS * PARTS * HD3
        ROWS = STACK + PARTS
        SLOTS, TURN = 4, H
        q_dram = scratch("q_heads", (B * H, PARTS, HD3, S), BF16)
        qk_parts = scratch("qk_parts", (2, PARTS, B * H, HD3, S), BF16)
        k_dram = scratch("k_heads", (B * H, PARTS, PARTS, HD3, S), BF16)
        heads = weights[0:ROWS, 0:SLOTS * S].bitcast(BF16).rearrange("p (n s c) -> p n s c", n=2, s=SLOTS)
        values = weights[:, 4096:4096 + NT * H * 9].rearrange("p (t h c) -> p t h c", t=NT, h=H)
        small_w = weights[:, 6400:8192]
        PT_COLS = sum(S - j * P for j in range(TB))
        expT = prep[:, 0:2 * PT_COLS].rearrange("p (n c) -> p n c", n=2)
        Kflat = Kt[:, :, :, :].rearrange("p b k c -> p (b k c)")
        Vflat = Vt[:, :, :, :].rearrange("p b c d -> p (b c d)")
        cosT, sinT = Kflat[:, 0:S], Kflat[:, S:2 * S]
        masks = Kflat[:, 2 * S:2 * S + 192].bitcast(BF16).rearrange("p (n c) -> p n c", n=3)
        causal, causalT, ident16 = (masks[:, n, :] for n in range(3))
        mrow = Kflat[0:TB, 3 * S:3 * S + 2 * P].rearrange("p (n c) -> p n c", n=2)
        mparts = Kflat[0:TB, 3 * S + 2 * P:3 * S + 5 * P].bitcast(BF16).rearrange("p (n a c) -> p n a c", n=2, a=PARTS)
        head_values = Kflat[:, 4 * S + P:4 * S + P + 2 * TB * 9].rearrange("p (n t c) -> p n t c", n=2, c=9)
        sums = Vflat[0:9, 0:2 * S].rearrange("p (n c) -> p n c", n=2)
        qT, kT = Vflat[:, 0:NT * P], Vflat[:, NT * P:2 * NT * P]
        cT = Vflat[:, 2 * NT * P:2 * NT * P + 2 * GRP].rearrange("p (n c) -> p n c", n=2)
        wd = prep[:, 0:KD * L].rearrange("p (k l) -> p k l", k=KD)
        wqkv = prep[:, 256:256 + 5 * L].rearrange("p (n l) -> p n l", n=5)
        w_up = small_w[:, 0:D]
        gain = small_w[:, 256:260].rearrange("p (n k) -> p n k", n=2)
        rope = prep[:, 1024:1024 + 4 * GRP].rearrange("p (n c) -> p n c", n=4)
        split = prep[:, 3072:3072 + 2 * PARTS * S].bitcast(BF16).rearrange("p (n a c) -> p n a c", n=2, a=PARTS)
        attended = shared[:, 0:NT * L].rearrange("p (t l) -> p t l", t=NT)
        maxima = row[:, :, 0:TB]
        shares = row[:, :, 16:16 + TB]

        load(dma_a, cosT, a["rope_cos"])
        load(dma_a, sinT, a["rope_sin"])
        load(dma_b, wd, a["L3_ffn_w_down"].rearrange("(k p) l -> p k l", p=P))
        for n, name in enumerate(("wq", "wk", "wv")):
            load(dma_b, wqkv[:, n, :], a["L3_ffn_" + name])
        load(dma_b, w_up, a["L3_ffn_w_up"])
        for n, name in enumerate(("g1", "g2")):
            got = load(dma_b, gain[:, n, :], a["L3_ffn_" + name].rearrange("(k p) -> p k", p=P), columns=True)
        load(dma_c, w_gate, a["L3_ffn_router_w"].rearrange("(k p) e -> p k e", p=P))
        descending()
        for mask_, sign in ((causal, 1), (causalT, -1)):
            G(lambda e: e.memset(mask_, 0.0))
            G(lambda e: e.affine_select(out=mask_, in_=mask_, compare_op=ALU.is_ge, fill=NEG, base=0,
                                        pattern=[[-sign, P]], channel_multiplier=sign))
        G(lambda e: e.tensor_copy(ident16, ident[:, :]))
        G(lambda e: e.memset(values[:, :, :, :].rearrange("p t h c -> p (t h c)"), 1.0))
        G(lambda e: e.memset(heads[:, 1, :, :].rearrange("p s c -> p (s c)"), 1.0))
        statistics(x, 1e-5)
        for t in range(NT):
            normalise(inner[:, t, :], x, t)

        def mean_square_statistics():
            statistics(inner, EPS)
            sq = top_a[:, :]
            V(lambda e: e.tensor_tensor(sq, meanvar[:, :, 0], meanvar[:, :, 0], ALU.mult))
            V(lambda e: e.tensor_tensor(meanvar[:, :, 1], meanvar[:, :, 1], sq, ALU.add))
            reciprocal_root(meanvar[:, :, 1], EPS, None)
            V(lambda e: e.memset(meanvar[:, :, 0], 0.0))

        mean_square_statistics()
        for n in range(2):
            w = wqkv[:, n, :].rearrange("p (j two) -> p j two", two=2)
            sw = wqkv[:, 3 + n, :].rearrange("p (j two) -> p j two", two=2)
            V(lambda e: e.tensor_scalar(sw[:, :, 0], w[:, :, 1], -1.0, None, ALU.mult), got)
            V(lambda e: e.tensor_scalar(sw[:, :, 1], w[:, :, 0], 1.0, None, ALU.mult))
        fence()
        feed_input(inner, xnT, gain=gain[:, 0, :])
        cT_read = None
        for g in range(NG):
            par = g % 2
            for k in range(KD):
                ins = nc.tensor.matmul(psum[:, 0, :], wd[:, k, :], xnT[:, k, g * GRP:(g + 1) * GRP],
                                       start=(k == 0), stop=(k == KD - 1))
            cp = A(lambda e: e.copy(cT[:, par, :], psum[:, 0, :]), PE.mark(ins))
            PE.wait(cp, cT_read)
            for n, w in enumerate((0, 3, 1, 4)):
                m = PE.mark(nc.tensor.matmul(psum[:, 1 + n, :], wqkv[:, w, :], cT[:, par, :], start=True, stop=True))
            for t in range(TG):
                mv = PE.mark(nc.tensor.matmul(psum[:, 5, t * P:(t + 1) * P], cT[:, par, t * P:(t + 1) * P],
                                              wqkv[:, 2, :], start=True, stop=True))
            at = (g * GRP) % S
            for n, dst in ((0, qT), (2, kT)):
                V(lambda e: e.tensor_tensor(rope[:, n, :], psum[:, 1 + n, :], cosT[:, at:at + GRP], ALU.mult), m)
                V(lambda e: e.tensor_tensor(rope[:, n + 1, :], psum[:, 2 + n, :], sinT[:, at:at + GRP], ALU.mult))
                V(lambda e: e.tensor_tensor(dst[:, g * GRP:(g + 1) * GRP], rope[:, n, :], rope[:, n + 1, :], ALU.add))
            cT_read = A(lambda e: e.copy(values[:, g * TG:(g + 1) * TG, :, 0:HD3],
                                         psum[:, 5, :].rearrange("p (t h c) -> p t h c", t=TG, h=H)), mv)
            PE.wait(V.last(), cT_read)
        for n, src in enumerate((qT, kT)):
            for a_ in range(PARTS):
                part = A(lambda e: e.copy(split[:, n, a_, :], src), V.last())
                if a_ < PARTS - 1:
                    V(lambda e: e.tensor_tensor(src, src, split[:, n, a_, :], ALU.subtract), part)
            for a_ in range(PARTS):
                for bt in range(B):
                    stored = load(dma_a, qk_parts[n, a_, bt * H:(bt + 1) * H].rearrange("h c s -> (h c) s"),
                                  split[:, n, a_, bt * S:(bt + 1) * S], part)
        by_head = [qk_parts[n].rearrange("a h c s -> h a (c s)") for n in range(2)]
        load(dma_b, q_dram.rearrange("h a c s -> h a (c s)"), by_head[0], stored)
        for b_ in range(PARTS):
            load(dma_b, k_dram[:, :, b_].rearrange("h a c s -> h a (c s)"), by_head[1])
        fence()

        def fetch_head(slot_, index, *after):
            lane = more_lanes[slot_]
            load(lane, heads[0:STACK, 1, slot_, :], k_dram[index].rearrange("a b c s -> (a b c) s"), *after)
            for a_ in range(PARTS):
                got_ = load(lane, heads[a_ * PARTS * HD3:(a_ + 1) * PARTS * HD3, 0, slot_, :],
                            q_dram[index].rearrange("b c s -> (b c) s"))
            return got_

        for s in range(3):
            fetch_head(s, s)
        fence()
        start = [sum(S - i * P for i in range(j)) for j in range(TB)]
        with nc.Fori(0, B * H // TURN) as i:
            free = [None, None]
            ring = Ring([4, 5])
            landed = {0: None, 1: None, 2: None}
            values_read, sums_read, exp_read, out_free = [None, None], [None, None], [None, None], None
            state = {"n": 0, "out_free": None}

            def score_maximum(h, t):
                s, n = h % SLOTS, state["n"]
                state["n"] += 1
                cols, base = (t + 1) * P, (n % 2) * 2 * BANK
                PE.wait(free[n % 2], landed[h])
                for at in range(0, cols, BANK):
                    w = min(BANK, cols - at)
                    ins = nc.tensor.matmul(flat[:, base + at:base + at + w], heads[0:STACK, 0, s, t * P:(t + 1) * P],
                                           heads[0:STACK, 1, s, at:at + w], start=True, stop=True)
                m = PE.mark(nc.tensor.matmul(flat[:, base + t * P:base + cols], ident16, causal, start=False, stop=True,
                                             skip_group_check=True))
                free[n % 2] = V(lambda e: e.tensor_reduce(maxima[:, h % 2, t:t + 1], flat[:, base:base + cols], AX.X, ALU.max), m,
                                maxima_read.get(h - 2))
                maximum_known[h] = free[n % 2]

            maximum_known, maxima_read = {}, {}

            def maxima_rows(h):
                bank, fr = ring.take()
                PE.wait(maximum_known[h], fr)
                tr = PE.mark(nc.tensor.transpose(psum[0:TB, bank, 0:P], maxima[:, h % 2, :], ident[:, :]))
                maxima_read[h] = tr
                left = mrow[:, h % 2, :]
                r = A(lambda e: e.mul(left, psum[0:TB, bank, 0:P], -1.0), tr)
                ring.give(r)
                A.wait(rows.get(h - 2))
                for a_ in range(PARTS):
                    r = A(lambda e: e.copy(mparts[:, h % 2, a_, :], left), V.last())
                    if a_ < PARTS - 1:
                        V(lambda e: e.tensor_tensor(left, left, mparts[:, h % 2, a_, :], ALU.subtract), r)
                for a_ in range(PARTS):
                    got_ = load((dma_c, dma_d)[h % 2], heads[STACK + a_:STACK + a_ + 1, 0, h % SLOTS, :],
                                mparts[:, h % 2, a_, :], r)
                return got_

            def exponentials(h, j, rows_landed):
                s = h % SLOTS
                for at in range(j * P, S, BANK):
                    w = min(BANK, S - at)
                    bank, fr = ring.take()
                    PE.wait(rows_landed, fr)
                    m = PE.mark(nc.tensor.matmul(psum[:, bank, 0:w], heads[:, 1, s, j * P:(j + 1) * P],
                                                 heads[:, 0, s, at:at + w], start=True, stop=True))
                    to = start[j] + at - j * P
                    if at == j * P:
                        m = PE.mark(nc.tensor.matmul(psum[:, bank, 0:P], ident16, causalT, start=False, stop=True,
                                                     skip_group_check=True))
                    ring.give(A(lambda e: e.activation(expT[:, h % 2, to:to + w], psum[:, bank, 0:w], ACT.Exp,
                                                       scale=float(HD3) ** -0.5), m, exp_read[h % 2]))

            def weigh(h, keys, done_exp):
                p_ = h % 2
                PE.wait(done_exp, vals[p_])
                if keys[0] == 0:
                    PE.wait(sums_read[0])
                for j in keys:
                    for lo, hi in ((0, BANK), (BANK, S)):
                        lo = max(lo, j * P)
                        if lo < hi:
                            ins = nc.tensor.matmul(flat[0:9, 6 * BANK + lo:6 * BANK + hi], head_values[:, p_, j, :],
                                                   expT[:, p_, start[j] + lo - j * P:start[j] + hi - j * P],
                                                   start=(j == 0), stop=(j == TB - 1 or (hi == BANK and j == 3)))
                return PE.mark(ins)

            def keep_sums(h, m):
                p_ = h % 2
                sums_read[0] = A(lambda e: e.copy(sums[:, p_, :], flat[0:9, 6 * BANK:8 * BANK]), m, sums_read[1])

            def divide(h):
                p_ = h % 2
                bank, fr = ring.take()
                PE.wait(sums_read[0], fr)
                o = psum[:, bank, 0:TB * 9].rearrange("p (t c) -> p t c", c=9)
                for t in range(TB):
                    ins = nc.tensor.transpose(o[:, t, :], sums[:, p_, t * P:(t + 1) * P], ident[0:9, 0:9])
                m = PE.mark(ins)
                sums_read[1] = m
                V(lambda e: e.reciprocal(shares[:, p_, :], o[:, :, HD3]), m)
                dst = attended.rearrange("p (b t) (h c) -> p b t h c", b=B, h=H)[:, i // (H // TURN), :,
                                                                                 (i * TURN + h) % H, :]
                ring.give(V(lambda e: e.tensor_tensor(dst, o[:, :, 0:HD3],
                                                      shares[:, p_, :].unsqueeze(2).to_broadcast([P, TB, HD3]), ALU.mult)))

            vals = [None, None]

            def take_values(h):
                vals[h % 2] = G(lambda e: e.tensor_copy(
                    head_values[:, h % 2, :, :],
                    values.rearrange("p (b t) h c -> p b t h c", b=B)[:, i // (H // TURN), :, (i * TURN + h) % H, :]),
                    values_read[h % 2])

            rows, done_exp = {}, {}
            for h in range(2):
                for t in range(TB):
                    score_maximum(h, t)
                rows[h] = maxima_rows(h)
            for h in range(TURN + 1):
                if h < TURN:
                    nxt = fetch_head((h + 3) % SLOTS, (i * TURN + h + 3) % (B * H), PE.last())
                    if h + 3 < TURN:
                        landed[h + 3] = nxt
                    take_values(h)
                for j in range(TB):
                    if h < TURN:
                        exponentials(h, j, rows[h])
                    if h + 2 < TURN:
                        score_maximum(h + 2, j)
                    if h >= 1:
                        m = weigh(h - 1, (j,), done_exp[h - 1])
                    if j == 0 and 2 <= h + 1 < TURN:
                        rows[h + 1] = maxima_rows(h + 1)
                    if j == 3 and h >= 2:
                        divide(h - 2)
                if h < TURN:
                    done_exp[h] = A.last()
                if h >= 1:
                    exp_read[(h - 1) % 2] = values_read[(h - 1) % 2] = m
                    keep_sums(h - 1, m)
            divide(TURN - 1)
            fence()

        oT_read, free = [None, None], [None, None]
        for t in range(NT):
            par = t % 2
            bank = psum[:, par, :]
            PE.wait(free[par])
            tr = PE.mark(nc.tensor.transpose(bank[:, 0:P], attended[:, t, :], ident[:, :]))
            cp = A(lambda e: e.copy(xnTt[:, par, 0, :], bank[:, 0:P]), tr, oT_read[par])
            PE.wait(cp)
            m = PE.mark(nc.tensor.matmul(bank[:, D:2 * D], xnTt[:, par, 0, :], w_up, start=True, stop=True))
            oT_read[par] = m
            free[par] = V(lambda e: e.tensor_tensor(inner[:, t, :], bank[:, D:2 * D], inner[:, t, :], ALU.add), m)
        mean_square_statistics()
        gain2 = small[:, 600:602]
        V(lambda e: e.tensor_copy(gain2, gain[:, 1, :]))
        fence()

        def fetch(lane, s, e, *after):
            return fetch_expert(lane, s, a["L3_ffn_w1"][e], a["L3_ffn_w3"][e], a["L3_ffn_w2"][e], None, *after)
        fetch(ahead, 0, 0)
        feed_input(inner, xnT, router(False, gain2), gain=gain2)
        p, first_, second_, left = (wide[:, n] for n in range(4))
        V(lambda e: e.tensor_reduce(top_a[:, :], logits[:, :, :], AX.X, ALU.max))
        V(lambda e: e.tensor_tensor(p, logits[:, :, :], over(top_a[:, :]), ALU.subtract))
        A(lambda e: e.activation(p, p, ACT.Exp), V.last())
        V.wait(A.last())
        first_best(first_, p, top_a[:, :], order[:, :])
        V(lambda e: e.scalar_tensor_tensor(left, first_, -2.0, p, ALU.mult, ALU.add))
        first_best(second_, left, top_b[:, :], order[:, :])
        V(lambda e: e.tensor_tensor(first_, first_, second_, ALU.add))
        V(lambda e: e.tensor_tensor(top_a[:, :], top_a[:, :], top_b[:, :], ALU.add))
        V(lambda e: e.reciprocal(top_a[:, :], top_a[:, :]))
        V(lambda e: e.tensor_tensor(p, p, over(top_a[:, :]), ALU.mult))
        V(lambda e: e.tensor_tensor(p, p, first_, ALU.mult))
        V(lambda e: e.tensor_scalar(gates[:, :, :], p, tanh_g[:, 7:8], None, ALU.mult))
        for t in range(NT):
            V(lambda e: e.scalar_tensor_tensor(x[:, t, :], inner[:, t, :], tanh_g[:, 7:8], x[:, t, :], ALU.mult, ALU.add))
        fence()
        expert_pairs(x, fetch, ACT.Silu, True, lambda s: xnT, lambda e, tile: gates[:, tile, bass.ds(e, 1)])

    if begins(7):
        latent_block()
    finish()


_TYPES = {"f": F32, "i": I32}


def rotation_tables():
    freq = np.float32(1.0) / np.float32(10000.0) ** (np.arange(0, HD3, 2, dtype=np.float32) / np.float32(HD3))
    angle = freq[:, None] * np.arange(S, dtype=np.float32)[None, :]
    rows = np.tile(np.repeat(angle, 2, axis=0), (H, 1))
    return np.cos(rows).astype(np.float32), np.sin(rows).astype(np.float32)


def kernel(**inputs):
    import concourse.bacc as bacc
    from concourse.bass_utils import run_bass_kernel_spmd

    nc = bacc.Bacc("TRN2", target_bir_lowering=False, num_devices=1)
    arrays, aps = {}, {}
    for name, value in inputs.items():
        v = np.ascontiguousarray(value)
        arrays["in_" + name] = v
        aps[name] = nc.dram_tensor("in_" + name, v.shape, _TYPES[v.dtype.kind], kind="ExternalInput").ap()
    for name, table in zip(("rope_cos", "rope_sin"), rotation_tables()):
        arrays["in_" + name] = table
        aps[name] = nc.dram_tensor("in_" + name, table.shape, F32, kind="ExternalInput").ap()
    out = nc.dram_tensor("out_0", (B, S, D), F32, kind="ExternalOutput").ap()
    program(nc, aps, out)
    r = run_bass_kernel_spmd(nc, [arrays], core_ids=[0])
    return r.results[0]["out_0"]
```

```python
from contextlib import ExitStack

import numpy as np

import concourse.bass as bass
from concourse import mybir
from concourse.alu_op_type import AluOpType as ALU

F32 = mybir.dt.float32
I32 = mybir.dt.int32
BF16 = mybir.dt.bfloat16
ACT = mybir.ActivationFunctionType
AX = mybir.AxisListType

P = 128
B, S, D = 2, 1024, 256
KD = D // P
TB = S // P
NT = B * TB
H, S2 = 16, 77
HK = H * S2
CH = -(-HK // P)
LASTROWS = HK - (CH - 1) * P
HE = H * 64
NTE = HE // P
PAIR = 2 * S2
VPAD = P + PAIR
CTX = B * S2
E, F = 8, 512
FC = F // P
CHUNK = 256
GRP = 512
TG = GRP // P
NG = NT // TG
NEG = -1.0e30
BANK = 512
HD3 = 8
STOP = None


class Queue:

    def __init__(self, eng, sem, step=1):
        self.eng, self.sem, self.step, self.count, self.seen = eng, sem, step, 0, {}

    def wait(self, *marks):
        for mark in marks:
            if mark is None:
                continue
            queue, value = mark
            if self.seen.get(id(queue), 0) < value:
                self.eng.wait_ge(queue.sem, value)
                self.seen[id(queue)] = value

    def mark(self, ins):
        ins.then_inc(self.sem, self.step)
        self.count += self.step
        return (self, self.count)

    def last(self):
        return (self, self.count) if self.count else None

    def __call__(self, build, *after):
        self.wait(self.last(), *after)
        return self.mark(build(self.eng))


class Lane(Queue):

    def __init__(self, sem):
        super().__init__(None, sem, 16)


def program(nc, a, out):
    with ExitStack() as ctx:
        build(nc, ctx, a, out)


def build(nc, ctx, a, out):
    def sb(name, shape, dt=F32):
        return ctx.enter_context(nc.sbuf_tensor(name, shape, dt))

    def sem(name):
        return ctx.enter_context(nc.semaphore(name))

    def scratch(name, shape, dt=F32):
        return nc.dram_tensor(name, shape, dt, kind="Internal").ap()

    PE = Queue(nc.tensor, sem("pe_done"))
    V = Queue(nc.vector, sem("vector_done"))
    A = Queue(nc.scalar, sem("scalar_done"))
    G = Queue(nc.gpsimd, sem("gpsimd_done"))
    SP = Queue(nc.sync, sem("sync_unused"))
    dma_lanes = [Lane(sem(f"dma_{n}_landed")) for n in "abcdefghij"]
    dma_a, dma_b, dma_c, dma_d, dma_e, dma_f, *more_lanes = dma_lanes
    gather_lanes = [Lane(sem(f"gather_{n}_landed")) for n in "abcdefgh"]
    dma_lanes += gather_lanes
    lanes = [PE, V, A, G, *dma_lanes]

    def load(lane, dst, src, *after, columns=False):
        SP.wait(*after)
        return lane.mark(SP.eng.dma_start(dst, src, allow_slow_non_contiguous=columns))

    ahead = dma_f

    def fence(spare=None):
        for lane in dma_lanes:
            if lane is not spare:
                SP.wait(lane.last())
        for q in (PE, V, A, G):
            q.wait(q.last())
        if any(lane.count for lane in gather_lanes):
            for lane in gather_lanes:
                G.wait(lane.last())
            nc.gpsimd.dma_reset(range(gather_lanes[0].sem.num, gather_lanes[-1].sem.num + 1))
        nc.all_engine_barrier()
        for q in lanes:
            if q.count and q is not spare:
                nc.vector.sem_clear(q.sem)
        nc.all_engine_barrier()
        for q in lanes:
            if q is not spare:
                q.count = 0
        for q in (PE, V, A, G, SP):
            q.seen = {}

    x = sb("x", [P, NT, D])
    inner = sb("inner", [P, NT, D])
    Kt = sb("Kt", [P, B, KD, HK])
    Vt = sb("Vt", [P, B, CH, D])
    weights = sb("weights", [P, 4 * 2048])
    expert_w = sb("expert_w", [P, 2 * 3072])
    prep = sb("prep", [P, 2048 + NTE * B * PAIR + B * (NTE * VPAD + P)])
    shared = sb("shared", [P, 2 * HK + 2 * CH * P])
    prob = shared[:, 0:2 * HK].rearrange("p (n c) -> p n c", n=2)
    probT = shared[:, 2 * HK:].rearrange("p (n c m) -> p n c m", n=2, c=CH)
    xnT = shared[:, 0:KD * NT * P].rearrange("p (k n) -> p k n", k=KD)
    bias = sb("bias", [P, NT, S2])
    ctxT = sb("ctxT", [P, KD, CTX])
    ident = sb("ident", [P, P])
    block = sb("block", [P, 8])
    ones = sb("ones", [P, P])
    small = sb("small", [P, 880])
    bn6 = sb("bn6", [P, NT, 6])
    meanvar = sb("meanvar", [P, NT, 2])
    rstd = sb("rstd", [P, NT])
    gates = sb("gates", [P, NT, E])
    tanh_g = sb("tanh_g", [P, 8])
    xn = sb("xn", [P, 2, D])
    xnTt = sb("xnTt", [P, 2, KD, P])
    qTt = sb("qTt", [P, 2, KD, P])
    row = sb("row", [P, 2, 64])
    psum = ctx.enter_context(nc.psum_tensor("psum", [P, 8, BANK], F32))
    flat = psum[:, :, :].rearrange("p b c -> p (b c)")

    sT = inner[:, :, :].rearrange("p t d -> p (t d)").rearrange("p (k n) -> p k n", k=KD)

    def bcast(src, n):
        return src.rearrange("(o n) -> o n", o=1).to_broadcast([P, n])

    fside = sb("fside", [P, NT, S2])
    for bt in range(B):
        load(dma_a, x[:, bt * TB:(bt + 1) * TB, :], a["x"][bt].rearrange("(t p) d -> p t d", p=P))
    graw = small[:, 0:8]
    load(dma_b, graw[:, 0:4], bcast(a["g_xattn"], 4))
    load(dma_b, graw[:, 4:8], bcast(a["g_ffn"], 4))
    ctx_rows = prep[:, 0:2 * D].rearrange("p (k d) -> p k d", k=2)
    ctx_flat = a["ctx_1024"].rearrange("b s d -> (b s) d")
    load(dma_b, ctx_rows[:, 0, :], ctx_flat[0:P])
    load(dma_b, ctx_rows[0:CTX - P, 1, :], ctx_flat[P:CTX])
    load(dma_c, fside[:, :, :], a["fside_BxSxS2_0"].rearrange("b (t p) s -> p (b t) s", p=P))
    G(lambda e: e.memset(ones[:, :], 1.0))
    G(lambda e: e.affine_select(out=ident[:, :], in_=ones[:, :], compare_op=ALU.is_equal, fill=0.0,
                                base=0, pattern=[[-1, P]], channel_multiplier=1))
    G(lambda e: e.affine_select(out=block[:, :], in_=ones[:, 0:8], compare_op=ALU.is_ge, fill=0.0,
                                base=0, pattern=[[-16, 8]], channel_multiplier=1))
    const = G(lambda e: e.affine_select(out=block[:, :], in_=block[:, :], compare_op=ALU.is_ge,
                                        fill=0.0, base=15, pattern=[[16, 8]], channel_multiplier=-1))
    A(lambda e: e.activation(tanh_g[:, :], graw, ACT.Tanh), dma_b.last())
    PE.wait(const, dma_b.last())
    for k in range(KD):
        nc.tensor.transpose(psum[:, k, 0:P], ctx_rows[:, 0, k * P:(k + 1) * P], ident[:, :])
        t = PE.mark(nc.tensor.transpose(psum[:, k, P:CTX], ctx_rows[0:CTX - P, 1, k * P:(k + 1) * P],
                                        ident[0:CTX - P, 0:CTX - P]))
        V(lambda e: e.tensor_copy(ctxT[:, k, :], psum[:, k, 0:CTX]), t)
    fence()


    collected = set()

    def collect(src, tile):
        return V(lambda e: e.bn_stats(bn6[:, tile, :], src[:, tile, :]))

    def statistics(src, inside=None, outside=None):
        if id(src) not in collected:
            for t in range(NT):
                collect(src, t)
        V.wait(V.last())
        for t in range(NT):
            V.mark(nc.vector.bn_aggr(meanvar[:, t, :], bn6[:, t, :]))
        reciprocal_root(meanvar[:, :, 1], inside, outside)

    def reciprocal_root(var, inside, outside):
        V(lambda e: e.tensor_scalar(rstd[:, :], var, inside or 0.0, None, ALU.add))
        r = A(lambda e: e.activation(rstd[:, :], rstd[:, :], ACT.Sqrt), V.last())
        V.wait(r)
        if outside:
            V(lambda e: e.tensor_scalar(rstd[:, :], rstd[:, :], outside, None, ALU.add))
        V(lambda e: e.reciprocal(rstd[:, :], rstd[:, :]))

    def normalise(dst, src, t, *after):
        return V(lambda e: e.tensor_scalar(dst, src[:, t, :], meanvar[:, t, 0:1], rstd[:, bass.ds(t, 1)],
                                           ALU.subtract, ALU.mult), *after)

    def turn(src, dst_psum, *after):
        PE.wait(*after)
        for k in range(KD):
            ins = nc.tensor.transpose(dst_psum[:, k * P:(k + 1) * P], src[:, k * P:(k + 1) * P],
                                      ident[:, :])
        return PE.mark(ins)

    class Ring:

        def __init__(self, banks):
            self.banks, self.free, self.n = banks, [None] * len(banks), -1

        def take(self):
            self.n = (self.n + 1) % len(self.banks)
            return self.banks[self.n], self.free[self.n]

        def give(self, mark):
            self.free[self.n] = mark


    WqT = prep[:, 0:2048].rearrange("p (t d) -> p t d", t=NTE)
    kexp = prep[:, 2048:2048 + NTE * B * PAIR].rearrange("p (t b c) -> p t b c", t=NTE, b=B)
    vexp = prep[:, 2048 + NTE * B * PAIR:].rearrange("p (b c) -> p b c", b=B)
    vexp16 = prep[:, 2048:2048 + B * KD * HK].rearrange("p (b g c) -> p b g c", b=B, g=KD)

    def clear_expanded():
        half = prep.shape[1] // 2
        G(lambda e: e.memset(prep[:, 0:half], 0.0))
        V(lambda e: e.memset(prep[:, half:], 0.0))
        fence()

    def fetch_wide(lane, wq, wk, wv, wo):
        for n, w in enumerate((wq, wk, wv)):
            load(lane, weights[:, n * 2048:(n + 1) * 2048].rearrange("p (k n) -> p k n", k=KD), w)
        return load(lane, weights[:, 6144:8192].rearrange("p (t d) -> p t d", t=NTE), wo)

    def prepare_wide(landed=None):
        Wq = weights[:, 0:2048].rearrange("p (k n) -> p k n", k=KD)
        Wk = weights[:, 2048:4096].rearrange("p (k n) -> p k n", k=KD)
        Wv = weights[:, 4096:6144].rearrange("p (k n) -> p k n", k=KD)
        Wo = weights[:, 6144:8192].rearrange("p (t d) -> p t d", t=NTE)
        ring = Ring(list(range(8)))
        for w, scale, dst in ((Wk, 0.125, lambda t, i: kexp[64 * i:64 * i + 64, t, :, S2 * i:S2 * i + S2]),
                                      (Wv, 1.0, lambda t, i: vexp[64 * i:64 * i + 64, :, t * VPAD + P + S2 * i:t * VPAD + P + S2 * i + S2])):
            for t in range(NTE):
                bank, free = ring.take()
                PE.wait(landed, free)
                for k in range(KD):
                    ins = nc.tensor.matmul(psum[:, bank, 0:CTX], w[:, k, t * P:(t + 1) * P], ctxT[:, k, :],
                                           start=(k == 0), stop=(k == KD - 1))
                m = PE.mark(ins)
                for i in range(2):
                    src = psum[64 * i:64 * i + 64, bank, 0:CTX].rearrange("p (b c) -> p b c", b=B)
                    r = A(lambda e: e.mul(dst(t, i), src, scale), m)
                ring.give(r)
        for t in range(0, NTE, 2):
            bank, free = ring.take()
            PE.wait(free)
            for i in range(2):
                for k in range(KD):
                    ins = nc.tensor.transpose(psum[:, bank, (2 * i + k) * P:(2 * i + k + 1) * P],
                                              Wq[:, k, (t + i) * P:(t + i + 1) * P], ident[:, :])
            m = PE.mark(ins)
            turned = V(lambda e: e.tensor_copy(WqT[:, t:t + 2, :].rearrange("p t d -> p (t d)"), psum[:, bank, :]), m)
            ring.give(turned)
        kv_done = A.last()
        for t in range(NTE):
            for k in range(KD):
                bank, free = ring.take()
                PE.wait(turned, kv_done, free)
                m = PE.mark(nc.tensor.matmul(psum[:, bank, 0:B * PAIR], WqT[:, t, k * P:(k + 1) * P],
                                             kexp[:, t, :, :].rearrange("p b c -> p (b c)"), start=True, stop=True))
                ring.give(A(lambda e: e.copy(Kt[:, :, k, t * PAIR:(t + 1) * PAIR],
                                             psum[:, bank, 0:B * PAIR].rearrange("p (b c) -> p b c", b=B)), m))
        for bt in range(B):
            for c in range(0, CH, 2):
                bank, free = ring.take()
                PE.wait(free)
                for i in range(2):
                    pairs = [t for t in range(NTE) if t * PAIR < (c + i + 1) * P and (t + 1) * PAIR > (c + i) * P]
                    for t in pairs:
                        at = (c + i) * P - t * PAIR + P + t * VPAD
                        ins = nc.tensor.matmul(psum[:, bank, i * D:(i + 1) * D], vexp[:, bt, at:at + P], Wo[:, t, :],
                                               start=(t == pairs[0]), stop=(t == pairs[-1]))
                m = PE.mark(ins)
                ring.give(V(lambda e: e.tensor_copy(Vt[:, bt, c:c + 2, :].rearrange("p c d -> p (c d)"), psum[:, bank, :]), m))

    def prepare_narrow(kT_of, vT_of, wo_turned, wo_after, kv_bias, out_bias):
        V(lambda e: e.tensor_scalar(out_bias, out_bias, 1.0 / H, None, ALU.mult), wo_after)
        kc = small[:, 0:KD * CTX].rearrange("p (g c) -> p g c", g=KD)
        vc = small[:, KD * CTX:2 * KD * CTX].rearrange("p (g c) -> p g c", g=KD)
        zeroed = G(lambda e: e.memset(vexp16[:, :, :, :].rearrange("p b g c -> p (b g c)"), 0.0))
        ring = Ring([4, 5, 6, 7])
        for g in range(KD):
            for n, (of, dst) in enumerate(((kT_of, kc), (vT_of, vc))):
                bank, free = ring.take()
                PE.wait(free)
                m = of(psum[:, bank, 0:CTX], g)
                add = kv_bias[:, 2 * g + n:2 * g + n + 1] if kv_bias is not None else 0.0
                r = V(lambda e: e.tensor_scalar(dst[:, g, :], psum[:, bank, 0:CTX], add, None, ALU.add), m)
                ring.give(r)
            for h in range(8):
                V(lambda e: e.tensor_scalar(Kt[:, :, g, h * S2:(h + 1) * S2],
                                            kc[:, g, :].rearrange("p (b c) -> p b c", b=B),
                                            block[:, h:h + 1], None, ALU.mult))
                at = (g * 8 + h) * S2
                V(lambda e: e.tensor_scalar(vexp16[:, :, g, at:at + S2],
                                            vc[:, g, :].rearrange("p (b c) -> p b c", b=B),
                                            block[:, h:h + 1], None, ALU.mult), zeroed)
        expanded = V.last()
        for bt in range(B):
            for c in range(CH):
                bank, free = ring.take()
                PE.wait(expanded, free, wo_after)
                rows = min(P, HK - c * P)
                halves = [g for g in range(KD) if g * 8 * S2 < (c + 1) * P and (g + 1) * 8 * S2 > c * P]
                for g in halves:
                    ins = nc.tensor.matmul(psum[0:rows, bank, 0:D], vexp16[:, bt, g, c * P:c * P + rows],
                                           wo_turned[:, g, :], start=(g == halves[0]), stop=(g == halves[-1]))
                m = PE.mark(ins)
                ring.give(V(lambda e: e.tensor_tensor(Vt[0:rows, bt, c, :], psum[0:rows, bank, 0:D], out_bias[0:rows, :],
                                                      ALU.add), m))


    WIDE = [[(n * BANK, min(BANK, HK - n * BANK), [(0, n * BANK), (1, n * BANK)])] for n in range(3)]
    HALF = 8 * S2
    NARROW = [[(0, BANK, [(0, 0)])],
              [(BANK, HALF - BANK, [(0, BANK)]), (HALF, 2 * BANK - HALF, [(1, 0)])],
              [(2 * BANK, HK - 2 * BANK, [(1, 2 * BANK - HALF)])]]

    def attention(stream, pieces, scale, biased, gate, project=None):
        free_s = [None, None]
        free_o = [None, None]
        free_p = [None, None]
        xn_read = [None, None]
        xt_read = [None, None]
        probT_read = [None, None]
        lhs_read = [None, None]

        def normal(t):
            return normalise(xn[:, t % 2, :], stream, t, xn_read[t % 2])

        def turn_tile(t, n):
            par = t % 2
            so = flat[:, (6 + par) * BANK:(6 + par) * BANK + D]
            tr = turn(xn[:, par, :], so, n, xt_read[par], free_o[par])
            xn_read[par] = tr
            return tr

        def keep_tile(t, tr):
            par = t % 2
            so = flat[:, (6 + par) * BANK:(6 + par) * BANK + D]
            cp = A(lambda e: e.copy(xnTt[:, par, :, :].rearrange("p k c -> p (k c)"), so), tr, lhs_read[par])
            xt_read[par] = cp
            return cp

        def queries(t, cp):
            par = t % 2
            if project is not None:
                cp = project(par, flat[:, (6 + par) * BANK:(6 + par) * BANK + D], cp)
                xt_read[par] = cp
            return cp

        def scores(t, cp):
            par = t % 2
            lhs = xnTt if project is None else qTt
            PE.wait(cp, free_s[par])
            for bank in pieces:
                for at, cols, parts in bank:
                    for k, src in parts:
                        ins = nc.tensor.matmul(flat[:, par * 3 * BANK + at:par * 3 * BANK + at + cols],
                                               lhs[:, par, k, :], Kt[:, t // TB, k, src:src + cols],
                                               start=(k == parts[0][0]), stop=(k == parts[-1][0]))
            lhs_read[par] = PE.mark(ins)
            return lhs_read[par]

        def softmax(t, m):
            par = t % 2
            S_ps = flat[:, par * 3 * BANK:par * 3 * BANK + HK].rearrange("p (h c) -> p h c", h=H)
            Pb = prob[:, par, :].rearrange("p (h c) -> p h c", h=H)
            negmax, total = row[:, par, 0:H], row[:, par, H:2 * H]
            V.wait(free_p[par], m)
            src = S_ps
            if biased:
                V(lambda e: e.tensor_tensor(Pb, S_ps, bias[:, t, :].unsqueeze(1).to_broadcast([P, H, S2]),
                                            ALU.add))
                src = Pb
            V(lambda e: e.tensor_reduce(negmax, src, AX.X, ALU.max, negate=True))
            V(lambda e: e.tensor_tensor(Pb, src, negmax.unsqueeze(2).to_broadcast([P, H, S2]), ALU.add))
            ex = A(lambda e: e.activation(prob[:, par, :], prob[:, par, :], ACT.Exp, scale=scale), V.last())
            return ex

        def share(t, ex):
            par = t % 2
            Pb = prob[:, par, :].rearrange("p (h c) -> p h c", h=H)
            total = row[:, par, H:2 * H]
            V(lambda e: e.tensor_reduce(total, Pb, AX.X, ALU.add), ex)
            V(lambda e: e.reciprocal(total, total))
            return V(lambda e: e.tensor_tensor(Pb, Pb, total.unsqueeze(2).to_broadcast([P, H, S2]), ALU.mult))

        def turn_probabilities(t, ready):
            par = t % 2
            base = par * 3 * BANK
            PE.wait(ready)
            marks = []
            for b0 in range(0, CH, 4):
                for c in range(b0, min(b0 + 4, CH)):
                    rows = min(P, HK - c * P)
                    ins = nc.tensor.transpose(flat[0:rows, base + c * P:base + (c + 1) * P],
                                              prob[:, par, c * P:c * P + rows], ident[:, :])
                marks.append(PE.mark(ins))
            free_p[par] = marks[-1]
            parts = []
            for b0, m in zip(range(0, CH, 4), marks):
                n = min(4, CH - 1 - b0)
                r = A(lambda e: e.copy(probT[:, par, b0:b0 + n, :].rearrange("p c n -> p (c n)"),
                                       flat[:, base + b0 * P:base + (b0 + n) * P]), m, probT_read[par])
                if b0 + n == CH - 1:
                    r = A(lambda e: e.copy(probT[0:LASTROWS, par, CH - 1, :],
                                           flat[0:LASTROWS, base + (CH - 1) * P:base + CH * P]))
                parts.append(r)
            free_s[par] = parts[-1]
            return parts

        def weigh_values(t, parts):
            par = t % 2
            PE.wait(free_o[par], xt_read[par])
            o = flat[:, (6 + par) * BANK + D:(6 + par) * BANK + 2 * D]
            for c in range(CH):
                rows = min(P, HK - c * P)
                PE.wait(parts[c // 4])
                ins = nc.tensor.matmul(o, probT[0:rows, par, c, :], Vt[0:rows, t // TB, c, :],
                                       start=(c == 0), stop=(c == CH - 1))
            probT_read[par] = PE.mark(ins)
            return probT_read[par]

        def residual(t, m):
            o = flat[:, (6 + t % 2) * BANK + D:(6 + t % 2) * BANK + 2 * D]
            free_o[t % 2] = V(lambda e: e.scalar_tensor_tensor(stream[:, t, :], o, gate, stream[:, t, :],
                                                               ALU.mult, ALU.add), m)
            collect(stream, t)

        cp = queries(0, keep_tile(0, turn_tile(0, normal(0))))
        scored = scores(0, cp)
        cp = queries(1, keep_tile(1, turn_tile(1, normal(1))))
        done = None
        for t in range(NT):
            ex = softmax(t, scored)
            n = normal(t + 2) if t + 2 < NT else None
            ready = share(t, ex)
            if done is not None:
                residual(t - 1, done)
            if t + 1 < NT:
                scored = scores(t + 1, cp)
            if t + 2 < NT:
                cp = keep_tile(t + 2, turn_tile(t + 2, n))
            parts = turn_probabilities(t, ready)
            if t + 2 < NT:
                cp = queries(t + 2, cp)
            done = weigh_values(t, parts)
        residual(NT - 1, done)
        fence(spare=ahead)
        collected.add(id(stream))


    def slot(s):
        w = expert_w[:, s * 3072:(s + 1) * 3072]
        return (w[:, 0:1024].rearrange("p (k f) -> p k f", k=KD), w[:, 1024:2048].rearrange("p (k f) -> p k f", k=KD),
                w[:, 2048:3072].rearrange("p (f d) -> p f d", f=FC))

    bias1 = sb("bias1", [P, 2, FC])
    hidden = prep[:, 0:4 * GRP].rearrange("p (n c) -> p n c", n=4)
    gated_tmp = prep[:, 4 * GRP:6 * GRP].rearrange("p (n c) -> p n c", n=2)

    def fresh_state():
        return {"ring": Ring([0, 1, 2, 3]), "hid": [None] * 4, "y": [None, None], "n": 0, "tmp": [None, None]}

    def experts(acc, slots, func, gated, xT, gate_of, state=None, last=None, feed=None, between=None):
        state = state or fresh_state()
        hring = state["ring"]

        def first(s, landed, g, f):
            w1, w3, _ = slot(s)
            n = state["n"]
            state["n"] += 1
            outs = []
            for w in ((w1, w3) if gated else (w1,)):
                bank, free = hring.take()
                i = hring.n
                PE.wait(free, landed)
                for k in range(KD):
                    ins = nc.tensor.matmul(psum[:, bank, :], w[:, k, f * P:(f + 1) * P],
                                           xT(s)[:, k, g * GRP:(g + 1) * GRP], start=(k == 0), stop=(k == KD - 1))
                outs.append((bank, i, PE.mark(ins)))
            h = hidden[:, n % 4, :]
            if gated:
                (b0, i0, m0), (b1, i1, m1) = outs
                tm = gated_tmp[:, n % 2, :]
                r = A(lambda e: e.activation(tm, psum[:, b0, :], func), m0, state["tmp"][n % 2])
                hring.free[i0] = r
                r = V(lambda e: e.tensor_tensor(h, psum[:, b1, :], tm, ALU.mult), m1, r, state["hid"][n % 4])
                hring.free[i1] = r
                state["tmp"][n % 2] = r
            else:
                b0, i0, m0 = outs[0]
                r = A(lambda e: e.activation(h, psum[:, b0, :], func, bias=bias1[:, s, f:f + 1]),
                      m0, state["hid"][n % 4], landed)
                hring.free[i0] = r
            return n, r

        def second(s, g, f, n, ready):
            _, _, w2 = slot(s)
            y = flat[:, (4 + 2 * (g % 2)) * BANK:(6 + 2 * (g % 2)) * BANK]
            PE.wait(ready, state["y"][g % 2] if f == 0 else None)
            for t in range(TG):
                ins = nc.tensor.matmul(y[:, t * D:(t + 1) * D], hidden[:, n % 4, t * P:(t + 1) * P], w2[:, f, :],
                                       start=(f == 0 and t % 2 == 0), stop=(f == FC - 1), skip_group_check=True)
            m = PE.mark(ins)
            state["hid"][n % 4] = m
            if f == FC - 1:
                for t in range(TG):
                    tile = g * TG + t
                    state["y"][g % 2] = V(lambda e: e.scalar_tensor_tensor(
                        acc[:, tile, :], y[:, t * D:(t + 1) * D], gate_of(s, tile), acc[:, tile, :],
                        ALU.mult, ALU.add), m)
                    if s == last:
                        collect(acc, tile)

        behind = None
        for s, landed in slots:
            for g in range(NG):
                if feed and s == slots[0][0] and g == 0:
                    feed(0, hring)
                for f in range(FC):
                    n, ready = first(s, landed, g, f)
                    if feed and s == slots[0][0] and g + 1 < NG and f == 0:
                        feed(g + 1, hring)
                    if between:
                        between()
                    if behind is not None:
                        second(*behind)
                    behind = (s, g, f, n, ready)
        second(*behind)

    def fetch_expert(lane, s, w1, w3, w2, b1, *after):
        to1, to3, to2 = slot(s)
        load(lane, to1, w1.rearrange("(k p) f -> p k f", p=P), *after)
        if w3 is not None:
            load(lane, to3, w3.rearrange("(k p) f -> p k f", p=P))
        if b1 is not None:
            load(lane, bias1[:, s, :], b1.rearrange("(f p) -> p f", p=P), columns=True)
        return load(lane, to2, w2.rearrange("(f p) d -> p f d", p=P))

    def expert_pairs(acc, fetch, func, gated, xT, gate_of):
        with nc.Fori(0, E // 2) as i:
            state = fresh_state()
            got1 = fetch(dma_b, 1, 2 * i + 1)
            experts(acc, [(0, None)], func, gated, xT, lambda s, tile: gate_of(2 * i, tile), state)
            fetch(dma_a, 0, (2 * i + 2) % E, PE.last(), A.last())
            experts(acc, [(1, got1)], func, gated, xT, lambda s, tile: gate_of(2 * i + 1, tile), state, last=1)
            fence(spare=ahead)
        collected.add(id(acc))


    def feed_input(src, dst, per_tile=None, gain=None):
        with nc.Fori(0, B) as bt:
            xn_read = [None, None]
            read = [None, None]
            for t in range(TB):
                par = t % 2
                tile = bt * TB + t
                bank = flat[:, par * BANK:(par + 1) * BANK]
                n = normalise(xn[:, par, :], src, tile, xn_read[par])
                tr = turn(xn[:, par, :], bank[:, 0:D], n, read[par])
                xn_read[par] = tr
                A.wait(tr)
                if gain is None:
                    read[par] = A(lambda e: e.copy(dst[:, :, bass.ds(tile * P, P)],
                                                   bank[:, 0:D].rearrange("p (k c) -> p k c", k=KD)))
                else:
                    for k in range(KD):
                        read[par] = A(lambda e: e.mul(dst[:, k, bass.ds(tile * P, P)], bank[:, k * P:(k + 1) * P],
                                                      gain[:, k:k + 1]))
                if per_tile:
                    read[par] = per_tile(tile, par, bank, read[par])
            fence(spare=ahead)

    logits = sb("logits", [P, NT, E])
    wide = small[:, 0:4 * NT * E].rearrange("p (n t e) -> p n t e", n=4, e=E)
    w_gate = small[:, 4 * NT * E:4 * NT * E + KD * E].rearrange("p (k e) -> p k e", k=KD)
    b_gate = small[0:1, 4 * NT * E + KD * E:4 * NT * E + KD * E + E]

    def router(with_bias, gain=None):
        def work(tile, par, bank, after):
            A.wait(after)
            if gain is None:
                A(lambda e: e.copy(xnTt[:, par, :, :].rearrange("p k c -> p (k c)"), bank[:, 0:D]))
            else:
                for k in range(KD):
                    A(lambda e: e.mul(xnTt[:, par, k, :], bank[:, k * P:(k + 1) * P], gain[:, k:k + 1]))
            PE.wait(A.last())
            o = bank[:, D:D + E]
            if with_bias:
                nc.tensor.matmul(o, ones[0:1, :], b_gate, start=True, stop=False)
            for k in range(KD):
                ins = nc.tensor.matmul(o, xnTt[:, par, k, :], w_gate[:, k, :], start=(k == 0 and not with_bias),
                                       stop=(k == KD - 1))
            return A(lambda e: e.copy(logits[:, tile, :], o), PE.mark(ins))
        return work

    def over(v):
        return v.unsqueeze(2).to_broadcast([P, NT, E])

    def first_best(best, scores_, top, order):
        V(lambda e: e.tensor_reduce(top, scores_, AX.X, ALU.max))
        V(lambda e: e.tensor_tensor(best, scores_, over(top), ALU.is_equal))
        V(lambda e: e.tensor_tensor(best, best, order.unsqueeze(1).to_broadcast([P, NT, E]), ALU.mult))
        V(lambda e: e.tensor_reduce(rank[:, :], best, AX.X, ALU.max))
        V(lambda e: e.tensor_tensor(best, best, over(rank[:, :]), ALU.is_equal))

    rank = sb("rank", [P, NT])
    top_a = sb("top_a", [P, NT])
    top_b = sb("top_b", [P, NT])
    order = sb("order", [P, E])

    def descending():
        for e_ in range(E):
            G(lambda e: e.memset(order[:, e_:e_ + 1], float(E - e_)))


    SROW = prep[:, 4096:]

    def routed(K, turns, per_turn, x_rows, y_rows, w1, w3, w2, chosen, gain, gate_of, rows_of, meanwhile):
        total = turns * per_turn
        assert total >= K * NT * P // CHUNK + E - 1 and per_turn % 3 == 0
        flat3 = lambda n, at: SROW[:, at:at + n]
        te = lambda at: SROW[:, at:at + NT * E].rearrange("p (t e) -> p t e", e=E)
        both, place, before, tile_count = te(0), te(128), te(256), te(384)
        per_expert, chunks, first_row, last_chunk = (flat3(E, 512 + E * n) for n in range(4))
        ramp, partition = flat3(8, 544), flat3(1, 552)
        steps = SROW[:, 560:560 + E * 8].rearrange("p (e c) -> p e c", c=8)
        numbers, expert_of = flat3(total, 640), flat3(total, 672)
        passed = SROW[:, 704:704 + total * (E - 1)].rearrange("p (c e) -> p c e", e=E - 1)
        where = flat3(K * NT, 900).rearrange("p (k t) -> p k t", k=K)
        where_i = flat3(K * NT, 940).bitcast(I32).rearrange("p (k t) -> p k t", k=K)
        w_row = flat3(total, 980).bitcast(I32)
        w_row_now = flat3(3, 1010).bitcast(I32)
        earlier = qTt[:, 0, 0, :]
        G(lambda e: e.affine_select(out=earlier, in_=ones[:, :], compare_op=ALU.is_ge, fill=0.0, base=-1,
                                    pattern=[[1, P]], channel_multiplier=-1))
        if K == 1:
            both = chosen[0]
        else:
            V(lambda e: e.tensor_tensor(both, chosen[0], chosen[1], ALU.add))
        both_flat = both.rearrange("p t e -> p (t e)")
        PE.wait(V.last(), G.last())
        nc.tensor.matmul(psum[:, 0, 0:NT * E], earlier, both_flat, start=True, stop=True)
        nc.tensor.matmul(psum[:, 0, NT * E:2 * NT * E], ones[:, :], both_flat, start=True, stop=True)
        m = PE.mark(nc.tensor.matmul(psum[:, 0, 2 * NT * E:2 * NT * E + 1], earlier, ones[:, 0:1], start=True, stop=True))
        counts = psum[:, 0, :].rearrange("p (n t e) -> p n t e", n=4, e=E)
        V(lambda e: e.tensor_copy(place, counts[:, 0]), m)
        V(lambda e: e.tensor_copy(tile_count, counts[:, 1]))
        V(lambda e: e.tensor_copy(partition, psum[:, 0, 2 * NT * E:2 * NT * E + 1]))
        PE.wait(V.last())
        V(lambda e: e.memset(before[:, 0, :], 0.0))
        for t in range(1, NT):
            V(lambda e: e.tensor_tensor(before[:, t, :], before[:, t - 1, :], tile_count[:, t - 1, :], ALU.add))
        V(lambda e: e.tensor_tensor(per_expert, before[:, NT - 1, :], tile_count[:, NT - 1, :], ALU.add))
        V(lambda e: e.tensor_scalar(ramp, order[:, :], -float(CHUNK), float(E * CHUNK), ALU.mult, ALU.add))
        V(lambda e: e.tensor_tensor(steps, per_expert.unsqueeze(2).to_broadcast([P, E, 8]),
                                    ramp.unsqueeze(1).to_broadcast([P, E, 8]), ALU.is_gt))
        V(lambda e: e.tensor_reduce(chunks, steps, AX.X, ALU.add))
        V(lambda e: e.tensor_copy(last_chunk[:, 0:1], chunks[:, 0:1]))
        for e_ in range(1, E):
            V(lambda e: e.tensor_tensor(last_chunk[:, e_:e_ + 1], last_chunk[:, e_ - 1:e_], chunks[:, e_:e_ + 1], ALU.add))
        V(lambda e: e.tensor_tensor(first_row, last_chunk, chunks, ALU.subtract))
        V(lambda e: e.tensor_scalar(first_row, first_row, float(CHUNK), None, ALU.mult))
        V(lambda e: e.tensor_tensor(place, place, before, ALU.add))
        V(lambda e: e.tensor_tensor(place, place, first_row.unsqueeze(1).to_broadcast([P, NT, E]), ALU.add))
        for k in range(K):
            V(lambda e: e.tensor_tensor(before, place, chosen[k], ALU.mult))
            V(lambda e: e.tensor_reduce(where[:, k, :], before, AX.X, ALU.add))
        V(lambda e: e.tensor_copy(where_i, where))
        for c in range(0, total, 8):
            n = min(8, total - c)
            V(lambda e: e.tensor_scalar(numbers[:, c:c + n], order[:, 0:n], -1.0, float(E + c), ALU.mult, ALU.add))
        V(lambda e: e.tensor_tensor(passed, numbers.unsqueeze(2).to_broadcast([P, total, E - 1]),
                                    last_chunk[:, 0:E - 1].unsqueeze(1).to_broadcast([P, total, E - 1]), ALU.is_ge))
        V(lambda e: e.tensor_reduce(expert_of, passed, AX.X, ALU.add))
        V(lambda e: e.tensor_scalar(expert_of, expert_of, float(P), None, ALU.mult))
        V(lambda e: e.tensor_tensor(expert_of, expert_of, partition.to_broadcast([P, total]), ALU.add))
        V(lambda e: e.tensor_copy(w_row, expert_of))

        by_row = (w1.rearrange("e (p k) f -> (e p) (k f)", k=KD), w3.rearrange("e (p k) f -> (e p) (k f)", k=KD),
                  w2.rearrange("e (p j) d -> (e p) (j d)", j=FC))
        slots = (expert_w[:, 0:3072], weights[:, 0:3072], expert_w[:, 3072:6144])
        flat_inner = inner[:, :, :].rearrange("p t d -> p (t d)")
        rows_in = flat_inner[:, 0:3 * 512].rearrange("p (s n d) -> p s n d", s=3, n=2)
        xT = flat_inner[:, 1536:1536 + 1024].rearrange("p (s k c) -> p s k c", s=2, k=KD)
        y_out = flat_inner[:, 2560:2560 + 1024].rearrange("p (s n d) -> p s n d", s=2, n=2)
        x_chunk = x_rows.rearrange("(c n p) d -> c p n d", n=2, p=P)
        y_chunk = y_rows.rearrange("(c n p) d -> c p n d", n=2, p=P)

        def fetch_weights(s, chunk, *after):
            G(lambda e: e.tensor_copy(w_row_now[:, s:s + 1], w_row[:, bass.ds(chunk, 1)]), *after)
            G.wait(G.last())
            for n in range(3):
                got_ = gather_lanes[s].mark(nc.gpsimd.indirect_dma_start(
                    slots[s][:, n * 1024:(n + 1) * 1024], None, by_row[n],
                    bass.IndirectOffsetOnAxis(w_row_now[:, s:s + 1], 0)))
            return got_

        def fetch_rows(s, chunk, *after):
            return load((dma_a, dma_b, dma_c)[s], rows_in[:, s, :, :], x_chunk[chunk], *after)

        G.wait(V.last())
        for t in range(NT):
            G.wait(rows_of(t))
            for k in range(K):
                sent = gather_lanes[3].mark(nc.gpsimd.indirect_dma_start(
                    x_rows, bass.IndirectOffsetOnAxis(where_i[:, k, t:t + 1], 0), inner[:, t, :], None))
        for s in range(2):
            fetch_weights(s, s)
        meanwhile()
        for s in range(2):
            fetch_rows(s, s, sent)
        fence()
        with nc.Fori(0, turns) as i:
            ring = Ring([0, 1, 2, 3])
            hid_read = [None] * 4
            state = {"n": 0}
            turned, landed_w, landed_x = {}, {0: None, 1: None}, {0: None, 1: None}
            rows_read, slot_read, xT_read, xT_bank = {}, {}, {}, {}
            y_free, y_stored = {}, {}

            def turn_rows(c):
                s, par = c % 3, c % 2
                bank = psum[:, 6 + par, :]
                PE.wait(landed_x[c], xT_bank.get(c - 2))
                for k in range(KD):
                    for n in range(2):
                        ins = nc.tensor.transpose(bank[:, (2 * k + n) * P:(2 * k + n + 1) * P],
                                                  rows_in[:, s, n, k::KD], ident[:, :])
                rows_read[c] = PE.mark(ins)
                for k in range(KD):
                    r_ = A(lambda e: e.mul(xT[:, par, k, :], bank[:, 2 * k * P:2 * (k + 1) * P],
                                           gain[:, k:k + 1] if gain is not None else 1.0), rows_read[c], xT_read.get(c - 2))
                turned[c] = xT_bank[c] = r_

            def first(c, j):
                s, par = c % 3, c % 2
                bank, free = ring.take()
                PE.wait(free, landed_w[c], turned[c])
                for n in range(2):
                    w = slots[s][:, n * 1024:(n + 1) * 1024].rearrange("p (k f) -> p k f", k=KD)
                    for k in range(KD):
                        ins = nc.tensor.matmul(psum[:, bank, n * CHUNK:(n + 1) * CHUNK], w[:, k, j::FC], xT[:, par, k, :],
                                               start=(k == 0), stop=(k == KD - 1))
                m = xT_read[c] = PE.mark(ins)
                n = state["n"]
                state["n"] += 1
                h, tm = hidden[:, n % 4, 0:CHUNK], gated_tmp[:, n % 2, 0:CHUNK]
                r_ = A(lambda e: e.activation(tm, psum[:, bank, 0:CHUNK], ACT.Silu), m, hid_read[(n - 2) % 4])
                r_ = V(lambda e: e.tensor_tensor(h, psum[:, bank, CHUNK:2 * CHUNK], tm, ALU.mult), r_, hid_read[n % 4])
                ring.give(r_)
                return c, j, n, r_

            def second(c, j, n, ready):
                s, par = c % 3, c % 2
                w = slots[s][:, 2048:3072].rearrange("p (j d) -> p j d", j=FC)
                PE.wait(ready, y_free.get(c - 2))
                for t in range(2):
                    ins = nc.tensor.matmul(psum[:, 4 + par, t * D:(t + 1) * D], hidden[:, n % 4, t * P:(t + 1) * P],
                                           w[:, j, :], start=(j == 0 and t == 0), stop=(j == FC - 1), skip_group_check=True)
                m = hid_read[n % 4] = PE.mark(ins)
                if j == FC - 1:
                    slot_read[c] = m
                    y_free[c] = V(lambda e: e.tensor_copy(y_out[:, par, :, :].rearrange("p n d -> p (n d)"),
                                                          psum[:, 4 + par, :]), m, y_stored.get(c - 2))
                    y_stored[c] = load((dma_d, dma_e)[par], y_chunk[i * per_turn + c], y_out[:, par, :, :], y_free[c])

            turn_rows(0)
            behind = None
            for c in range(per_turn):
                for j in range(FC):
                    now = first(c, j)
                    if behind is not None:
                        second(*behind)
                    behind = now
                    if j == 0:
                        nxt = (i * per_turn + c + 2) % total
                        w_, x_ = fetch_weights((c + 2) % 3, nxt, slot_read.get(c - 1)), \
                            fetch_rows((c + 2) % 3, nxt, rows_read.get(c - 1))
                        if c + 2 < per_turn:
                            landed_w[c + 2], landed_x[c + 2] = w_, x_
                    if j == 2 and c + 1 < per_turn:
                        turn_rows(c + 1)
            second(*behind)
            fence()
        back = (inner, shared[:, 0:NT * D].rearrange("p (t d) -> p t d", t=NT))
        arrived = {}
        for q in range(0, NT, 4):
            for k in range(K):
                lane = gather_lanes[K * (q // 4) + k]
                for t in range(q, q + 4):
                    arrived[k, q] = lane.mark(nc.gpsimd.indirect_dma_start(
                        back[k][:, t, :], None, y_rows, bass.IndirectOffsetOnAxis(where_i[:, k, t:t + 1], 0)))
        for t in range(NT):
            for k in range(K):
                V(lambda e: e.scalar_tensor_tensor(x[:, t, :], back[k][:, t, :], gate_of(k, t), x[:, t, :],
                                                   ALU.mult, ALU.add), arrived[k, t // 4 * 4])
            collect(x, t)
        collected.add(id(x))
        fence()

    def clear_rows(dst):
        zeros = qTt[:, :, :, :].rearrange("p n k c -> p (n k c)")
        V(lambda e: e.memset(zeros, 0.0))
        view = dst.rearrange("(n p) d -> p n d", p=P)
        n = view.shape[1]
        for at in range(0, n, 2):
            load(ahead, view[:, at:at + 2, :], zeros.rearrange("p (n d) -> p n d", n=2), V.last())

    def finish():
        o = None
        for bt in range(B):
            o = load(dma_a, out[bt].rearrange("(t p) d -> p t d", p=P), x[:, bt * TB:(bt + 1) * TB, :])
        SP.wait(o)

    def head64(ap):
        return ap.rearrange("(k p) n h -> p k (n h)", p=P)

    def begins(stage):
        return STOP is None or (STOP[1] < stage <= STOP[0])

    if begins(0):
        load(dma_c, bias[:, :, :], a["mask_Bx1xSxS2_ff0"][:, 0].rearrange("b (t p) s -> p (b t) s", p=P))
        fetch_wide(dma_d, head64(a["L0_xattn_wq"]), head64(a["L0_xattn_wk"]), head64(a["L0_xattn_wv"]),
                   a["L0_xattn_wo"].rearrange("n h d -> (n h) d").rearrange("(t p) d -> p t d", p=P))
        clear_expanded()
        prepare_wide()
        statistics(x, 1e-5)
        fence()
        attention(x, WIDE, 1.0, True, tanh_g[:, 0:1])

    def quantised_ffn():
        NL, R = 6, 32
        WT = expert_w[:, 0:NL * 2 * D].rearrange("p (j k o) -> p j k o", j=NL, k=KD)
        q = expert_w[:, NL * 2 * D:2 * NL * 2 * D].bitcast(I32).rearrange("p (j h d) -> p j h d", j=NL, h=2)
        z = prep[:, 0:NT * D].rearrange("p (t d) -> p t d", t=NT)
        rest = prep[:, NT * D:]
        sc = rest[:, 0:192].rearrange("p (j h g) -> p j h g", j=NL, h=2)
        lb = rest[:, 192:576].rearrange("p (j h r) -> p j h r", j=NL, h=2)
        la = rest[0:R, 576:2112].rearrange("p (j d) -> p j d", j=NL)
        brow = rest[:, 2112:3648].rearrange("p (j o) -> p j o", j=NL)
        gamma = rest[:, 3648:3654].rearrange("p (b k) -> p b k", b=3)
        beta = rest[:, 3654:3660].rearrange("p (b k) -> p b k", b=3)
        wf = rest[:, 3660:3660 + 2 * D].rearrange("p (n d) -> p n d", n=2)
        lbT = rest[0:R, 3660 + 2 * D:3660 + 2 * D + 2 * P].rearrange("p (n c) -> p n c", n=2)
        l_q = load(dma_a, q, a["L0_ffn_qweights"].rearrange("j (h p) d -> p j h d", p=P))
        load(dma_b, sc, a["L0_ffn_scales"].rearrange("j (h p) g -> p j h g", p=P))
        load(dma_b, lb, a["L0_ffn_lora_b"].rearrange("j (h p) r -> p j h r", p=P))
        load(dma_b, la, a["L0_ffn_lora_a"].rearrange("j r d -> r j d"))
        load(dma_b, brow, a["L0_ffn_biases"].rearrange("(o j) d -> o j d", o=1).to_broadcast([P, NL, D]))
        for blk in range(3):
            load(dma_b, gamma[:, blk, :], a["L0_ffn_ln_gamma"][blk].rearrange("(k p) -> p k", p=P), columns=True)
            l_s = load(dma_b, beta[:, blk, :], a["L0_ffn_ln_beta"][blk].rearrange("(k p) -> p k", p=P), columns=True)
        statistics(x, 1e-5)
        for t in range(NT):
            normalise(inner[:, t, :], x, t)
        ring = Ring([0, 1, 2, 3, 4, 5, 6, 7])
        V.wait(l_q, l_s)
        PE.wait(l_s)
        lb_read, wf_read = [None, None], [None, None]
        for n in range(2 * NL):
            j, h, i = n // 2, n % 2, n % 2
            bank, free = ring.take()
            PE.wait(free)
            m = PE.mark(nc.tensor.transpose(psum[0:R, bank, 0:P], lb[:, j, h, :], ident[:, :]))
            cp = A(lambda e: e.copy(lbT[:, i, :], psum[0:R, bank, 0:P]), m, lb_read[i])
            PE.wait(cp)
            lora = PE.mark(nc.tensor.matmul(psum[:, bank, D:2 * D], lbT[:, i, :], la[:, j, :], start=True, stop=True))
            lb_read[i] = lora
            V(lambda e: e.tensor_scalar(wf[:, i, :], q[:, j, h, :], 1.0 / 7.5, -1.0, ALU.mult, ALU.add), wf_read[i])
            w3d = wf[:, i, :].rearrange("p (g c) -> p g c", g=16)
            V(lambda e: e.tensor_tensor(w3d, w3d, sc[:, j, h, :].unsqueeze(2).to_broadcast([P, 16, 16]), ALU.mult))
            w = V(lambda e: e.tensor_tensor(wf[:, i, :], psum[:, bank, D:2 * D], wf[:, i, :], ALU.add), lora)
            tr = turn(wf[:, i, :], psum[:, bank, 0:D], w)
            wf_read[i] = tr
            ring.give(A(lambda e: e.copy(WT[:, j, :, h * P:(h + 1) * P],
                                         psum[:, bank, 0:D].rearrange("p (k c) -> p k c", k=KD)), tr))
        fence()
        with nc.Fori(0, 3) as blk:
            turned_tile = [xnTt[:, 0], xnTt[:, 1], qTt[:, 0], qTt[:, 1]]
            for layer in range(2):
                ring = Ring([0, 1, 2, 3, 4, 5, 6, 7])
                lhs_read = [None] * 4
                waiting = []

                def product(t, bank, cp):
                    PE.wait(cp)
                    y = psum[:, bank, D:2 * D]
                    for k in range(KD):
                        ins = nc.tensor.matmul(y, turned_tile[t % 4][:, k, :], WT[:, 2 * blk + layer, k, :],
                                               start=(k == 0), stop=(k == KD - 1))
                    m = PE.mark(ins)
                    lhs_read[t % 4] = m
                    if layer == 0:
                        ring.free[bank] = V(lambda e: e.tensor_tensor(z[:, t, :], y, brow[:, 2 * blk, :], ALU.add), m)
                        V(lambda e: e.bn_stats(bn6[:, t, :], z[:, t, :]))
                        G(lambda e: e.tensor_tensor(inner[:, t, :], inner[:, t, :], brow[:, 2 * blk + 1, :], ALU.add), m)
                        V(lambda e: e.bn_aggr(meanvar[:, t, :], bn6[:, t, :]))
                    else:
                        ring.free[bank] = V(lambda e: e.tensor_tensor(inner[:, t, :], y, inner[:, t, :], ALU.add), m, G.last())

                for t in range(NT):
                    bank, free = ring.take()
                    if layer == 0:
                        tr = turn(inner[:, t, :], psum[:, bank, 0:D], free)
                        cp = A(lambda e: e.copy(turned_tile[t % 4].rearrange("p k c -> p (k c)"), psum[:, bank, 0:D]),
                               tr, lhs_read[t % 4])
                    else:
                        n = V(lambda e: e.tensor_scalar(z[:, t, :], z[:, t, :], meanvar[:, t, 0:1], rstd[:, t:t + 1],
                                                        ALU.subtract, ALU.mult))
                        tr = turn(z[:, t, :], psum[:, bank, 0:D], n, free)
                        for k in range(KD):
                            cp = A(lambda e: e.activation(turned_tile[t % 4][:, k, :], psum[:, bank, k * P:(k + 1) * P],
                                                          ACT.Gelu, bias=beta[:, bass.ds(blk, 1), k],
                                                          scale=gamma[:, bass.ds(blk, 1), k]), tr, lhs_read[t % 4])
                    waiting.append((t, bank, cp))
                    if len(waiting) > 2:
                        product(*waiting.pop(0))
                for w in waiting:
                    product(*w)
                if layer == 0:
                    reciprocal_root(meanvar[:, :, 1], 1e-5, None)
            fence()
        for t in range(NT):
            V(lambda e: e.scalar_tensor_tensor(x[:, t, :], inner[:, t, :], tanh_g[:, 4:5], x[:, t, :],
                                               ALU.mult, ALU.add))
            collect(x, t)
        collected.add(id(x))
        fence()

    wq4, wk4, wv4 = (a["L1_xattn_" + n].rearrange("l (k p) n h -> l p k (n h)", p=P) for n in ("Wq", "Wk", "Wv"))
    wo4 = a["L1_xattn_Wo"].rearrange("l n h d -> l (n h) d").rearrange("l (t p) d -> l p t d", p=P)
    fetch_wide(ahead, wq4[0], wk4[0], wv4[0], wo4[0])
    if begins(1):
        quantised_ffn()
    fence()

    def decoder():
        K = 32
        mask = small[:, 0:B * S2].rearrange("p (b s) -> p b s", b=B)
        wth, bth, wto, bto = (small[:, 160 + 32 * n:192 + 32 * n] for n in range(4))
        b2 = small[:, 320:320 + D]
        load(dma_a, mask, a["mask_Bx1x1xS2_ff0"].rearrange("b x y s -> (x y) b s").to_broadcast([P, B, S2]))
        flat_bias = bias[:, :, :].rearrange("p t s -> p (t s)")
        flat_side = fside[:, :, :].rearrange("p t s -> p (t s)")
        hinge = Kt[:, 0, :, :]

        class Distance:

            def __init__(self, layer):
                def vector_of(name, n):
                    return a[name][layer].rearrange("(o n) -> o n", o=1).to_broadcast([P, n])

                load(dma_e, wth, a["L1_xattn_Wth"][layer].to_broadcast([P, K]))
                load(dma_e, bth, vector_of("L1_xattn_bth", K))
                load(dma_e, wto, a["L1_xattn_Wto"][layer].rearrange("k o -> o k").to_broadcast([P, K]), columns=True)
                self.got = load(dma_e, bto[:, 0:1], vector_of("L1_xattn_bto", 1), columns=True)
                self.j, self.used = -1, [None, None]

            def step(self):
                j = self.j
                self.j += 1
                if j >= K:
                    return
                if j < 0:
                    for bt in range(B):
                        V(lambda e: e.tensor_scalar(bias[:, bt * TB:(bt + 1) * TB, :],
                                                    mask[:, bt, :].unsqueeze(1).to_broadcast([P, TB, S2]),
                                                    bto[:, 0:1], None, ALU.add), self.got)
                    return
                r = hinge[:, j % 2, :]
                m = A(lambda e: e.activation(r, flat_side, ACT.Relu, scale=wth[:, j:j + 1], bias=bth[:, j:j + 1]),
                      self.got, self.used[j % 2])
                self.used[j % 2] = V(lambda e: e.scalar_tensor_tensor(flat_bias, r, wto[:, j:j + 1], flat_bias,
                                                                      ALU.mult, ALU.add), m)

        statistics(x, 1e-5)
        for t in range(NT):
            normalise(inner[:, t, :], x, t)
            collect(inner, t)
        collected.add(id(inner))
        clear_expanded()
        first_distance = Distance(0)
        for _ in range(K + 1):
            first_distance.step()
        fence()
        with nc.Fori(0, 4) as layer:
            nxt = (layer + 1) % 4
            load(dma_a, b2, a["L1_xattn_bf2"][layer].rearrange("(o n) -> o n", o=1).to_broadcast([P, D]))
            prepare_wide()
            statistics(inner, None, 1e-6)
            fence()
            for h in range(2):
                fetch_expert(ahead, h, a["L1_xattn_Wf1"][layer][:, h * F:(h + 1) * F], None,
                             a["L1_xattn_Wf2"][layer][h * F:(h + 1) * F, :], a["L1_xattn_bf1"][layer][h * F:(h + 1) * F])
            attention(inner, WIDE, 1.0, True, 1.0)
            statistics(inner, None, 1e-6)
            fence()
            fetch_wide(ahead, wq4[nxt], wk4[nxt], wv4[nxt], wo4[nxt])
            distance = Distance(nxt)
            xn_read = [None, None]

            def feed(g, ring):
                for t in range(g * TG, (g + 1) * TG):
                    par = t % 2
                    bank, fr = ring.take()
                    n = normalise(xn[:, par, :], inner, t, xn_read[par])
                    xn_read[par] = turn(xn[:, par, :], psum[:, bank, 0:D], n, fr)
                    ring.give(A(lambda e: e.copy(xnT[:, :, t * P:(t + 1) * P],
                                                 psum[:, bank, 0:D].rearrange("p (k c) -> p k c", k=KD)), xn_read[par]))
                    V(lambda e: e.tensor_tensor(inner[:, t, :], inner[:, t, :], b2, ALU.add))
                PE.wait(A.last())

            experts(inner, [(0, None), (1, None)], ACT.Relu, False, lambda s: xnT, lambda s, tile: 1.0,
                    last=1, feed=feed, between=distance.step)
            while distance.j < K:
                distance.step()
            fence()
        statistics(inner, None, 1e-6)
        for t in range(NT):
            par = t % 2
            normalise(xn[:, par, :], inner, t)
            V(lambda e: e.scalar_tensor_tensor(x[:, t, :], xn[:, par, :], tanh_g[:, 1:2], x[:, t, :], ALU.mult, ALU.add))
            collect(x, t)
        collected.add(id(x))
        fence()

    if begins(2):
        decoder()

    def one_gate_experts():
        gw = small[0:E, 600:600 + D]
        b2 = small[0:E, 600:600 + D]
        def fetch(lane, s, e, *after):
            return fetch_expert(lane, s, a["L1_ffn_w1"][e], None, a["L1_ffn_w2"][e], a["L1_ffn_b1"][e], *after)
        fetch(ahead, 0, 0)
        got = load(dma_b, gw, a["L1_ffn_gate_w"])
        load(dma_b, rms_w[:, :], bcast(a["L1_ffn_rms_w"], E))
        got = load(dma_b, b_gate, a["L1_ffn_gate_b"].rearrange("(o e) -> o e", o=1))
        for k in range(KD):
            PE.wait(got)
            m = PE.mark(nc.tensor.transpose(psum[:, k, 0:E], gw[:, k * P:(k + 1) * P], ident[0:E, 0:E]))
            A(lambda e: e.copy(w_gate[:, k, :], psum[:, k, 0:E]), m)
        statistics(x, 1e-5)
        fence()
        feed_input(x, xnT, router(True))
        got = load(dma_b, b2, a["L1_ffn_b2"])
        sq = wide[:, 0]
        V(lambda e: e.tensor_tensor(sq, logits[:, :, :], logits[:, :, :], ALU.mult))
        V(lambda e: e.tensor_reduce(top_a[:, :], sq, AX.X, ALU.add))
        V(lambda e: e.tensor_scalar(top_a[:, :], top_a[:, :], 1.0 / E, float(np.finfo(np.float32).eps), ALU.mult, ALU.add))
        A(lambda e: e.activation(top_a[:, :], top_a[:, :], ACT.Sqrt), V.last())
        V(lambda e: e.reciprocal(top_a[:, :], top_a[:, :]), A.last())
        V(lambda e: e.tensor_tensor(sq, logits[:, :, :], over(top_a[:, :]), ALU.mult))
        V(lambda e: e.tensor_tensor(sq, sq, rms_w[:, :].unsqueeze(1).to_broadcast([P, NT, E]), ALU.mult))
        V(lambda e: e.tensor_reduce(top_b[:, :], sq, AX.X, ALU.max))
        V(lambda e: e.tensor_tensor(sq, sq, over(top_b[:, :]), ALU.subtract))
        A(lambda e: e.activation(sq, sq, ACT.Exp, scale=2.0), V.last())
        V(lambda e: e.tensor_reduce(top_a[:, :], sq, AX.X, ALU.add), A.last())
        V(lambda e: e.reciprocal(top_a[:, :], top_a[:, :]))
        V(lambda e: e.tensor_scalar(top_b[:, :], top_a[:, :], 1e-6, None, ALU.add))
        V(lambda e: e.reciprocal(top_b[:, :], top_b[:, :]))
        V(lambda e: e.tensor_tensor(top_a[:, :], top_a[:, :], top_b[:, :], ALU.mult))
        V(lambda e: e.tensor_scalar(gates[:, :, 0], top_a[:, :], tanh_g[:, 5:6], None, ALU.mult))
        PE.wait(got)
        m = PE.mark(nc.tensor.matmul(psum[:, 0, 0:D], ones[0:E, :], b2, start=True, stop=True))
        for t in range(NT):
            V(lambda e: e.scalar_tensor_tensor(x[:, t, :], psum[:, 0, 0:D], gates[:, t, 0:1], x[:, t, :],
                                               ALU.mult, ALU.add), m)
        fence()
        expert_pairs(x, fetch, ACT.Gelu, False, lambda s: xnT, lambda e, tile: gates[:, tile, 0:1])

    rms_w = sb("rms_w", [P, E])
    if begins(3):
        one_gate_experts()

    def block_diagonal(dst, lhs, rhs, bank, landed):
        PE.wait(landed)
        m = PE.mark(nc.tensor.matmul(psum[:, bank, 0:P], lhs, rhs, start=True, stop=True))
        b3 = block[:, :].unsqueeze(2).to_broadcast([P, 8, 16])
        V(lambda e: e.tensor_tensor(dst.rearrange("p (h c) -> p h c", h=8),
                                    psum[:, bank, 0:P].rearrange("p (h c) -> p h c", h=8), b3, ALU.mult), m)

    def shared_head_attention():
        rep = weights[0:16, 0:3 * P].rearrange("p (n h c) -> p n h c", n=3, h=8)
        raw = weights[0:16, 3 * P:3 * P + 48].rearrange("p (n c) -> p n c", n=3)
        bd = weights[:, 512:512 + 2 * P].rearrange("p (n c) -> p n c", n=2)
        wo_rows = weights[:, 1024:1024 + KD * D].rearrange("p (k d) -> p k d", k=KD)
        woT = weights[:, 2048:2048 + KD * D].rearrange("p (k d) -> p k d", k=KD)
        bo = weights[:, 3072:3072 + D]
        mask_i = prep[:, 7000:7000 + NT * S2].bitcast(I32).rearrange("p (t s) -> p t s", t=NT)
        for n, name in enumerate(("Wk", "Wq", "Wv")):
            got = load(dma_a, raw[:, n, :], a["L2_xattn_" + name])
        load(dma_b, wo_rows, a["L2_xattn_Wo"].rearrange("(k p) d -> p k d", p=P))
        got_o = load(dma_b, bo, bcast(a["L2_xattn_bo"], D))
        got_m = load(dma_c, mask_i, a["mask_Bx1xSxS2_ik1"][:, 0].rearrange("b (t p) s -> p (b t) s", p=P))
        statistics(x, 1e-5)
        V(lambda e: e.tensor_scalar(bias[:, :, :], mask_i, 0.0, -1e20, ALU.is_equal, ALU.mult), got_m)
        for n in range(3):
            V(lambda e: e.tensor_copy(rep[:, n, :, :], raw[:, n, :].unsqueeze(1).to_broadcast([16, 8, 16])), got)
        wide_rep = rep[:, :, :, :].rearrange("p n h c -> p n (h c)")
        block_diagonal(bd[:, 0, :], wide_rep[:, 0, :], wide_rep[:, 1, :], 0, V.last())
        eye = weights[0:16, 3400:3400 + P].rearrange("p (h c) -> p h c", h=8)
        V(lambda e: e.tensor_copy(eye, ident[0:16, 0:16].unsqueeze(1).to_broadcast([16, 8, 16])))
        block_diagonal(bd[:, 1, :], wide_rep[:, 2, :], eye.rearrange("p h c -> p (h c)"), 1, V.last())
        for k in range(KD):
            PE.wait(got_o)
            for o in range(KD):
                ins = nc.tensor.transpose(psum[:, 2 + k, o * P:(o + 1) * P], wo_rows[:, o, k * P:(k + 1) * P], ident[:, :])
            turned_ = V(lambda e: e.tensor_copy(woT[:, k, :], psum[:, 2 + k, 0:D]), PE.mark(ins))

        def projection(n):
            def of(dst, g):
                PE.wait(V.last())
                return PE.mark(nc.tensor.matmul(dst, bd[:, n, :], ctxT[:, g, :], start=True, stop=True))
            return of
        prepare_narrow(projection(0), projection(1), woT, turned_, None, bo)
        fence()
        attention(x, NARROW, 1.0 / 16.0, True, tanh_g[:, 2:3])

    if begins(4):
        shared_head_attention()

    def best_expert():
        x_rows, y_rows = (scratch(n, (15 * CHUNK, D)) for n in ("L2_sorted", "L2_results"))
        fetch_expert(ahead, 1, a["L2_ffn_sh_gate"], a["L2_ffn_sh_up"], a["L2_ffn_sh_down"], None)
        descending()
        load(dma_b, w_gate, a["L2_ffn_gate_w"].rearrange("(k p) e -> p k e", p=P))
        clear_rows(x_rows)
        statistics(x, 1e-5)
        fence(spare=ahead)
        feed_input(x, xnT, router(False))
        best = wide[:, 0]
        first_best(best, logits[:, :, :], top_a[:, :], order[:, :])
        A(lambda e: e.activation(top_a[:, :], top_a[:, :], ACT.Exp, scale=-1.0), V.last())
        V(lambda e: e.tensor_scalar(top_a[:, :], top_a[:, :], 1.0, None, ALU.add), A.last())
        V(lambda e: e.reciprocal(top_a[:, :], top_a[:, :]))
        V(lambda e: e.tensor_tensor(rstd[:, :], rstd[:, :], top_a[:, :], ALU.mult))
        fence()
        routed(1, 5, 3, x_rows, y_rows, a["L2_ffn_rt_gate"], a["L2_ffn_rt_up"], a["L2_ffn_rt_down"], [best], None,
               lambda k, t: tanh_g[:, 6:7], lambda t: normalise(inner[:, t, :], x, t),
               lambda: experts(x, [(1, None)], ACT.Silu, True, lambda s: xnT, lambda s, tile: tanh_g[:, 6:7]))

    if begins(5):
        best_expert()

    def biased_attention():
        w = [weights[:, n * KD * D:(n + 1) * KD * D].rearrange("p (k d) -> p k d", k=KD) for n in range(4)]
        kv_bias = weights[:, 2400:2404]
        bq = weights[:, 2404:2406]
        bo = weights[:, 2410:2410 + D]
        for n, name in enumerate(("Wq", "Wk", "Wv", "Wo")):
            got = load(dma_a, w[n], a["L3_xattn_" + name].rearrange("(k p) d -> p k d", p=P))
        for g in range(KD):
            for n, name in enumerate(("bk", "bv")):
                load(dma_b, kv_bias[:, 2 * g + n:2 * g + n + 1],
                     a["L3_xattn_" + name][g * P:(g + 1) * P].rearrange("(p o) -> p o", o=1), columns=True)
            load(dma_b, bq[:, g:g + 1], a["L3_xattn_bq"][g * P:(g + 1) * P].rearrange("(p o) -> p o", o=1), columns=True)
        got_b = load(dma_b, bo, bcast(a["L3_xattn_bo"], D))
        statistics(x, 1e-5)
        V.wait(got_b, got)

        def projection(n):
            def of(dst, g):
                PE.wait(got)
                for k in range(KD):
                    ins = nc.tensor.matmul(dst, w[n][:, k, g * P:(g + 1) * P], ctxT[:, k, :], start=(k == 0), stop=(k == KD - 1))
                return PE.mark(ins)
            return of
        prepare_narrow(projection(1), projection(2), w[3], got, kv_bias, bo)
        fence()
        q_read = [None, None]

        def project(par, so, after):
            PE.wait(after)
            for g in range(KD):
                for k in range(KD):
                    ins = nc.tensor.matmul(so[:, g * P:(g + 1) * P], w[0][:, k, g * P:(g + 1) * P], xnTt[:, par, k, :],
                                           start=(k == 0), stop=(k == KD - 1))
            m = PE.mark(ins)
            for g in range(KD):
                r = A(lambda e: e.activation(qTt[:, par, g, :], so[:, g * P:(g + 1) * P], ACT.Identity,
                                             bias=bq[:, g:g + 1]), m)
            return r
        attention(x, NARROW, 0.25, False, tanh_g[:, 3:4], project=project)

    if begins(6):
        biased_attention()

    def latent_block():
        L = H * HD3
        EPS = 1e-5
        PARTS = 3
        STACK = PARTS * PARTS * HD3
        ROWS = STACK + PARTS
        SLOTS, TURN = 4, H
        q_dram = scratch("q_heads", (B * H, PARTS, HD3, S), BF16)
        qk_parts = scratch("qk_parts", (2, PARTS, B * H, HD3, S), BF16)
        k_dram = scratch("k_heads", (B * H, PARTS, PARTS, HD3, S), BF16)
        heads = weights[0:ROWS, 0:SLOTS * S].bitcast(BF16).rearrange("p (n s c) -> p n s c", n=2, s=SLOTS)
        values = weights[:, 4096:4096 + NT * H * 9].rearrange("p (t h c) -> p t h c", t=NT, h=H)
        small_w = weights[:, 6400:8192]
        PT_COLS = sum(S - j * P for j in range(TB))
        expT = prep[:, 0:2 * PT_COLS].rearrange("p (n c) -> p n c", n=2)
        Kflat = Kt[:, :, :, :].rearrange("p b k c -> p (b k c)")
        Vflat = Vt[:, :, :, :].rearrange("p b c d -> p (b c d)")
        cosT, sinT = Kflat[:, 0:S], Kflat[:, S:2 * S]
        masks = Kflat[:, 2 * S:2 * S + 192].bitcast(BF16).rearrange("p (n c) -> p n c", n=3)
        causal, causalT, ident16 = (masks[:, n, :] for n in range(3))
        mrow = Kflat[0:TB, 3 * S:3 * S + 2 * P].rearrange("p (n c) -> p n c", n=2)
        mparts = Kflat[0:TB, 3 * S + 2 * P:3 * S + 5 * P].bitcast(BF16).rearrange("p (n a c) -> p n a c", n=2, a=PARTS)
        head_values = Kflat[:, 4 * S + P:4 * S + P + 2 * TB * 9].rearrange("p (n t c) -> p n t c", n=2, c=9)
        sums = Vflat[0:9, 0:2 * S].rearrange("p (n c) -> p n c", n=2)
        qT, kT = Vflat[:, 0:NT * P], Vflat[:, NT * P:2 * NT * P]
        cT = Vflat[:, 2 * NT * P:2 * NT * P + 2 * GRP].rearrange("p (n c) -> p n c", n=2)
        wd = prep[:, 0:KD * L].rearrange("p (k l) -> p k l", k=KD)
        wqkv = prep[:, 256:256 + 5 * L].rearrange("p (n l) -> p n l", n=5)
        w_up = small_w[:, 0:D]
        gain = small_w[:, 256:260].rearrange("p (n k) -> p n k", n=2)
        rope = prep[:, 1024:1024 + 4 * GRP].rearrange("p (n c) -> p n c", n=4)
        split = prep[:, 3072:3072 + 2 * PARTS * S].bitcast(BF16).rearrange("p (n a c) -> p n a c", n=2, a=PARTS)
        attended = shared[:, 0:NT * L].rearrange("p (t l) -> p t l", t=NT)
        maxima = row[:, :, 0:TB]
        shares = row[:, :, 16:16 + TB]

        load(dma_a, cosT, a["rope_cos"])
        load(dma_a, sinT, a["rope_sin"])
        load(dma_b, wd, a["L3_ffn_w_down"].rearrange("(k p) l -> p k l", p=P))
        for n, name in enumerate(("wq", "wk", "wv")):
            load(dma_b, wqkv[:, n, :], a["L3_ffn_" + name])
        load(dma_b, w_up, a["L3_ffn_w_up"])
        for n, name in enumerate(("g1", "g2")):
            got = load(dma_b, gain[:, n, :], a["L3_ffn_" + name].rearrange("(k p) -> p k", p=P), columns=True)
        load(dma_c, w_gate, a["L3_ffn_router_w"].rearrange("(k p) e -> p k e", p=P))
        descending()
        for mask_, sign in ((causal, 1), (causalT, -1)):
            G(lambda e: e.memset(mask_, 0.0))
            G(lambda e: e.affine_select(out=mask_, in_=mask_, compare_op=ALU.is_ge, fill=NEG, base=0,
                                        pattern=[[-sign, P]], channel_multiplier=sign))
        G(lambda e: e.tensor_copy(ident16, ident[:, :]))
        G(lambda e: e.memset(values[:, :, :, :].rearrange("p t h c -> p (t h c)"), 1.0))
        G(lambda e: e.memset(heads[:, 1, :, :].rearrange("p s c -> p (s c)"), 1.0))
        statistics(x, 1e-5)
        for t in range(NT):
            normalise(inner[:, t, :], x, t)
            collect(inner, t)
        collected.add(id(inner))

        def mean_square_statistics():
            statistics(inner, EPS)
            sq = top_a[:, :]
            V(lambda e: e.tensor_tensor(sq, meanvar[:, :, 0], meanvar[:, :, 0], ALU.mult))
            V(lambda e: e.tensor_tensor(meanvar[:, :, 1], meanvar[:, :, 1], sq, ALU.add))
            reciprocal_root(meanvar[:, :, 1], EPS, None)
            V(lambda e: e.memset(meanvar[:, :, 0], 0.0))

        mean_square_statistics()
        for n in range(2):
            w = wqkv[:, n, :].rearrange("p (j two) -> p j two", two=2)
            sw = wqkv[:, 3 + n, :].rearrange("p (j two) -> p j two", two=2)
            V(lambda e: e.tensor_scalar(sw[:, :, 0], w[:, :, 1], -1.0, None, ALU.mult), got)
            V(lambda e: e.tensor_scalar(sw[:, :, 1], w[:, :, 0], 1.0, None, ALU.mult))
        fence()
        feed_input(inner, xnT, gain=gain[:, 0, :])
        cT_read = None
        for g in range(NG):
            par = g % 2
            for k in range(KD):
                ins = nc.tensor.matmul(psum[:, 0, :], wd[:, k, :], xnT[:, k, g * GRP:(g + 1) * GRP],
                                       start=(k == 0), stop=(k == KD - 1))
            cp = A(lambda e: e.copy(cT[:, par, :], psum[:, 0, :]), PE.mark(ins))
            PE.wait(cp, cT_read)
            for n, w in enumerate((0, 3, 1, 4)):
                m = PE.mark(nc.tensor.matmul(psum[:, 1 + n, :], wqkv[:, w, :], cT[:, par, :], start=True, stop=True))
            for t in range(TG):
                mv = PE.mark(nc.tensor.matmul(psum[:, 5, t * P:(t + 1) * P], cT[:, par, t * P:(t + 1) * P],
                                              wqkv[:, 2, :], start=True, stop=True))
            at = (g * GRP) % S
            for n, dst in ((0, qT), (2, kT)):
                V(lambda e: e.tensor_tensor(rope[:, n, :], psum[:, 1 + n, :], cosT[:, at:at + GRP], ALU.mult), m)
                V(lambda e: e.tensor_tensor(rope[:, n + 1, :], psum[:, 2 + n, :], sinT[:, at:at + GRP], ALU.mult))
                V(lambda e: e.tensor_tensor(dst[:, g * GRP:(g + 1) * GRP], rope[:, n, :], rope[:, n + 1, :], ALU.add))
            cT_read = A(lambda e: e.copy(values[:, g * TG:(g + 1) * TG, :, 0:HD3],
                                         psum[:, 5, :].rearrange("p (t h c) -> p t h c", t=TG, h=H)), mv)
            PE.wait(V.last(), cT_read)
        for n, src in enumerate((qT, kT)):
            for a_ in range(PARTS):
                part = A(lambda e: e.copy(split[:, n, a_, :], src), V.last())
                if a_ < PARTS - 1:
                    V(lambda e: e.tensor_tensor(src, src, split[:, n, a_, :], ALU.subtract), part)
            for a_ in range(PARTS):
                for bt in range(B):
                    stored = load(dma_a, qk_parts[n, a_, bt * H:(bt + 1) * H].rearrange("h c s -> (h c) s"),
                                  split[:, n, a_, bt * S:(bt + 1) * S], part)
        by_head = [qk_parts[n].rearrange("a h c s -> h a (c s)") for n in range(2)]
        load(dma_b, q_dram.rearrange("h a c s -> h a (c s)"), by_head[0], stored)
        for b_ in range(PARTS):
            load(dma_b, k_dram[:, :, b_].rearrange("h a c s -> h a (c s)"), by_head[1])
        fence()

        def fetch_head(slot_, index, *after):
            lane = more_lanes[slot_]
            load(lane, heads[0:STACK, 1, slot_, :], k_dram[index].rearrange("a b c s -> (a b c) s"), *after)
            for a_ in range(PARTS):
                got_ = load(lane, heads[a_ * PARTS * HD3:(a_ + 1) * PARTS * HD3, 0, slot_, :],
                            q_dram[index].rearrange("b c s -> (b c) s"))
            return got_

        for s in range(3):
            fetch_head(s, s)
        fence()
        start = [sum(S - i * P for i in range(j)) for j in range(TB)]
        with nc.Fori(0, B * H // TURN) as i:
            free = [None, None]
            ring = Ring([4, 5])
            landed = {0: None, 1: None, 2: None}
            values_read, sums_read, exp_read, out_free = [None, None], [None, None], [None, None], None
            state = {"n": 0, "out_free": None}

            def score_maximum(h, t):
                s, n = h % SLOTS, state["n"]
                state["n"] += 1
                cols, base = (t + 1) * P, (n % 2) * 2 * BANK
                PE.wait(free[n % 2], landed[h])
                for at in range(0, cols, BANK):
                    w = min(BANK, cols - at)
                    ins = nc.tensor.matmul(flat[:, base + at:base + at + w], heads[0:STACK, 0, s, t * P:(t + 1) * P],
                                           heads[0:STACK, 1, s, at:at + w], start=True, stop=True)
                m = PE.mark(nc.tensor.matmul(flat[:, base + t * P:base + cols], ident16, causal, start=False, stop=True,
                                             skip_group_check=True))
                free[n % 2] = V(lambda e: e.tensor_reduce(maxima[:, h % 2, t:t + 1], flat[:, base:base + cols], AX.X, ALU.max), m,
                                maxima_read.get(h - 2))
                maximum_known[h] = free[n % 2]

            maximum_known, maxima_read = {}, {}

            def maxima_rows(h):
                bank, fr = ring.take()
                PE.wait(maximum_known[h], fr)
                tr = PE.mark(nc.tensor.transpose(psum[0:TB, bank, 0:P], maxima[:, h % 2, :], ident[:, :]))
                maxima_read[h] = tr
                left = mrow[:, h % 2, :]
                r = A(lambda e: e.mul(left, psum[0:TB, bank, 0:P], -1.0), tr)
                ring.give(r)
                A.wait(rows.get(h - 2))
                for a_ in range(PARTS):
                    r = A(lambda e: e.copy(mparts[:, h % 2, a_, :], left), V.last())
                    if a_ < PARTS - 1:
                        V(lambda e: e.tensor_tensor(left, left, mparts[:, h % 2, a_, :], ALU.subtract), r)
                for a_ in range(PARTS):
                    got_ = load((dma_c, dma_d)[h % 2], heads[STACK + a_:STACK + a_ + 1, 0, h % SLOTS, :],
                                mparts[:, h % 2, a_, :], r)
                return got_

            def exponentials(h, j, rows_landed):
                s = h % SLOTS
                for at in range(j * P, S, BANK):
                    w = min(BANK, S - at)
                    bank, fr = ring.take()
                    PE.wait(rows_landed, fr)
                    m = PE.mark(nc.tensor.matmul(psum[:, bank, 0:w], heads[:, 1, s, j * P:(j + 1) * P],
                                                 heads[:, 0, s, at:at + w], start=True, stop=True))
                    to = start[j] + at - j * P
                    if at == j * P:
                        m = PE.mark(nc.tensor.matmul(psum[:, bank, 0:P], ident16, causalT, start=False, stop=True,
                                                     skip_group_check=True))
                    ring.give(A(lambda e: e.activation(expT[:, h % 2, to:to + w], psum[:, bank, 0:w], ACT.Exp,
                                                       scale=float(HD3) ** -0.5), m, exp_read[h % 2]))

            def weigh(h, keys, done_exp):
                p_ = h % 2
                PE.wait(done_exp, vals[p_])
                if keys[0] == 0:
                    PE.wait(sums_read[0])
                for j in keys:
                    for lo, hi in ((0, BANK), (BANK, S)):
                        lo = max(lo, j * P)
                        if lo < hi:
                            ins = nc.tensor.matmul(flat[0:9, 6 * BANK + lo:6 * BANK + hi], head_values[:, p_, j, :],
                                                   expT[:, p_, start[j] + lo - j * P:start[j] + hi - j * P],
                                                   start=(j == 0), stop=(j == TB - 1 or (hi == BANK and j == 3)))
                return PE.mark(ins)

            def keep_sums(h, m):
                p_ = h % 2
                sums_read[0] = A(lambda e: e.copy(sums[:, p_, :], flat[0:9, 6 * BANK:8 * BANK]), m, sums_read[1])

            def divide(h):
                p_ = h % 2
                bank, fr = ring.take()
                PE.wait(sums_read[0], fr)
                o = psum[:, bank, 0:TB * 9].rearrange("p (t c) -> p t c", c=9)
                for t in range(TB):
                    ins = nc.tensor.transpose(o[:, t, :], sums[:, p_, t * P:(t + 1) * P], ident[0:9, 0:9])
                m = PE.mark(ins)
                sums_read[1] = m
                V(lambda e: e.reciprocal(shares[:, p_, :], o[:, :, HD3]), m)
                dst = attended.rearrange("p (b t) (h c) -> p b t h c", b=B, h=H)[:, i // (H // TURN), :,
                                                                                 (i * TURN + h) % H, :]
                ring.give(V(lambda e: e.tensor_tensor(dst, o[:, :, 0:HD3],
                                                      shares[:, p_, :].unsqueeze(2).to_broadcast([P, TB, HD3]), ALU.mult)))

            vals = [None, None]

            def take_values(h):
                vals[h % 2] = G(lambda e: e.tensor_copy(
                    head_values[:, h % 2, :, :],
                    values.rearrange("p (b t) h c -> p b t h c", b=B)[:, i // (H // TURN), :, (i * TURN + h) % H, :]),
                    values_read[h % 2])

            rows, done_exp = {}, {}
            for h in range(2):
                for t in range(TB):
                    score_maximum(h, t)
                rows[h] = maxima_rows(h)
            for h in range(TURN + 1):
                if h < TURN:
                    nxt = fetch_head((h + 3) % SLOTS, (i * TURN + h + 3) % (B * H), PE.last())
                    if h + 3 < TURN:
                        landed[h + 3] = nxt
                    take_values(h)
                for j in range(TB):
                    if h < TURN:
                        exponentials(h, j, rows[h])
                    if h + 2 < TURN:
                        score_maximum(h + 2, j)
                    if h >= 1:
                        m = weigh(h - 1, (j,), done_exp[h - 1])
                    if j == 0 and 2 <= h + 1 < TURN:
                        rows[h + 1] = maxima_rows(h + 1)
                    if j == 3 and h >= 2:
                        divide(h - 2)
                if h < TURN:
                    done_exp[h] = A.last()
                if h >= 1:
                    exp_read[(h - 1) % 2] = values_read[(h - 1) % 2] = m
                    keep_sums(h - 1, m)
            divide(TURN - 1)
            fence()

        oT_read, free = [None, None], [None, None]
        for t in range(NT):
            par = t % 2
            bank = psum[:, par, :]
            PE.wait(free[par])
            tr = PE.mark(nc.tensor.transpose(bank[:, 0:P], attended[:, t, :], ident[:, :]))
            cp = A(lambda e: e.copy(xnTt[:, par, 0, :], bank[:, 0:P]), tr, oT_read[par])
            PE.wait(cp)
            m = PE.mark(nc.tensor.matmul(bank[:, D:2 * D], xnTt[:, par, 0, :], w_up, start=True, stop=True))
            oT_read[par] = m
            free[par] = V(lambda e: e.tensor_tensor(inner[:, t, :], bank[:, D:2 * D], inner[:, t, :], ALU.add), m)
            collect(inner, t)
        mean_square_statistics()
        gain2 = small[:, 600:602]
        V(lambda e: e.tensor_copy(gain2, gain[:, 1, :]))
        fence()

        x_rows, y_rows = (scratch(n, (24 * CHUNK, D)) for n in ("L3_sorted", "L3_results"))
        clear_rows(x_rows)
        row_gain = small[:, 604:606]
        load(dma_e, row_gain, a["L3_ffn_g2"].rearrange("(p k) -> p k", k=KD))
        fence(spare=ahead)
        feed_input(inner, xnT, router(False, gain2), gain=gain2)
        p, first_, second_, left = (wide[:, n] for n in range(4))
        V(lambda e: e.tensor_reduce(top_a[:, :], logits[:, :, :], AX.X, ALU.max))
        V(lambda e: e.tensor_tensor(p, logits[:, :, :], over(top_a[:, :]), ALU.subtract))
        A(lambda e: e.activation(p, p, ACT.Exp), V.last())
        V.wait(A.last())
        first_best(first_, p, top_a[:, :], order[:, :])
        V(lambda e: e.scalar_tensor_tensor(left, first_, -2.0, p, ALU.mult, ALU.add))
        first_best(second_, left, top_b[:, :], order[:, :])
        V(lambda e: e.tensor_tensor(rank[:, :], top_a[:, :], top_b[:, :], ALU.add))
        V(lambda e: e.reciprocal(rank[:, :], rank[:, :]))
        for k, top in enumerate((top_a, top_b)):
            V(lambda e: e.tensor_tensor(gates[:, :, k], top[:, :], rank[:, :], ALU.mult))
            V(lambda e: e.tensor_scalar(gates[:, :, k], gates[:, :, k], tanh_g[:, 7:8], None, ALU.mult))
        for t in range(NT):
            V(lambda e: e.scalar_tensor_tensor(x[:, t, :], inner[:, t, :], tanh_g[:, 7:8], x[:, t, :], ALU.mult, ALU.add))
        fence()
        routed(2, 4, 6, x_rows, y_rows, a["L3_ffn_w1"], a["L3_ffn_w3"], a["L3_ffn_w2"], [first_, second_], row_gain,
               lambda k, t: gates[:, t, k:k + 1], lambda t: normalise(inner[:, t, :], inner, t), lambda: None)

    if begins(7):
        latent_block()
    finish()


_TYPES = {"f": F32, "i": I32}


def rotation_tables():
    freq = np.float32(1.0) / np.float32(10000.0) ** (np.arange(0, HD3, 2, dtype=np.float32) / np.float32(HD3))
    angle = freq[:, None] * np.arange(S, dtype=np.float32)[None, :]
    rows = np.tile(np.repeat(angle, 2, axis=0), (H, 1))
    return np.cos(rows).astype(np.float32), np.sin(rows).astype(np.float32)


def kernel(**inputs):
    import concourse.bacc as bacc
    from concourse.bass_utils import run_bass_kernel_spmd

    nc = bacc.Bacc("TRN2", target_bir_lowering=False, num_devices=1)
    arrays, aps = {}, {}
    for name, value in inputs.items():
        v = np.ascontiguousarray(value)
        arrays["in_" + name] = v
        aps[name] = nc.dram_tensor("in_" + name, v.shape, _TYPES[v.dtype.kind], kind="ExternalInput").ap()
    for name, table in zip(("rope_cos", "rope_sin"), rotation_tables()):
        arrays["in_" + name] = table
        aps[name] = nc.dram_tensor("in_" + name, table.shape, F32, kind="ExternalInput").ap()
    out = nc.dram_tensor("out_0", (B, S, D), F32, kind="ExternalOutput").ap()
    program(nc, aps, out)
    r = run_bass_kernel_spmd(nc, [arrays], core_ids=[0])
    return r.results[0]["out_0"]
```

```python
from contextlib import ExitStack

import numpy as np

import concourse.bass as bass
from concourse import mybir
from concourse.alu_op_type import AluOpType as ALU

F32 = mybir.dt.float32
I32 = mybir.dt.int32
BF16 = mybir.dt.bfloat16
ACT = mybir.ActivationFunctionType
AX = mybir.AxisListType

P = 128
B, S, D = 2, 1024, 256
KD = D // P
TB = S // P
NT = B * TB
H, S2 = 16, 77
HK = H * S2
CH = -(-HK // P)
LASTROWS = HK - (CH - 1) * P
HE = H * 64
NTE = HE // P
PAIR = 2 * S2
VPAD = P + PAIR
CTX = B * S2
E, F = 8, 512
FC = F // P
CHUNK = 256
GRP = 512
TG = GRP // P
NG = NT // TG
NEG = -1.0e30
BANK = 512
HD3 = 8


class Queue:

    def __init__(self, eng, sem, step=1):
        self.eng, self.sem, self.step, self.count, self.seen = eng, sem, step, 0, {}

    def wait(self, *marks):
        for mark in marks:
            if mark is None:
                continue
            queue, value = mark
            if self.seen.get(id(queue), 0) < value:
                self.eng.wait_ge(queue.sem, value)
                self.seen[id(queue)] = value

    def mark(self, ins):
        ins.then_inc(self.sem, self.step)
        self.count += self.step
        return (self, self.count)

    def last(self):
        return (self, self.count) if self.count else None

    def __call__(self, build, *after):
        self.wait(self.last(), *after)
        return self.mark(build(self.eng))


class Lane(Queue):

    def __init__(self, sem):
        super().__init__(None, sem, 16)


def program(nc, a, out):
    with ExitStack() as ctx:
        build(nc, ctx, a, out)


def build(nc, ctx, a, out):
    def sb(name, shape, dt=F32):
        return ctx.enter_context(nc.sbuf_tensor(name, shape, dt))

    def sem(name):
        return ctx.enter_context(nc.semaphore(name))

    def scratch(name, shape, dt=F32):
        return nc.dram_tensor(name, shape, dt, kind="Internal").ap()

    PE = Queue(nc.tensor, sem("pe_done"))
    V = Queue(nc.vector, sem("vector_done"))
    A = Queue(nc.scalar, sem("scalar_done"))
    G = Queue(nc.gpsimd, sem("gpsimd_done"))
    SP = Queue(nc.sync, sem("sync_unused"))
    dma_lanes = [Lane(sem(f"dma_{n}_landed")) for n in "abcdefghij"]
    dma_a, dma_b, dma_c, dma_d, dma_e, dma_f, *more_lanes = dma_lanes
    gather_lanes = [Lane(sem(f"gather_{n}_landed")) for n in "abcdefgh"]
    dma_lanes += gather_lanes
    lanes = [PE, V, A, G, *dma_lanes]

    def load(lane, dst, src, *after, columns=False):
        SP.wait(*after)
        return lane.mark(SP.eng.dma_start(dst, src, allow_slow_non_contiguous=columns))

    ahead = dma_f
    clearing = Lane(sem("clearing_landed"))

    def fence(spare=None):
        for lane in dma_lanes:
            if lane is not spare:
                SP.wait(lane.last())
        for q in (PE, V, A, G):
            q.wait(q.last())
        if any(lane.count for lane in gather_lanes):
            for lane in gather_lanes:
                G.wait(lane.last())
            nc.gpsimd.dma_reset(range(gather_lanes[0].sem.num, gather_lanes[-1].sem.num + 1))
        nc.all_engine_barrier()
        for q in lanes:
            if q.count and q is not spare:
                nc.vector.sem_clear(q.sem)
        nc.all_engine_barrier()
        for q in lanes:
            if q is not spare:
                q.count = 0
        for q in (PE, V, A, G, SP):
            q.seen = {}

    def join(spare=None):
        for q in (PE, V, A, G, SP):
            q.wait(*(other.last() for other in lanes if other is not spare))

    x = sb("x", [P, NT, D])
    inner = sb("inner", [P, NT, D])
    Kt = sb("Kt", [P, B, KD, HK])
    Vt = sb("Vt", [P, B, CH, D])
    weights = sb("weights", [P, 4 * 2048])
    expert_w = sb("expert_w", [P, 2 * 3072])
    prep = sb("prep", [P, 2048 + NTE * B * PAIR + B * (NTE * VPAD + P)])
    shared = sb("shared", [P, 2 * HK + 2 * CH * P])
    prob = shared[:, 0:2 * HK].rearrange("p (n c) -> p n c", n=2)
    probT = shared[:, 2 * HK:].rearrange("p (n c m) -> p n c m", n=2, c=CH)
    xnT = shared[:, 0:KD * NT * P].rearrange("p (k n) -> p k n", k=KD)
    bias = sb("bias", [P, NT, S2])
    ctxT = sb("ctxT", [P, KD, CTX])
    ident = sb("ident", [P, P])
    block = sb("block", [P, 8])
    ones = sb("ones", [P, P])
    small = sb("small", [P, 880])
    bn6 = sb("bn6", [P, NT, 6])
    meanvar = sb("meanvar", [P, NT, 2])
    rstd = sb("rstd", [P, NT])
    gates = sb("gates", [P, NT, E])
    tanh_g = sb("tanh_g", [P, 8])
    xn = sb("xn", [P, 2, D])
    xnTt = sb("xnTt", [P, 2, KD, P])
    qTt = sb("qTt", [P, 2, KD, P])
    row = sb("row", [P, 2, 64])
    psum = ctx.enter_context(nc.psum_tensor("psum", [P, 8, BANK], F32))
    flat = psum[:, :, :].rearrange("p b c -> p (b c)")

    sT = inner[:, :, :].rearrange("p t d -> p (t d)").rearrange("p (k n) -> p k n", k=KD)

    def bcast(src, n):
        return src.rearrange("(o n) -> o n", o=1).to_broadcast([P, n])

    def head64(ap):
        return ap.rearrange("(k p) n h -> p k (n h)", p=P)

    def fetch_wide(lanes_, wq, wk, wv, wo):
        return [load(lane, weights[:, at:at + 2048].rearrange("p (k n) -> p k n", k=k), w)
                for lane, at, w, k in zip(lanes_, (2048, 4096, 0, 6144), (wk, wv, wq, wo), (KD, KD, KD, NTE))]

    fside = sb("fside", [P, NT, S2])
    graw = small[:, 0:8]
    load(dma_b, graw[:, 0:4], bcast(a["g_xattn"], 4))
    load(dma_b, graw[:, 4:8], bcast(a["g_ffn"], 4))
    ctx_rows = prep[:, 0:2 * D].rearrange("p (k d) -> p k d", k=2)
    ctx_flat = a["ctx_1024"].rearrange("b s d -> (b s) d")
    load(dma_b, ctx_rows[:, 0, :], ctx_flat[0:P])
    load(dma_b, ctx_rows[0:CTX - P, 1, :], ctx_flat[P:CTX])
    wide0 = fetch_wide(more_lanes, head64(a["L0_xattn_wq"]), head64(a["L0_xattn_wk"]), head64(a["L0_xattn_wv"]),
                       a["L0_xattn_wo"].rearrange("n h d -> (n h) d").rearrange("(t p) d -> p t d", p=P))
    for bt in range(B):
        got_x = load(dma_a, x[:, bt * TB:(bt + 1) * TB, :], a["x"][bt].rearrange("(t p) d -> p t d", p=P))
    load(dma_c, bias[:, :, :], a["mask_Bx1xSxS2_ff0"][:, 0].rearrange("b (t p) s -> p (b t) s", p=P))
    load(dma_c, fside[:, :, :], a["fside_BxSxS2_0"].rearrange("b (t p) s -> p (b t) s", p=P))
    G(lambda e: e.memset(ones[:, :], 1.0))
    G(lambda e: e.affine_select(out=ident[:, :], in_=ones[:, :], compare_op=ALU.is_equal, fill=0.0,
                                base=0, pattern=[[-1, P]], channel_multiplier=1))
    G(lambda e: e.affine_select(out=block[:, :], in_=ones[:, 0:8], compare_op=ALU.is_ge, fill=0.0,
                                base=0, pattern=[[-16, 8]], channel_multiplier=1))
    const = G(lambda e: e.affine_select(out=block[:, :], in_=block[:, :], compare_op=ALU.is_ge,
                                        fill=0.0, base=15, pattern=[[16, 8]], channel_multiplier=-1))
    A(lambda e: e.activation(tanh_g[:, :], graw, ACT.Tanh), dma_b.last())
    PE.wait(const, dma_b.last())
    for k in range(KD):
        nc.tensor.transpose(psum[:, k, 0:P], ctx_rows[:, 0, k * P:(k + 1) * P], ident[:, :])
        t = PE.mark(nc.tensor.transpose(psum[:, k, P:CTX], ctx_rows[0:CTX - P, 1, k * P:(k + 1) * P],
                                        ident[0:CTX - P, 0:CTX - P]))
        V(lambda e: e.tensor_copy(ctxT[:, k, :], psum[:, k, 0:CTX]), t)
    PE.wait(V.last())


    collected = set()

    def collect(src, tile):
        return V(lambda e: e.bn_stats(bn6[:, tile, :], src[:, tile, :]))

    def statistics(src, inside=None, outside=None):
        if id(src) not in collected:
            for t in range(NT):
                collect(src, t)
        V.wait(V.last())
        for t in range(NT):
            V.mark(nc.vector.bn_aggr(meanvar[:, t, :], bn6[:, t, :]))
        reciprocal_root(meanvar[:, :, 1], inside, outside)

    def reciprocal_root(var, inside, outside):
        V(lambda e: e.tensor_scalar(rstd[:, :], var, inside or 0.0, None, ALU.add))
        r = A(lambda e: e.activation(rstd[:, :], rstd[:, :], ACT.Sqrt), V.last())
        V.wait(r)
        if outside:
            V(lambda e: e.tensor_scalar(rstd[:, :], rstd[:, :], outside, None, ALU.add))
        V(lambda e: e.reciprocal(rstd[:, :], rstd[:, :]))

    def normalise(dst, src, t, *after):
        return V(lambda e: e.tensor_scalar(dst, src[:, t, :], meanvar[:, t, 0:1], rstd[:, bass.ds(t, 1)],
                                           ALU.subtract, ALU.mult), *after)

    def turn(src, dst_psum, *after):
        PE.wait(*after)
        for k in range(KD):
            ins = nc.tensor.transpose(dst_psum[:, k * P:(k + 1) * P], src[:, k * P:(k + 1) * P],
                                      ident[:, :])
        return PE.mark(ins)

    class Ring:

        def __init__(self, banks):
            self.banks, self.free, self.n = banks, [None] * len(banks), -1

        def take(self):
            self.n = (self.n + 1) % len(self.banks)
            return self.banks[self.n], self.free[self.n]

        def give(self, mark):
            self.free[self.n] = mark


    WqT = prep[:, 0:2048].rearrange("p (t d) -> p t d", t=NTE)
    kexp = prep[:, 2048:2048 + NTE * B * PAIR].rearrange("p (t b c) -> p t b c", t=NTE, b=B)
    vexp = prep[:, 2048 + NTE * B * PAIR:].rearrange("p (b c) -> p b c", b=B)
    vexp16 = prep[:, 2048:2048 + B * KD * HK].rearrange("p (b g c) -> p b g c", b=B, g=KD)

    def clear_expanded():
        cut = 2048 + (prep.shape[1] - 2048) // 4
        G(lambda e: e.memset(prep[:, 2048:cut], 0.0))
        V(lambda e: e.memset(prep[:, cut:], 0.0))
        A.wait(G.last(), V.last())

    def prepare_wide(landed=(None,) * 4):
        Wq = weights[:, 0:2048].rearrange("p (k n) -> p k n", k=KD)
        Wk = weights[:, 2048:4096].rearrange("p (k n) -> p k n", k=KD)
        Wv = weights[:, 4096:6144].rearrange("p (k n) -> p k n", k=KD)
        Wo = weights[:, 6144:8192].rearrange("p (t d) -> p t d", t=NTE)
        ring = Ring(list(range(8)))
        for w, there, scale, dst in ((Wk, landed[0], 0.125, lambda t, i: kexp[64 * i:64 * i + 64, t, :, S2 * i:S2 * i + S2]),
                                      (Wv, landed[1], 1.0, lambda t, i: vexp[64 * i:64 * i + 64, :, t * VPAD + P + S2 * i:t * VPAD + P + S2 * i + S2])):
            for t in range(NTE):
                bank, free = ring.take()
                PE.wait(there, free)
                for k in range(KD):
                    ins = nc.tensor.matmul(psum[:, bank, 0:CTX], w[:, k, t * P:(t + 1) * P], ctxT[:, k, :],
                                           start=(k == 0), stop=(k == KD - 1))
                m = PE.mark(ins)
                for i in range(2):
                    src = psum[64 * i:64 * i + 64, bank, 0:CTX].rearrange("p (b c) -> p b c", b=B)
                    r = A(lambda e: e.mul(dst(t, i), src, scale), m)
                ring.give(r)
        for t in range(0, NTE, 2):
            bank, free = ring.take()
            PE.wait(landed[2], free)
            for i in range(2):
                for k in range(KD):
                    ins = nc.tensor.transpose(psum[:, bank, (2 * i + k) * P:(2 * i + k + 1) * P],
                                              Wq[:, k, (t + i) * P:(t + i + 1) * P], ident[:, :])
            m = PE.mark(ins)
            turned = V(lambda e: e.tensor_copy(WqT[:, t:t + 2, :].rearrange("p t d -> p (t d)"), psum[:, bank, :]), m)
            ring.give(turned)
        kv_done = A.last()
        for t in range(NTE):
            for k in range(KD):
                bank, free = ring.take()
                PE.wait(turned, kv_done, free)
                m = PE.mark(nc.tensor.matmul(psum[:, bank, 0:B * PAIR], WqT[:, t, k * P:(k + 1) * P],
                                             kexp[:, t, :, :].rearrange("p b c -> p (b c)"), start=True, stop=True))
                ring.give(A(lambda e: e.copy(Kt[:, :, k, t * PAIR:(t + 1) * PAIR],
                                             psum[:, bank, 0:B * PAIR].rearrange("p (b c) -> p b c", b=B)), m))
        for bt in range(B):
            for c in range(0, CH, 2):
                bank, free = ring.take()
                PE.wait(landed[3], free)
                for i in range(2):
                    pairs = [t for t in range(NTE) if t * PAIR < (c + i + 1) * P and (t + 1) * PAIR > (c + i) * P]
                    for t in pairs:
                        at = (c + i) * P - t * PAIR + P + t * VPAD
                        ins = nc.tensor.matmul(psum[:, bank, i * D:(i + 1) * D], vexp[:, bt, at:at + P], Wo[:, t, :],
                                               start=(t == pairs[0]), stop=(t == pairs[-1]))
                m = PE.mark(ins)
                ring.give(V(lambda e: e.tensor_copy(Vt[:, bt, c:c + 2, :].rearrange("p c d -> p (c d)"), psum[:, bank, :]), m))

    def prepare_narrow(kT_of, vT_of, wo_turned, wo_after, kv_bias, out_bias):
        V(lambda e: e.tensor_scalar(out_bias, out_bias, 1.0 / H, None, ALU.mult), wo_after)
        kc = small[:, 0:KD * CTX].rearrange("p (g c) -> p g c", g=KD)
        vc = small[:, KD * CTX:2 * KD * CTX].rearrange("p (g c) -> p g c", g=KD)
        zeroed = G(lambda e: e.memset(vexp16[:, :, :, :].rearrange("p b g c -> p (b g c)"), 0.0))
        ring = Ring([4, 5, 6, 7])
        for g in range(KD):
            for n, (of, dst) in enumerate(((kT_of, kc), (vT_of, vc))):
                bank, free = ring.take()
                PE.wait(free)
                m = of(psum[:, bank, 0:CTX], g)
                add = kv_bias[:, 2 * g + n:2 * g + n + 1] if kv_bias is not None else 0.0
                r = V(lambda e: e.tensor_scalar(dst[:, g, :], psum[:, bank, 0:CTX], add, None, ALU.add), m)
                ring.give(r)
            for h in range(8):
                V(lambda e: e.tensor_scalar(Kt[:, :, g, h * S2:(h + 1) * S2],
                                            kc[:, g, :].rearrange("p (b c) -> p b c", b=B),
                                            block[:, h:h + 1], None, ALU.mult))
                at = (g * 8 + h) * S2
                V(lambda e: e.tensor_scalar(vexp16[:, :, g, at:at + S2],
                                            vc[:, g, :].rearrange("p (b c) -> p b c", b=B),
                                            block[:, h:h + 1], None, ALU.mult), zeroed)
        expanded = V.last()
        for bt in range(B):
            for c in range(CH):
                bank, free = ring.take()
                PE.wait(expanded, free, wo_after)
                rows = min(P, HK - c * P)
                halves = [g for g in range(KD) if g * 8 * S2 < (c + 1) * P and (g + 1) * 8 * S2 > c * P]
                for g in halves:
                    ins = nc.tensor.matmul(psum[0:rows, bank, 0:D], vexp16[:, bt, g, c * P:c * P + rows],
                                           wo_turned[:, g, :], start=(g == halves[0]), stop=(g == halves[-1]))
                m = PE.mark(ins)
                ring.give(V(lambda e: e.tensor_tensor(Vt[0:rows, bt, c, :], psum[0:rows, bank, 0:D], out_bias[0:rows, :],
                                                      ALU.add), m))


    WIDE = [[(n * BANK, min(BANK, HK - n * BANK), [(0, n * BANK), (1, n * BANK)])] for n in range(3)]
    HALF = 8 * S2
    NARROW = [[(0, BANK, [(0, 0)])],
              [(BANK, HALF - BANK, [(0, BANK)]), (HALF, 2 * BANK - HALF, [(1, 0)])],
              [(2 * BANK, HK - 2 * BANK, [(1, 2 * BANK - HALF)])]]

    def attention(stream, pieces, scale, biased, gate, project=None):
        free_s = [None, None]
        free_o = [None, None]
        free_p = [None, None]
        xn_read = [None, None]
        xt_read = [None, None]
        probT_read = [None, None]
        lhs_read = [None, None]

        def normal(t):
            return normalise(xn[:, t % 2, :], stream, t, xn_read[t % 2])

        def turn_tile(t, n):
            par = t % 2
            so = flat[:, (6 + par) * BANK:(6 + par) * BANK + D]
            tr = turn(xn[:, par, :], so, n, xt_read[par], free_o[par])
            xn_read[par] = tr
            return tr

        def keep_tile(t, tr):
            par = t % 2
            so = flat[:, (6 + par) * BANK:(6 + par) * BANK + D]
            cp = A(lambda e: e.copy(xnTt[:, par, :, :].rearrange("p k c -> p (k c)"), so), tr, lhs_read[par])
            xt_read[par] = cp
            return cp

        def queries(t, cp):
            par = t % 2
            if project is not None:
                cp = project(par, flat[:, (6 + par) * BANK:(6 + par) * BANK + D], cp)
                xt_read[par] = cp
            return cp

        def scores(t, cp):
            par = t % 2
            lhs = xnTt if project is None else qTt
            PE.wait(cp, free_s[par])
            for bank in pieces:
                for at, cols, parts in bank:
                    for k, src in parts:
                        ins = nc.tensor.matmul(flat[:, par * 3 * BANK + at:par * 3 * BANK + at + cols],
                                               lhs[:, par, k, :], Kt[:, t // TB, k, src:src + cols],
                                               start=(k == parts[0][0]), stop=(k == parts[-1][0]))
            lhs_read[par] = PE.mark(ins)
            return lhs_read[par]

        def softmax(t, m):
            par = t % 2
            S_ps = flat[:, par * 3 * BANK:par * 3 * BANK + HK].rearrange("p (h c) -> p h c", h=H)
            Pb = prob[:, par, :].rearrange("p (h c) -> p h c", h=H)
            negmax, total = row[:, par, 0:H], row[:, par, H:2 * H]
            V.wait(free_p[par], m)
            src = S_ps
            if biased:
                V(lambda e: e.tensor_tensor(Pb, S_ps, bias[:, t, :].unsqueeze(1).to_broadcast([P, H, S2]),
                                            ALU.add))
                src = Pb
            V(lambda e: e.tensor_reduce(negmax, src, AX.X, ALU.max, negate=True))
            V(lambda e: e.tensor_tensor(Pb, src, negmax.unsqueeze(2).to_broadcast([P, H, S2]), ALU.add))
            ex = A(lambda e: e.activation(prob[:, par, :], prob[:, par, :], ACT.Exp, scale=scale), V.last())
            return ex

        def share(t, ex):
            par = t % 2
            Pb = prob[:, par, :].rearrange("p (h c) -> p h c", h=H)
            total = row[:, par, H:2 * H]
            V(lambda e: e.tensor_reduce(total, Pb, AX.X, ALU.add), ex)
            V(lambda e: e.reciprocal(total, total))
            return V(lambda e: e.tensor_tensor(Pb, Pb, total.unsqueeze(2).to_broadcast([P, H, S2]), ALU.mult))

        def turn_probabilities(t, ready):
            par = t % 2
            base = par * 3 * BANK
            PE.wait(ready)
            marks = []
            for b0 in range(0, CH, 4):
                for c in range(b0, min(b0 + 4, CH)):
                    rows = min(P, HK - c * P)
                    ins = nc.tensor.transpose(flat[0:rows, base + c * P:base + (c + 1) * P],
                                              prob[:, par, c * P:c * P + rows], ident[:, :])
                marks.append(PE.mark(ins))
            free_p[par] = marks[-1]
            parts = []
            for b0, m in zip(range(0, CH, 4), marks):
                n = min(4, CH - 1 - b0)
                r = A(lambda e: e.copy(probT[:, par, b0:b0 + n, :].rearrange("p c n -> p (c n)"),
                                       flat[:, base + b0 * P:base + (b0 + n) * P]), m, probT_read[par])
                if b0 + n == CH - 1:
                    r = A(lambda e: e.copy(probT[0:LASTROWS, par, CH - 1, :],
                                           flat[0:LASTROWS, base + (CH - 1) * P:base + CH * P]))
                parts.append(r)
            free_s[par] = parts[-1]
            return parts

        def weigh_values(t, parts):
            par = t % 2
            PE.wait(free_o[par], xt_read[par])
            o = flat[:, (6 + par) * BANK + D:(6 + par) * BANK + 2 * D]
            for c in range(CH):
                rows = min(P, HK - c * P)
                PE.wait(parts[c // 4])
                ins = nc.tensor.matmul(o, probT[0:rows, par, c, :], Vt[0:rows, t // TB, c, :],
                                       start=(c == 0), stop=(c == CH - 1))
            probT_read[par] = PE.mark(ins)
            return probT_read[par]

        def residual(t, m):
            o = flat[:, (6 + t % 2) * BANK + D:(6 + t % 2) * BANK + 2 * D]
            free_o[t % 2] = V(lambda e: e.scalar_tensor_tensor(stream[:, t, :], o, gate, stream[:, t, :],
                                                               ALU.mult, ALU.add), m)
            collect(stream, t)

        cp = queries(0, keep_tile(0, turn_tile(0, normal(0))))
        scored = scores(0, cp)
        cp = queries(1, keep_tile(1, turn_tile(1, normal(1))))
        done = None
        for t in range(NT):
            ex = softmax(t, scored)
            n = normal(t + 2) if t + 2 < NT else None
            ready = share(t, ex)
            if done is not None:
                residual(t - 1, done)
            if t + 1 < NT:
                scored = scores(t + 1, cp)
            if t + 2 < NT:
                cp = keep_tile(t + 2, turn_tile(t + 2, n))
            parts = turn_probabilities(t, ready)
            if t + 2 < NT:
                cp = queries(t + 2, cp)
            done = weigh_values(t, parts)
        residual(NT - 1, done)
        join(spare=ahead)
        collected.add(id(stream))


    def slot(s):
        w = expert_w[:, s * 3072:(s + 1) * 3072]
        return (w[:, 0:1024].rearrange("p (k f) -> p k f", k=KD), w[:, 1024:2048].rearrange("p (k f) -> p k f", k=KD),
                w[:, 2048:3072].rearrange("p (f d) -> p f d", f=FC))

    bias1 = sb("bias1", [P, 2, FC])
    hidden = prep[:, 0:4 * GRP].rearrange("p (n c) -> p n c", n=4)
    gated_tmp = prep[:, 4 * GRP:6 * GRP].rearrange("p (n c) -> p n c", n=2)

    def fresh_state():
        return {"ring": Ring([0, 1, 2, 3]), "hid": [None] * 4, "y": [None, None], "n": 0, "tmp": [None, None]}

    def experts(acc, slots, func, gated, xT, gate_of, state=None, last=None, feed=None, between=None):
        state = state or fresh_state()
        hring = state["ring"]

        def first(s, landed, g, f):
            w1, w3, _ = slot(s)
            n = state["n"]
            state["n"] += 1
            outs = []
            for w in ((w1, w3) if gated else (w1,)):
                bank, free = hring.take()
                i = hring.n
                PE.wait(free, landed)
                for k in range(KD):
                    ins = nc.tensor.matmul(psum[:, bank, :], w[:, k, f * P:(f + 1) * P],
                                           xT(s)[:, k, g * GRP:(g + 1) * GRP], start=(k == 0), stop=(k == KD - 1))
                outs.append((bank, i, PE.mark(ins)))
            h = hidden[:, n % 4, :]
            if gated:
                (b0, i0, m0), (b1, i1, m1) = outs
                tm = gated_tmp[:, n % 2, :]
                r = A(lambda e: e.activation(tm, psum[:, b0, :], func), m0, state["tmp"][n % 2])
                hring.free[i0] = r
                r = V(lambda e: e.tensor_tensor(h, psum[:, b1, :], tm, ALU.mult), m1, r, state["hid"][n % 4])
                hring.free[i1] = r
                state["tmp"][n % 2] = r
            else:
                b0, i0, m0 = outs[0]
                r = A(lambda e: e.activation(h, psum[:, b0, :], func, bias=bias1[:, s, f:f + 1]),
                      m0, state["hid"][n % 4], landed)
                hring.free[i0] = r
            return n, r

        def second(s, g, f, n, ready):
            _, _, w2 = slot(s)
            y = flat[:, (4 + 2 * (g % 2)) * BANK:(6 + 2 * (g % 2)) * BANK]
            PE.wait(ready, state["y"][g % 2] if f == 0 else None)
            for t in range(TG):
                ins = nc.tensor.matmul(y[:, t * D:(t + 1) * D], hidden[:, n % 4, t * P:(t + 1) * P], w2[:, f, :],
                                       start=(f == 0 and t % 2 == 0), stop=(f == FC - 1), skip_group_check=True)
            m = PE.mark(ins)
            state["hid"][n % 4] = m
            if f == FC - 1:
                for t in range(TG):
                    tile = g * TG + t
                    state["y"][g % 2] = V(lambda e: e.scalar_tensor_tensor(
                        acc[:, tile, :], y[:, t * D:(t + 1) * D], gate_of(s, tile), acc[:, tile, :],
                        ALU.mult, ALU.add), m)
                    if s == last:
                        collect(acc, tile)

        behind = None
        for s, landed in slots:
            for g in range(NG):
                if feed and s == slots[0][0] and g == 0:
                    feed(0, hring)
                for f in range(FC):
                    n, ready = first(s, landed, g, f)
                    if feed and s == slots[0][0] and g + 1 < NG and f == 0:
                        feed(g + 1, hring)
                    if between:
                        between()
                    if behind is not None:
                        second(*behind)
                    behind = (s, g, f, n, ready)
        second(*behind)

    def fetch_expert(lane, s, w1, w3, w2, b1, *after):
        to1, to3, to2 = slot(s)
        load(lane, to1, w1.rearrange("(k p) f -> p k f", p=P), *after)
        if w3 is not None:
            load(lane, to3, w3.rearrange("(k p) f -> p k f", p=P))
        if b1 is not None:
            load(lane, bias1[:, s, :], b1.rearrange("(f p) -> p f", p=P), columns=True)
        return load(lane, to2, w2.rearrange("(f p) d -> p f d", p=P))

    def all_experts(acc, fetch, func, gated, xT, gate_of):
        per_turn = 4
        with nc.Fori(0, E // per_turn) as i:
            state = fresh_state()
            landed = {0: None, 1: fetch(dma_b, 1, per_turn * i + 1)}
            for n in range(per_turn):
                experts(acc, [(n % 2, landed[n])], func, gated, xT, lambda s, tile: gate_of(per_turn * i + n, tile),
                        state, last=n % 2 if n == per_turn - 1 else None)
                if n + 2 <= per_turn:
                    landed[n + 2] = fetch((dma_a, dma_b)[n % 2], n % 2, (per_turn * i + n + 2) % E, PE.last(), A.last())
            fence(spare=ahead)
        collected.add(id(acc))


    def feed_input(src, dst, route=None):
        xn_read, read = [None, None], [None] * 4
        waiting = []
        o = psum[:, 7, 0:NT * E].rearrange("p (t e) -> p t e", e=E)

        def product(t, cp):
            PE.wait(cp)
            if route == "bias":
                nc.tensor.matmul(o[:, t, :], ones[0:1, :], b_gate, start=True, stop=False)
            for k in range(KD):
                ins = nc.tensor.matmul(o[:, t, :], dst[:, k, t * P:(t + 1) * P], w_gate[:, k, :],
                                       start=(k == 0 and route != "bias"), stop=(k == KD - 1))
            return PE.mark(ins)

        for t in range(NT):
            par = t % 2
            bank = psum[:, t % 4, 0:D]
            n = normalise(xn[:, par, :], src, t, xn_read[par])
            xn_read[par] = turn(xn[:, par, :], bank, n, read[t % 4])
            read[t % 4] = A(lambda e: e.copy(dst[:, :, t * P:(t + 1) * P], bank.rearrange("p (k c) -> p k c", k=KD)),
                            xn_read[par])
            waiting.append((t, read[t % 4]))
            if route and len(waiting) > 2:
                product(*waiting.pop(0))
        if route:
            for w in waiting:
                m = product(*w)
            V(lambda e: e.tensor_copy(logits[:, :, :], o), m)

    logits = sb("logits", [P, NT, E])
    wide = small[:, 0:4 * NT * E].rearrange("p (n t e) -> p n t e", n=4, e=E)
    w_gate = small[:, 4 * NT * E:4 * NT * E + KD * E].rearrange("p (k e) -> p k e", k=KD)
    b_gate = small[0:1, 4 * NT * E + KD * E:4 * NT * E + KD * E + E]

    def over(v):
        return v.unsqueeze(2).to_broadcast([P, NT, E])

    def first_best(best, scores_, top, order):
        V(lambda e: e.tensor_reduce(top, scores_, AX.X, ALU.max))
        V(lambda e: e.tensor_tensor(best, scores_, over(top), ALU.is_equal))
        V(lambda e: e.tensor_tensor(best, best, order.unsqueeze(1).to_broadcast([P, NT, E]), ALU.mult))
        V(lambda e: e.tensor_reduce(rank[:, :], best, AX.X, ALU.max))
        V(lambda e: e.tensor_tensor(best, best, over(rank[:, :]), ALU.is_equal))

    rank = sb("rank", [P, NT])
    top_a = sb("top_a", [P, NT])
    top_b = sb("top_b", [P, NT])
    order = sb("order", [P, E])

    def descending():
        for e_ in range(E):
            G(lambda e: e.memset(order[:, e_:e_ + 1], float(E - e_)))


    SROW = prep[:, 4096:]

    def routed(K, turns, per_turn, x_rows, y_rows, w1, w3, w2, chosen, gain, gate_of, send, rows_of, meanwhile,
               finished=None):
        total = turns * per_turn
        assert total >= K * NT * P // CHUNK + E - 1 and per_turn % 3 == 0
        flat3 = lambda n, at: SROW[:, at:at + n]
        te = lambda at: SROW[:, at:at + NT * E].rearrange("p (t e) -> p t e", e=E)
        both, place, before, tile_count = te(0), te(128), te(256), te(384)
        per_expert, chunks, first_row, last_chunk = (flat3(E, 512 + E * n) for n in range(4))
        ramp, partition = flat3(8, 544), flat3(1, 552)
        steps = SROW[:, 560:560 + E * 8].rearrange("p (e c) -> p e c", c=8)
        numbers, expert_of = flat3(total, 640), flat3(total, 672)
        passed = SROW[:, 704:704 + total * (E - 1)].rearrange("p (c e) -> p c e", e=E - 1)
        where = flat3(K * NT, 900).rearrange("p (k t) -> p k t", k=K)
        where_i = flat3(K * NT, 940).bitcast(I32).rearrange("p (k t) -> p k t", k=K)
        w_row = flat3(total, 980).bitcast(I32)
        w_row_now = flat3(3, 1010).bitcast(I32)
        earlier = qTt[:, 0, 0, :]
        G.wait(clearing.last())
        G(lambda e: e.affine_select(out=earlier, in_=ones[:, :], compare_op=ALU.is_ge, fill=0.0, base=-1,
                                    pattern=[[1, P]], channel_multiplier=-1))
        if K == 1:
            both = chosen[0]
        else:
            V(lambda e: e.tensor_tensor(both, chosen[0], chosen[1], ALU.add))
        both_flat = both.rearrange("p t e -> p (t e)")
        PE.wait(V.last(), G.last())
        nc.tensor.matmul(psum[:, 0, 0:NT * E], earlier, both_flat, start=True, stop=True)
        nc.tensor.matmul(psum[:, 0, NT * E:2 * NT * E], ones[:, :], both_flat, start=True, stop=True)
        m = PE.mark(nc.tensor.matmul(psum[:, 0, 2 * NT * E:2 * NT * E + 1], earlier, ones[:, 0:1], start=True, stop=True))
        counts = psum[:, 0, :].rearrange("p (n t e) -> p n t e", n=4, e=E)
        V(lambda e: e.tensor_copy(place, counts[:, 0]), m)
        V(lambda e: e.tensor_copy(tile_count, counts[:, 1]))
        V(lambda e: e.tensor_copy(partition, psum[:, 0, 2 * NT * E:2 * NT * E + 1]))
        PE.wait(V.last())
        V(lambda e: e.memset(before[:, 0, :], 0.0))
        for t in range(1, NT):
            V(lambda e: e.tensor_tensor(before[:, t, :], before[:, t - 1, :], tile_count[:, t - 1, :], ALU.add))
        V(lambda e: e.tensor_tensor(per_expert, before[:, NT - 1, :], tile_count[:, NT - 1, :], ALU.add))
        V(lambda e: e.tensor_scalar(ramp, order[:, :], -float(CHUNK), float(E * CHUNK), ALU.mult, ALU.add))
        V(lambda e: e.tensor_tensor(steps, per_expert.unsqueeze(2).to_broadcast([P, E, 8]),
                                    ramp.unsqueeze(1).to_broadcast([P, E, 8]), ALU.is_gt))
        V(lambda e: e.tensor_reduce(chunks, steps, AX.X, ALU.add))
        V(lambda e: e.tensor_copy(last_chunk[:, 0:1], chunks[:, 0:1]))
        for e_ in range(1, E):
            V(lambda e: e.tensor_tensor(last_chunk[:, e_:e_ + 1], last_chunk[:, e_ - 1:e_], chunks[:, e_:e_ + 1], ALU.add))
        V(lambda e: e.tensor_tensor(first_row, last_chunk, chunks, ALU.subtract))
        V(lambda e: e.tensor_scalar(first_row, first_row, float(CHUNK), None, ALU.mult))
        V(lambda e: e.tensor_tensor(place, place, before, ALU.add))
        V(lambda e: e.tensor_tensor(place, place, first_row.unsqueeze(1).to_broadcast([P, NT, E]), ALU.add))
        for k in range(K):
            V(lambda e: e.tensor_tensor(before, place, chosen[k], ALU.mult))
            V(lambda e: e.tensor_reduce(where[:, k, :], before, AX.X, ALU.add))
        V(lambda e: e.tensor_copy(where_i, where))
        for c in range(0, total, 8):
            n = min(8, total - c)
            V(lambda e: e.tensor_scalar(numbers[:, c:c + n], order[:, 0:n], -1.0, float(E + c), ALU.mult, ALU.add))
        V(lambda e: e.tensor_tensor(passed, numbers.unsqueeze(2).to_broadcast([P, total, E - 1]),
                                    last_chunk[:, 0:E - 1].unsqueeze(1).to_broadcast([P, total, E - 1]), ALU.is_ge))
        V(lambda e: e.tensor_reduce(expert_of, passed, AX.X, ALU.add))
        V(lambda e: e.tensor_scalar(expert_of, expert_of, float(P), None, ALU.mult))
        V(lambda e: e.tensor_tensor(expert_of, expert_of, partition.to_broadcast([P, total]), ALU.add))
        V(lambda e: e.tensor_copy(w_row, expert_of))

        by_row = (w1.rearrange("e (p k) f -> (e p) (k f)", k=KD), w3.rearrange("e (p k) f -> (e p) (k f)", k=KD),
                  w2.rearrange("e (p j) d -> (e p) (j d)", j=FC))
        slots = (expert_w[:, 0:3072], weights[:, 0:3072], expert_w[:, 3072:6144])
        flat_inner = inner[:, :, :].rearrange("p t d -> p (t d)")
        rows_in = flat_inner[:, 0:3 * 512].rearrange("p (s n d) -> p s n d", s=3, n=2)
        xT = flat_inner[:, 1536:1536 + 1024].rearrange("p (s k c) -> p s k c", s=2, k=KD)
        y_out = flat_inner[:, 2560:2560 + 1024].rearrange("p (s n d) -> p s n d", s=2, n=2)
        x_chunk = x_rows.rearrange("(c n p) d -> c p n d", n=2, p=P)
        y_chunk = y_rows.rearrange("(c n p) d -> c p n d", n=2, p=P)

        def fetch_weights(s, chunk, *after):
            G(lambda e: e.tensor_copy(w_row_now[:, s:s + 1], w_row[:, bass.ds(chunk, 1)]), *after)
            G.wait(G.last())
            for n in range(3):
                got_ = gather_lanes[s].mark(nc.gpsimd.indirect_dma_start(
                    slots[s][:, n * 1024:(n + 1) * 1024], None, by_row[n],
                    bass.IndirectOffsetOnAxis(w_row_now[:, s:s + 1], 0)))
            return got_

        def fetch_rows(s, chunk, *after):
            return load((dma_a, dma_b, dma_c)[s], rows_in[:, s, :, :], x_chunk[chunk], *after)

        for s in range(2):
            fetch_weights(s, s, V.last())
        for t in range(NT):
            G.wait(rows_of(t))
            for k in range(K):
                sent = gather_lanes[3].mark(nc.gpsimd.indirect_dma_start(
                    x_rows, bass.IndirectOffsetOnAxis(where_i[:, k, t:t + 1], 0), send[:, t, :], None))
        meanwhile()
        for s in range(2):
            fetch_rows(s, s, sent)
        fence()
        with nc.Fori(0, turns) as i:
            ring = Ring([0, 1, 2, 3])
            hid_read = [None] * 4
            state = {"n": 0}
            turned, landed_w, landed_x = {}, {0: None, 1: None}, {0: None, 1: None}
            rows_read, slot_read, xT_read, xT_bank = {}, {}, {}, {}
            y_free, y_stored = {}, {}

            def turn_rows(c):
                s, par = c % 3, c % 2
                bank = psum[:, 6 + par, :]
                PE.wait(landed_x[c], xT_bank.get(c - 2))
                for k in range(KD):
                    for n in range(2):
                        ins = nc.tensor.transpose(bank[:, (2 * k + n) * P:(2 * k + n + 1) * P],
                                                  rows_in[:, s, n, k::KD], ident[:, :])
                rows_read[c] = PE.mark(ins)
                for k in range(KD):
                    r_ = A(lambda e: e.mul(xT[:, par, k, :], bank[:, 2 * k * P:2 * (k + 1) * P],
                                           gain[:, k:k + 1] if gain is not None else 1.0), rows_read[c], xT_read.get(c - 2))
                turned[c] = xT_bank[c] = r_

            def first(c, j):
                s, par = c % 3, c % 2
                bank, free = ring.take()
                PE.wait(free, landed_w[c], turned[c])
                for n in range(2):
                    w = slots[s][:, n * 1024:(n + 1) * 1024].rearrange("p (k f) -> p k f", k=KD)
                    for k in range(KD):
                        ins = nc.tensor.matmul(psum[:, bank, n * CHUNK:(n + 1) * CHUNK], w[:, k, j::FC], xT[:, par, k, :],
                                               start=(k == 0), stop=(k == KD - 1))
                m = xT_read[c] = PE.mark(ins)
                n = state["n"]
                state["n"] += 1
                h, tm = hidden[:, n % 4, 0:CHUNK], gated_tmp[:, n % 2, 0:CHUNK]
                r_ = A(lambda e: e.activation(tm, psum[:, bank, 0:CHUNK], ACT.Silu), m, hid_read[(n - 2) % 4])
                r_ = V(lambda e: e.tensor_tensor(h, psum[:, bank, CHUNK:2 * CHUNK], tm, ALU.mult), r_, hid_read[n % 4])
                ring.give(r_)
                return c, j, n, r_

            def second(c, j, n, ready):
                s, par = c % 3, c % 2
                w = slots[s][:, 2048:3072].rearrange("p (j d) -> p j d", j=FC)
                PE.wait(ready, y_free.get(c - 2))
                for t in range(2):
                    ins = nc.tensor.matmul(psum[:, 4 + par, t * D:(t + 1) * D], hidden[:, n % 4, t * P:(t + 1) * P],
                                           w[:, j, :], start=(j == 0 and t == 0), stop=(j == FC - 1), skip_group_check=True)
                m = hid_read[n % 4] = PE.mark(ins)
                if j == FC - 1:
                    slot_read[c] = m
                    y_free[c] = V(lambda e: e.tensor_copy(y_out[:, par, :, :].rearrange("p n d -> p (n d)"),
                                                          psum[:, 4 + par, :]), m, y_stored.get(c - 2))
                    y_stored[c] = load((dma_d, dma_e)[par], y_chunk[i * per_turn + c], y_out[:, par, :, :], y_free[c])

            turn_rows(0)
            behind = None
            for c in range(per_turn):
                for j in range(FC):
                    now = first(c, j)
                    if behind is not None:
                        second(*behind)
                    behind = now
                    if j == 0:
                        nxt = (i * per_turn + c + 2) % total
                        w_, x_ = fetch_weights((c + 2) % 3, nxt, slot_read.get(c - 1)), \
                            fetch_rows((c + 2) % 3, nxt, rows_read.get(c - 1))
                        if c + 2 < per_turn:
                            landed_w[c + 2], landed_x[c + 2] = w_, x_
                    if j == 2 and c + 1 < per_turn:
                        turn_rows(c + 1)
            second(*behind)
            fence()
        back = (inner, shared[:, 0:NT * D].rearrange("p (t d) -> p t d", t=NT))
        arrived = {}
        for q in range(0, NT, 4):
            for k in range(K):
                lane = gather_lanes[K * (q // 4) + k]
                for t in range(q, q + 4):
                    arrived[k, q] = lane.mark(nc.gpsimd.indirect_dma_start(
                        back[k][:, t, :], None, y_rows, bass.IndirectOffsetOnAxis(where_i[:, k, t:t + 1], 0)))
        for t in range(NT):
            for k in range(K):
                V(lambda e: e.scalar_tensor_tensor(x[:, t, :], back[k][:, t, :], gate_of(k, t), x[:, t, :],
                                                   ALU.mult, ALU.add), arrived[k, t // 4 * 4])
            if finished:
                finished(t, V.last())
            else:
                collect(x, t)
        collected.add(id(x))
        join()

    def clear_rows(*matrices):
        zeros = qTt[:, :, :, :].rearrange("p n k c -> p (n k c)")
        zeroed = V(lambda e: e.memset(zeros, 0.0))
        for dst in matrices:
            view = dst.rearrange("(p n r) d -> p n (r d)", p=P, r=2)
            load(clearing, view, zeros.unsqueeze(1).to_broadcast([P, view.shape[1], 2 * D]), zeroed)

    clear_expanded()
    prepare_wide(wide0)
    V.wait(got_x)
    statistics(x, 1e-5)
    join()
    attention(x, WIDE, 1.0, True, tanh_g[:, 0:1])


    HINGES = 32
    mask = small[:, 0:B * S2].rearrange("p (b s) -> p b s", b=B)
    wth, bth, wto, bto = (small[:, 160 + 32 * n:192 + 32 * n] for n in range(4))
    flat_bias = bias[:, :, :].rearrange("p t s -> p (t s)")
    flat_side = fside[:, :, :].rearrange("p t s -> p (t s)")
    hinge = Kt[:, 0, :, :]

    class Distance:

        def __init__(self, layer):
            def vector_of(name, n):
                return a[name][layer].rearrange("(o n) -> o n", o=1).to_broadcast([P, n])

            load(dma_e, wth, a["L1_xattn_Wth"][layer].to_broadcast([P, HINGES]))
            load(dma_e, bth, vector_of("L1_xattn_bth", HINGES))
            load(dma_e, wto, a["L1_xattn_Wto"][layer].rearrange("k o -> o k").to_broadcast([P, HINGES]), columns=True)
            self.got = load(dma_e, bto[:, 0:1], vector_of("L1_xattn_bto", 1), columns=True)
            self.j, self.used = -1, [None, None]

        def start(self):
            for bt in range(B):
                V(lambda e: e.tensor_scalar(bias[:, bt * TB:(bt + 1) * TB, :],
                                            mask[:, bt, :].unsqueeze(1).to_broadcast([P, TB, S2]),
                                            bto[:, 0:1], None, ALU.add), self.got)

        def step(self):
            j = self.j
            self.j += 1
            if j < 0:
                self.start()
            elif j < HINGES:
                r = hinge[:, j % 2, :]
                m = A(lambda e: e.activation(r, flat_side, ACT.Relu, scale=wth[:, j:j + 1], bias=bth[:, j:j + 1]),
                      self.got, self.used[j % 2])
                self.used[j % 2] = V(lambda e: e.scalar_tensor_tensor(flat_bias, r, wto[:, j:j + 1], flat_bias,
                                                                      ALU.mult, ALU.add), m)

    def quantised_ffn():
        NL, R = 6, 32
        WT = expert_w[:, 0:NL * 2 * D].rearrange("p (j k o) -> p j k o", j=NL, k=KD)
        q = expert_w[:, NL * 2 * D:2 * NL * 2 * D].bitcast(I32).rearrange("p (j h d) -> p j h d", j=NL, h=2)
        z = prep[:, 0:NT * D].rearrange("p (t d) -> p t d", t=NT)
        rest = prep[:, NT * D:]
        sc = rest[:, 0:192].rearrange("p (j h g) -> p j h g", j=NL, h=2)
        lb = rest[:, 192:576].rearrange("p (j h r) -> p j h r", j=NL, h=2)
        la = rest[0:R, 576:2112].rearrange("p (j d) -> p j d", j=NL)
        brow = rest[:, 2112:3648].rearrange("p (j o) -> p j o", j=NL)
        gamma = rest[:, 3648:3654].rearrange("p (b k) -> p b k", b=3)
        beta = rest[:, 3654:3660].rearrange("p (b k) -> p b k", b=3)
        wf = rest[:, 3660:3660 + 2 * D].rearrange("p (n d) -> p n d", n=2)
        lbT = rest[0:R, 3660 + 2 * D:3660 + 2 * D + 2 * P].rearrange("p (n c) -> p n c", n=2)
        l_q = load(dma_a, q, a["L0_ffn_qweights"].rearrange("j (h p) d -> p j h d", p=P))
        load(dma_b, sc, a["L0_ffn_scales"].rearrange("j (h p) g -> p j h g", p=P))
        load(dma_b, lb, a["L0_ffn_lora_b"].rearrange("j (h p) r -> p j h r", p=P))
        load(dma_b, la, a["L0_ffn_lora_a"].rearrange("j r d -> r j d"))
        load(dma_b, brow, a["L0_ffn_biases"].rearrange("(o j) d -> o j d", o=1).to_broadcast([P, NL, D]))
        for blk in range(3):
            load(dma_b, gamma[:, blk, :], a["L0_ffn_ln_gamma"][blk].rearrange("(k p) -> p k", p=P), columns=True)
            l_s = load(dma_b, beta[:, blk, :], a["L0_ffn_ln_beta"][blk].rearrange("(k p) -> p k", p=P), columns=True)
        statistics(x, 1e-5)
        for t in range(NT):
            normalise(inner[:, t, :], x, t)
        ring = Ring([0, 1, 2, 3, 4, 5, 6, 7])
        V.wait(l_q, l_s)
        PE.wait(l_s)
        lb_read, wf_read = [None, None], [None, None]
        for n in range(2 * NL):
            j, h, i = n // 2, n % 2, n % 2
            bank, free = ring.take()
            PE.wait(free)
            m = PE.mark(nc.tensor.transpose(psum[0:R, bank, 0:P], lb[:, j, h, :], ident[:, :]))
            cp = A(lambda e: e.copy(lbT[:, i, :], psum[0:R, bank, 0:P]), m, lb_read[i])
            PE.wait(cp)
            lora = PE.mark(nc.tensor.matmul(psum[:, bank, D:2 * D], lbT[:, i, :], la[:, j, :], start=True, stop=True))
            lb_read[i] = lora
            V(lambda e: e.tensor_scalar(wf[:, i, :], q[:, j, h, :], 1.0 / 7.5, -1.0, ALU.mult, ALU.add), wf_read[i])
            w3d = wf[:, i, :].rearrange("p (g c) -> p g c", g=16)
            V(lambda e: e.tensor_tensor(w3d, w3d, sc[:, j, h, :].unsqueeze(2).to_broadcast([P, 16, 16]), ALU.mult))
            w = V(lambda e: e.tensor_tensor(wf[:, i, :], psum[:, bank, D:2 * D], wf[:, i, :], ALU.add), lora)
            tr = turn(wf[:, i, :], psum[:, bank, 0:D], w)
            wf_read[i] = tr
            ring.give(A(lambda e: e.copy(WT[:, j, :, h * P:(h + 1) * P],
                                         psum[:, bank, 0:D].rearrange("p (k c) -> p k c", k=KD)), tr))
        fence()
        with nc.Fori(0, 3) as blk:
            turned_tile = [xnTt[:, 0], xnTt[:, 1], qTt[:, 0], qTt[:, 1]]
            for layer in range(2):
                ring = Ring([0, 1, 2, 3, 4, 5, 6, 7])
                lhs_read = [None] * 4
                waiting = []

                def product(t, bank, cp):
                    PE.wait(cp)
                    y = psum[:, bank, D:2 * D]
                    for k in range(KD):
                        ins = nc.tensor.matmul(y, turned_tile[t % 4][:, k, :], WT[:, 2 * blk + layer, k, :],
                                               start=(k == 0), stop=(k == KD - 1))
                    m = PE.mark(ins)
                    lhs_read[t % 4] = m
                    if layer == 0:
                        ring.free[bank] = V(lambda e: e.tensor_tensor(z[:, t, :], y, brow[:, 2 * blk, :], ALU.add), m)
                        V(lambda e: e.bn_stats(bn6[:, t, :], z[:, t, :]))
                        G(lambda e: e.tensor_tensor(inner[:, t, :], inner[:, t, :], brow[:, 2 * blk + 1, :], ALU.add), m)
                        V(lambda e: e.bn_aggr(meanvar[:, t, :], bn6[:, t, :]))
                    else:
                        ring.free[bank] = V(lambda e: e.tensor_tensor(inner[:, t, :], y, inner[:, t, :], ALU.add), m, G.last())

                for t in range(NT):
                    bank, free = ring.take()
                    if layer == 0:
                        tr = turn(inner[:, t, :], psum[:, bank, 0:D], free)
                        cp = A(lambda e: e.copy(turned_tile[t % 4].rearrange("p k c -> p (k c)"), psum[:, bank, 0:D]),
                               tr, lhs_read[t % 4])
                    else:
                        n = V(lambda e: e.tensor_scalar(z[:, t, :], z[:, t, :], meanvar[:, t, 0:1], rstd[:, t:t + 1],
                                                        ALU.subtract, ALU.mult))
                        tr = turn(z[:, t, :], psum[:, bank, 0:D], n, free)
                        for k in range(KD):
                            cp = A(lambda e: e.activation(turned_tile[t % 4][:, k, :], psum[:, bank, k * P:(k + 1) * P],
                                                          ACT.Gelu, bias=beta[:, bass.ds(blk, 1), k],
                                                          scale=gamma[:, bass.ds(blk, 1), k]), tr, lhs_read[t % 4])
                    waiting.append((t, bank, cp))
                    if len(waiting) > 2:
                        product(*waiting.pop(0))
                for w in waiting:
                    product(*w)
                if layer == 0:
                    reciprocal_root(meanvar[:, :, 1], 1e-5, None)
            fence()
        for t in range(NT):
            V(lambda e: e.scalar_tensor_tensor(x[:, t, :], inner[:, t, :], tanh_g[:, 4:5], x[:, t, :],
                                               ALU.mult, ALU.add))
            collect(x, t)
        collected.add(id(x))
        join()

    wq4, wk4, wv4 = (a["L1_xattn_" + n].rearrange("l (k p) n h -> l p k (n h)", p=P) for n in ("Wq", "Wk", "Wv"))
    wo4 = a["L1_xattn_Wo"].rearrange("l n h d -> l (n h) d").rearrange("l (t p) d -> l p t d", p=P)
    fetch_wide([ahead] * 4, wq4[0], wk4[0], wv4[0], wo4[0])
    quantised_ffn()
    join()

    rep = weights[0:16, 0:3 * P].rearrange("p (n h c) -> p n h c", n=3, h=8)
    raw = weights[0:16, 3 * P:3 * P + 48].rearrange("p (n c) -> p n c", n=3)
    bd = weights[:, 512:512 + 2 * P].rearrange("p (n c) -> p n c", n=2)
    wo_rows = weights[:, 1024:1024 + KD * D].rearrange("p (k d) -> p k d", k=KD)
    woT = weights[:, 2048:2048 + KD * D].rearrange("p (k d) -> p k d", k=KD)
    bo = weights[:, 3072:3072 + D]
    mask_i = prep[:, 7000:7000 + NT * S2].bitcast(I32).rearrange("p (t s) -> p t s", t=NT)

    def fetch_shared_head():
        for n, name in enumerate(("Wk", "Wq", "Wv")):
            load(ahead, raw[:, n, :], a["L2_xattn_" + name])
        load(ahead, wo_rows, a["L2_xattn_Wo"].rearrange("(k p) d -> p k d", p=P))
        load(ahead, bo, bcast(a["L2_xattn_bo"], D))
        load(ahead, mask_i, a["mask_Bx1xSxS2_ik1"][:, 0].rearrange("b (t p) s -> p (b t) s", p=P))

    def fetch_gelu_expert(lane, s, e, *after):
        return fetch_expert(lane, s, a["L1_ffn_w1"][e], None, a["L1_ffn_w2"][e], a["L1_ffn_b1"][e], *after)

    rms_w = sb("rms_w", [P, E])

    def gate_inputs():
        load(dma_b, small[0:E, 600:600 + D], a["L1_ffn_gate_w"])
        load(dma_b, rms_w[:, :], bcast(a["L1_ffn_rms_w"], E))
        load(dma_b, b_gate, a["L1_ffn_gate_b"].rearrange("(o e) -> o e", o=1))
        fetch_gelu_expert(ahead, 0, 0)

    def decoder():
        load(dma_e, mask, a["mask_Bx1x1xS2_ff0"].rearrange("b x y s -> (x y) b s").to_broadcast([P, B, S2]))
        first_distance = Distance(0)
        statistics(x, 1e-5)
        for t in range(NT):
            normalise(inner[:, t, :], x, t)
            collect(inner, t)
        collected.add(id(inner))
        clear_expanded()
        for _ in range(HINGES + 1):
            first_distance.step()
        fence()
        with nc.Fori(0, 4) as layer:
            nxt = (layer + 1) % 4
            b2 = small[:, 320:320 + D]
            load(dma_a, b2, a["L1_xattn_bf2"][layer].rearrange("(o n) -> o n", o=1).to_broadcast([P, D]))
            prepare_wide()
            statistics(inner, None, 1e-6)
            join()
            for h in range(2):
                fetch_expert(ahead, h, a["L1_xattn_Wf1"][layer][:, h * F:(h + 1) * F], None,
                             a["L1_xattn_Wf2"][layer][h * F:(h + 1) * F, :], a["L1_xattn_bf1"][layer][h * F:(h + 1) * F])
            attention(inner, WIDE, 1.0, True, 1.0)
            statistics(inner, None, 1e-6)
            join()
            fetch_wide([ahead] * 4, wq4[nxt], wk4[nxt], wv4[nxt], wo4[nxt])
            distance = Distance(nxt)
            xn_read = [None, None]

            def feed(g, ring):
                for t in range(g * TG, (g + 1) * TG):
                    par = t % 2
                    bank, fr = ring.take()
                    n = normalise(xn[:, par, :], inner, t, xn_read[par])
                    xn_read[par] = turn(xn[:, par, :], psum[:, bank, 0:D], n, fr)
                    ring.give(A(lambda e: e.copy(xnT[:, :, t * P:(t + 1) * P],
                                                 psum[:, bank, 0:D].rearrange("p (k c) -> p k c", k=KD)), xn_read[par]))
                    V(lambda e: e.tensor_tensor(inner[:, t, :], inner[:, t, :], b2, ALU.add))
                PE.wait(A.last())

            experts(inner, [(0, None), (1, None)], ACT.Relu, False, lambda s: xnT, lambda s, tile: 1.0,
                    last=1, feed=feed, between=distance.step)
            while distance.j < HINGES:
                distance.step()
            fence()
        gate_inputs()
        statistics(inner, None, 1e-6)
        for t in range(NT):
            par = t % 2
            normalise(xn[:, par, :], inner, t)
            V(lambda e: e.scalar_tensor_tensor(x[:, t, :], xn[:, par, :], tanh_g[:, 1:2], x[:, t, :], ALU.mult, ALU.add))
            collect(x, t)
        collected.add(id(x))
        join()

    decoder()

    def one_gate_experts():
        gw = small[0:E, 600:600 + D]
        b2 = small[0:E, 600:600 + D]
        fetch = fetch_gelu_expert
        got = None
        for k in range(KD):
            PE.wait(got)
            m = PE.mark(nc.tensor.transpose(psum[:, k, 0:E], gw[:, k * P:(k + 1) * P], ident[0:E, 0:E]))
            A(lambda e: e.copy(w_gate[:, k, :], psum[:, k, 0:E]), m)
        statistics(x, 1e-5)
        feed_input(x, xnT, "bias")
        got = load(dma_b, b2, a["L1_ffn_b2"], PE.last())
        sq = wide[:, 0]
        V(lambda e: e.tensor_tensor(sq, logits[:, :, :], logits[:, :, :], ALU.mult))
        V(lambda e: e.tensor_reduce(top_a[:, :], sq, AX.X, ALU.add))
        V(lambda e: e.tensor_scalar(top_a[:, :], top_a[:, :], 1.0 / E, float(np.finfo(np.float32).eps), ALU.mult, ALU.add))
        A(lambda e: e.activation(top_a[:, :], top_a[:, :], ACT.Sqrt), V.last())
        V(lambda e: e.reciprocal(top_a[:, :], top_a[:, :]), A.last())
        V(lambda e: e.tensor_tensor(sq, logits[:, :, :], over(top_a[:, :]), ALU.mult))
        V(lambda e: e.tensor_tensor(sq, sq, rms_w[:, :].unsqueeze(1).to_broadcast([P, NT, E]), ALU.mult))
        V(lambda e: e.tensor_reduce(top_b[:, :], sq, AX.X, ALU.max))
        V(lambda e: e.tensor_tensor(sq, sq, over(top_b[:, :]), ALU.subtract))
        A(lambda e: e.activation(sq, sq, ACT.Exp, scale=2.0), V.last())
        V(lambda e: e.tensor_reduce(top_a[:, :], sq, AX.X, ALU.add), A.last())
        V(lambda e: e.reciprocal(top_a[:, :], top_a[:, :]))
        V(lambda e: e.tensor_scalar(top_b[:, :], top_a[:, :], 1e-6, None, ALU.add))
        V(lambda e: e.reciprocal(top_b[:, :], top_b[:, :]))
        V(lambda e: e.tensor_tensor(top_a[:, :], top_a[:, :], top_b[:, :], ALU.mult))
        V(lambda e: e.tensor_scalar(gates[:, :, 0], top_a[:, :], tanh_g[:, 5:6], None, ALU.mult))
        PE.wait(got)
        m = PE.mark(nc.tensor.matmul(psum[:, 0, 0:D], ones[0:E, :], b2, start=True, stop=True))
        for t in range(NT):
            V(lambda e: e.scalar_tensor_tensor(x[:, t, :], psum[:, 0, 0:D], gates[:, t, 0:1], x[:, t, :],
                                               ALU.mult, ALU.add), m)
        fence()
        fetch_shared_head()
        all_experts(x, fetch, ACT.Gelu, False, lambda s: xnT, lambda e, tile: gates[:, tile, 0:1])

    L2_rows, L3_rows = ([scratch(f"{layer}_{what}", (chunks_ * CHUNK, D)) for what in ("sorted", "results")]
                        for layer, chunks_ in (("L2", 15), ("L3", 24)))
    clear_rows(L2_rows[0], L3_rows[0])
    one_gate_experts()

    def block_diagonal(dst, lhs, rhs, bank, landed):
        PE.wait(landed)
        m = PE.mark(nc.tensor.matmul(psum[:, bank, 0:P], lhs, rhs, start=True, stop=True))
        b3 = block[:, :].unsqueeze(2).to_broadcast([P, 8, 16])
        V(lambda e: e.tensor_tensor(dst.rearrange("p (h c) -> p h c", h=8),
                                    psum[:, bank, 0:P].rearrange("p (h c) -> p h c", h=8), b3, ALU.mult), m)

    def shared_head_attention():
        got = got_o = got_m = None
        statistics(x, 1e-5)
        V(lambda e: e.tensor_scalar(bias[:, :, :], mask_i, 0.0, -1e20, ALU.is_equal, ALU.mult), got_m)
        for n in range(3):
            V(lambda e: e.tensor_copy(rep[:, n, :, :], raw[:, n, :].unsqueeze(1).to_broadcast([16, 8, 16])), got)
        wide_rep = rep[:, :, :, :].rearrange("p n h c -> p n (h c)")
        block_diagonal(bd[:, 0, :], wide_rep[:, 0, :], wide_rep[:, 1, :], 0, V.last())
        eye = weights[0:16, 3400:3400 + P].rearrange("p (h c) -> p h c", h=8)
        V(lambda e: e.tensor_copy(eye, ident[0:16, 0:16].unsqueeze(1).to_broadcast([16, 8, 16])))
        block_diagonal(bd[:, 1, :], wide_rep[:, 2, :], eye.rearrange("p h c -> p (h c)"), 1, V.last())
        for k in range(KD):
            PE.wait(got_o)
            for o in range(KD):
                ins = nc.tensor.transpose(psum[:, 2 + k, o * P:(o + 1) * P], wo_rows[:, o, k * P:(k + 1) * P], ident[:, :])
            turned_ = V(lambda e: e.tensor_copy(woT[:, k, :], psum[:, 2 + k, 0:D]), PE.mark(ins))

        def projection(n):
            def of(dst, g):
                PE.wait(V.last())
                return PE.mark(nc.tensor.matmul(dst, bd[:, n, :], ctxT[:, g, :], start=True, stop=True))
            return of
        prepare_narrow(projection(0), projection(1), woT, turned_, None, bo)
        join()
        attention(x, NARROW, 1.0 / 16.0, True, tanh_g[:, 2:3])

    join()
    shared_head_attention()

    def best_expert():
        x_rows, y_rows = L2_rows
        fetch_expert(ahead, 1, a["L2_ffn_sh_gate"], a["L2_ffn_sh_up"], a["L2_ffn_sh_down"], None)
        descending()
        got = load(dma_b, w_gate, a["L2_ffn_gate_w"].rearrange("(k p) e -> p k e", p=P))
        statistics(x, 1e-5)
        V.wait(G.last())
        PE.wait(got)
        feed_input(x, xnT, "plain")
        best = wide[:, 0]
        first_best(best, logits[:, :, :], top_a[:, :], order[:, :])
        A(lambda e: e.activation(top_a[:, :], top_a[:, :], ACT.Exp, scale=-1.0), V.last())
        V(lambda e: e.tensor_scalar(top_a[:, :], top_a[:, :], 1.0, None, ALU.add), A.last())
        V(lambda e: e.reciprocal(top_a[:, :], top_a[:, :]))
        V(lambda e: e.tensor_tensor(rstd[:, :], rstd[:, :], top_a[:, :], ALU.mult))
        join()
        routed(1, 5, 3, x_rows, y_rows, a["L2_ffn_rt_gate"], a["L2_ffn_rt_up"], a["L2_ffn_rt_down"], [best], None,
               lambda k, t: tanh_g[:, 6:7], inner, lambda t: normalise(inner[:, t, :], x, t),
               lambda: experts(x, [(1, None)], ACT.Silu, True, lambda s: xnT, lambda s, tile: tanh_g[:, 6:7]))

    best_expert()

    def biased_attention():
        w = [weights[:, n * KD * D:(n + 1) * KD * D].rearrange("p (k d) -> p k d", k=KD) for n in range(4)]
        kv_bias = weights[:, 2400:2404]
        bq = weights[:, 2404:2406]
        bo = weights[:, 2410:2410 + D]
        for n, name in enumerate(("Wq", "Wk", "Wv", "Wo")):
            got = load(dma_a, w[n], a["L3_xattn_" + name].rearrange("(k p) d -> p k d", p=P))
        for g in range(KD):
            for n, name in enumerate(("bk", "bv")):
                load(dma_b, kv_bias[:, 2 * g + n:2 * g + n + 1],
                     a["L3_xattn_" + name][g * P:(g + 1) * P].rearrange("(p o) -> p o", o=1), columns=True)
            load(dma_b, bq[:, g:g + 1], a["L3_xattn_bq"][g * P:(g + 1) * P].rearrange("(p o) -> p o", o=1), columns=True)
        got_b = load(dma_b, bo, bcast(a["L3_xattn_bo"], D))
        statistics(x, 1e-5)
        V.wait(got_b, got)

        def projection(n):
            def of(dst, g):
                PE.wait(got)
                for k in range(KD):
                    ins = nc.tensor.matmul(dst, w[n][:, k, g * P:(g + 1) * P], ctxT[:, k, :], start=(k == 0), stop=(k == KD - 1))
                return PE.mark(ins)
            return of
        prepare_narrow(projection(1), projection(2), w[3], got, kv_bias, bo)
        join()
        q_read = [None, None]

        def project(par, so, after):
            PE.wait(after)
            for g in range(KD):
                for k in range(KD):
                    ins = nc.tensor.matmul(so[:, g * P:(g + 1) * P], w[0][:, k, g * P:(g + 1) * P], xnTt[:, par, k, :],
                                           start=(k == 0), stop=(k == KD - 1))
            m = PE.mark(ins)
            for g in range(KD):
                r = A(lambda e: e.activation(qTt[:, par, g, :], so[:, g * P:(g + 1) * P], ACT.Identity,
                                             bias=bq[:, g:g + 1]), m)
            return r
        attention(x, NARROW, 0.25, False, tanh_g[:, 3:4], project=project)

    biased_attention()

    def latent_block():
        L = H * HD3
        EPS = 1e-5
        PARTS = 3
        STACK = PARTS * PARTS * HD3
        ROWS = STACK + PARTS
        SLOTS, TURN = 4, H
        q_dram = scratch("q_heads", (B * H, PARTS, HD3, S), BF16)
        qk_parts = scratch("qk_parts", (2, PARTS, B * H, HD3, S), BF16)
        k_dram = scratch("k_heads", (B * H, PARTS, PARTS, HD3, S), BF16)
        heads = weights[0:ROWS, 0:SLOTS * S].bitcast(BF16).rearrange("p (n s c) -> p n s c", n=2, s=SLOTS)
        values = weights[:, 4096:4096 + NT * H * 9].rearrange("p (t h c) -> p t h c", t=NT, h=H)
        small_w = weights[:, 6400:8192]
        PT_COLS = sum(S - j * P for j in range(TB))
        expT = prep[:, 0:2 * PT_COLS].rearrange("p (n c) -> p n c", n=2)
        Kflat = Kt[:, :, :, :].rearrange("p b k c -> p (b k c)")
        Vflat = Vt[:, :, :, :].rearrange("p b c d -> p (b c d)")
        cosT, sinT = Kflat[:, 0:S], Kflat[:, S:2 * S]
        masks = Kflat[:, 2 * S:2 * S + 192].bitcast(BF16).rearrange("p (n c) -> p n c", n=3)
        causal, causalT, ident16 = (masks[:, n, :] for n in range(3))
        mrow = Kflat[0:TB, 3 * S:3 * S + 2 * P].rearrange("p (n c) -> p n c", n=2)
        mparts = Kflat[0:TB, 3 * S + 2 * P:3 * S + 5 * P].bitcast(BF16).rearrange("p (n a c) -> p n a c", n=2, a=PARTS)
        head_values = Kflat[:, 4 * S + P:4 * S + P + 2 * TB * 9].rearrange("p (n t c) -> p n t c", n=2, c=9)
        sums = Vflat[0:9, 0:2 * S].rearrange("p (n c) -> p n c", n=2)
        qT, kT = Vflat[:, 0:NT * P], Vflat[:, NT * P:2 * NT * P]
        cT = prep[:, 6144:6144 + NT * P].rearrange("p (g c) -> p g c", g=NG)
        wd = prep[:, 0:KD * L].rearrange("p (k l) -> p k l", k=KD)
        wqkv = prep[:, 256:256 + 5 * L].rearrange("p (n l) -> p n l", n=5)
        w_up = small_w[:, 0:D]
        gain = small_w[:, 256:260].rearrange("p (n k) -> p n k", n=2)
        rope = prep[:, 1024:1024 + 4 * GRP].rearrange("p (n c) -> p n c", n=4)
        split = prep[:, 3072:3072 + 2 * PARTS * S].bitcast(BF16).rearrange("p (n a c) -> p n a c", n=2, a=PARTS)
        attended = shared[:, 0:NT * L].rearrange("p (t l) -> p t l", t=NT)
        maxima = row[:, :, 0:TB]
        shares = row[:, :, 16:16 + TB]

        load(dma_a, cosT, a["rope_cos"])
        load(dma_a, sinT, a["rope_sin"])
        load(dma_b, wd, a["L3_ffn_w_down"].rearrange("(k p) l -> p k l", p=P))
        for n, name in enumerate(("wq", "wk", "wv")):
            load(dma_b, wqkv[:, n, :], a["L3_ffn_" + name])
        load(dma_b, w_up, a["L3_ffn_w_up"])
        for n, name in enumerate(("g1", "g2")):
            got = load(dma_b, gain[:, n, :], a["L3_ffn_" + name].rearrange("(k p) -> p k", p=P), columns=True)
        load(dma_c, w_gate, a["L3_ffn_router_w"].rearrange("(k p) e -> p k e", p=P))
        descending()
        for mask_, sign in ((causal, 1), (causalT, -1)):
            G(lambda e: e.memset(mask_, 0.0))
            G(lambda e: e.affine_select(out=mask_, in_=mask_, compare_op=ALU.is_ge, fill=NEG, base=0,
                                        pattern=[[-sign, P]], channel_multiplier=sign))
        G(lambda e: e.tensor_copy(ident16, ident[:, :]))
        G(lambda e: e.memset(values[:, :, :, :].rearrange("p t h c -> p (t h c)"), 1.0))
        G(lambda e: e.memset(heads[:, 1, :, :].rearrange("p s c -> p (s c)"), 1.0))
        statistics(x, 1e-5)
        for t in range(NT):
            normalise(inner[:, t, :], x, t)
            collect(inner, t)
        collected.add(id(inner))

        def mean_square_statistics():
            statistics(inner, EPS)
            sq = top_a[:, :]
            V(lambda e: e.tensor_tensor(sq, meanvar[:, :, 0], meanvar[:, :, 0], ALU.mult))
            V(lambda e: e.tensor_tensor(meanvar[:, :, 1], meanvar[:, :, 1], sq, ALU.add))
            reciprocal_root(meanvar[:, :, 1], EPS, None)
            V(lambda e: e.memset(meanvar[:, :, 0], 0.0))

        mean_square_statistics()
        for n in range(2):
            w = wqkv[:, n, :].rearrange("p (j two) -> p j two", two=2)
            sw = wqkv[:, 3 + n, :].rearrange("p (j two) -> p j two", two=2)
            V(lambda e: e.tensor_scalar(sw[:, :, 0], w[:, :, 1], -1.0, None, ALU.mult), got)
            V(lambda e: e.tensor_scalar(sw[:, :, 1], w[:, :, 0], 1.0, None, ALU.mult))
        for k in range(KD):
            V(lambda e: e.tensor_scalar(wd[:, k, :], wd[:, k, :], gain[:, 0, k:k + 1], None, ALU.mult))
        PE.wait(got, V.last())
        A.wait(G.last())
        feed_input(inner, xnT)
        PE.wait(A.last(), V.last())
        bank_read = [None, None]
        for g in range(NG):
            for k in range(KD):
                ins = nc.tensor.matmul(psum[:, g, :], wd[:, k, :], xnT[:, k, g * GRP:(g + 1) * GRP],
                                       start=(k == 0), stop=(k == KD - 1))
            cp = A(lambda e: e.copy(cT[:, g, :], psum[:, g, :]), PE.mark(ins))
        PE.wait(cp)
        pair_read = [None] * 3
        for g in range(NG):
            at = (g * GRP) % S
            for n, dst in enumerate((qT, kT)):
                pair = (2 * g + n) % 3
                PE.wait(pair_read[pair])
                for i, w in enumerate(((0, 3), (1, 4))[n]):
                    m = PE.mark(nc.tensor.matmul(psum[:, 2 * pair + i, :], wqkv[:, w, :], cT[:, g, :], start=True, stop=True))
                V(lambda e: e.tensor_tensor(rope[:, 2 * n, :], psum[:, 2 * pair, :], cosT[:, at:at + GRP], ALU.mult), m)
                pair_read[pair] = V(lambda e: e.tensor_tensor(rope[:, 2 * n + 1, :], psum[:, 2 * pair + 1, :],
                                                              sinT[:, at:at + GRP], ALU.mult))
                V(lambda e: e.tensor_tensor(dst[:, g * GRP:(g + 1) * GRP], rope[:, 2 * n, :], rope[:, 2 * n + 1, :], ALU.add))
            PE.wait(bank_read[g % 2])
            for t in range(TG):
                mv = PE.mark(nc.tensor.matmul(psum[:, 6 + g % 2, t * P:(t + 1) * P], cT[:, g, t * P:(t + 1) * P],
                                              wqkv[:, 2, :], start=True, stop=True))
            bank_read[g % 2] = A(lambda e: e.copy(values[:, g * TG:(g + 1) * TG, :, 0:HD3],
                                                  psum[:, 6 + g % 2, :].rearrange("p (t h c) -> p t h c", t=TG, h=H)), mv)
        for n, src in enumerate((qT, kT)):
            for a_ in range(PARTS):
                part = A(lambda e: e.copy(split[:, n, a_, :], src), V.last())
                if a_ < PARTS - 1:
                    V(lambda e: e.tensor_tensor(src, src, split[:, n, a_, :], ALU.subtract), part)
            for a_ in range(PARTS):
                for bt in range(B):
                    stored = load(dma_a, qk_parts[n, a_, bt * H:(bt + 1) * H].rearrange("h c s -> (h c) s"),
                                  split[:, n, a_, bt * S:(bt + 1) * S], part)
        by_head = [qk_parts[n].rearrange("a h c s -> h a (c s)") for n in range(2)]
        load(dma_b, q_dram.rearrange("h a c s -> h a (c s)"), by_head[0], stored)
        for b_ in range(PARTS):
            load(dma_b, k_dram[:, :, b_].rearrange("h a c s -> h a (c s)"), by_head[1])
        join()

        def fetch_head(slot_, index, *after):
            lane = more_lanes[slot_]
            load(lane, heads[0:STACK, 1, slot_, :], k_dram[index].rearrange("a b c s -> (a b c) s"), *after)
            for a_ in range(PARTS):
                got_ = load(lane, heads[a_ * PARTS * HD3:(a_ + 1) * PARTS * HD3, 0, slot_, :],
                            q_dram[index].rearrange("b c s -> (b c) s"))
            return got_

        for s in range(3):
            fetch_head(s, s)
        fence()
        start = [sum(S - i * P for i in range(j)) for j in range(TB)]
        with nc.Fori(0, B * H // TURN) as i:
            free = [None, None]
            ring = Ring([4, 5])
            landed = {0: None, 1: None, 2: None}
            values_read, sums_read, exp_read, out_free = [None, None], [None, None], [None, None], None
            state = {"n": 0, "out_free": None}

            def score_maximum(h, t):
                s, n = h % SLOTS, state["n"]
                state["n"] += 1
                cols, base = (t + 1) * P, (n % 2) * 2 * BANK
                PE.wait(free[n % 2], landed[h])
                for at in range(0, cols, BANK):
                    w = min(BANK, cols - at)
                    ins = nc.tensor.matmul(flat[:, base + at:base + at + w], heads[0:STACK, 0, s, t * P:(t + 1) * P],
                                           heads[0:STACK, 1, s, at:at + w], start=True, stop=True)
                m = PE.mark(nc.tensor.matmul(flat[:, base + t * P:base + cols], ident16, causal, start=False, stop=True,
                                             skip_group_check=True))
                free[n % 2] = V(lambda e: e.tensor_reduce(maxima[:, h % 2, t:t + 1], flat[:, base:base + cols], AX.X, ALU.max), m,
                                maxima_read.get(h - 2))
                maximum_known[h] = free[n % 2]

            maximum_known, maxima_read = {}, {}

            def maxima_rows(h):
                bank, fr = ring.take()
                PE.wait(maximum_known[h], fr)
                tr = PE.mark(nc.tensor.transpose(psum[0:TB, bank, 0:P], maxima[:, h % 2, :], ident[:, :]))
                maxima_read[h] = tr
                left = mrow[:, h % 2, :]
                r = A(lambda e: e.mul(left, psum[0:TB, bank, 0:P], -1.0), tr)
                ring.give(r)
                A.wait(rows.get(h - 2))
                for a_ in range(PARTS):
                    r = A(lambda e: e.copy(mparts[:, h % 2, a_, :], left), V.last())
                    if a_ < PARTS - 1:
                        V(lambda e: e.tensor_tensor(left, left, mparts[:, h % 2, a_, :], ALU.subtract), r)
                for a_ in range(PARTS):
                    got_ = load((dma_c, dma_d)[h % 2], heads[STACK + a_:STACK + a_ + 1, 0, h % SLOTS, :],
                                mparts[:, h % 2, a_, :], r)
                return got_

            def exponentials(h, j, rows_landed):
                s = h % SLOTS
                for at in range(j * P, S, BANK):
                    w = min(BANK, S - at)
                    bank, fr = ring.take()
                    PE.wait(rows_landed, fr)
                    m = PE.mark(nc.tensor.matmul(psum[:, bank, 0:w], heads[:, 1, s, j * P:(j + 1) * P],
                                                 heads[:, 0, s, at:at + w], start=True, stop=True))
                    to = start[j] + at - j * P
                    if at == j * P:
                        m = PE.mark(nc.tensor.matmul(psum[:, bank, 0:P], ident16, causalT, start=False, stop=True,
                                                     skip_group_check=True))
                    ring.give(A(lambda e: e.activation(expT[:, h % 2, to:to + w], psum[:, bank, 0:w], ACT.Exp,
                                                       scale=float(HD3) ** -0.5), m, exp_read[h % 2]))

            def weigh(h, keys, done_exp):
                p_ = h % 2
                PE.wait(done_exp, vals[p_])
                if keys[0] == 0:
                    PE.wait(sums_read[0])
                for j in keys:
                    for lo, hi in ((0, BANK), (BANK, S)):
                        lo = max(lo, j * P)
                        if lo < hi:
                            ins = nc.tensor.matmul(flat[0:9, 6 * BANK + lo:6 * BANK + hi], head_values[:, p_, j, :],
                                                   expT[:, p_, start[j] + lo - j * P:start[j] + hi - j * P],
                                                   start=(j == 0), stop=(j == TB - 1 or (hi == BANK and j == 3)))
                return PE.mark(ins)

            def keep_sums(h, m):
                p_ = h % 2
                sums_read[0] = A(lambda e: e.copy(sums[:, p_, :], flat[0:9, 6 * BANK:8 * BANK]), m, sums_read[1])

            def divide(h):
                p_ = h % 2
                bank, fr = ring.take()
                PE.wait(sums_read[0], fr)
                o = psum[:, bank, 0:TB * 9].rearrange("p (t c) -> p t c", c=9)
                for t in range(TB):
                    ins = nc.tensor.transpose(o[:, t, :], sums[:, p_, t * P:(t + 1) * P], ident[0:9, 0:9])
                m = PE.mark(ins)
                sums_read[1] = m
                V(lambda e: e.reciprocal(shares[:, p_, :], o[:, :, HD3]), m)
                dst = attended.rearrange("p (b t) (h c) -> p b t h c", b=B, h=H)[:, i // (H // TURN), :,
                                                                                 (i * TURN + h) % H, :]
                ring.give(V(lambda e: e.tensor_tensor(dst, o[:, :, 0:HD3],
                                                      shares[:, p_, :].unsqueeze(2).to_broadcast([P, TB, HD3]), ALU.mult)))

            vals = [None, None]

            def take_values(h):
                vals[h % 2] = G(lambda e: e.tensor_copy(
                    head_values[:, h % 2, :, :],
                    values.rearrange("p (b t) h c -> p b t h c", b=B)[:, i // (H // TURN), :, (i * TURN + h) % H, :]),
                    values_read[h % 2])

            rows, done_exp = {}, {}
            for h in range(2):
                for t in range(TB):
                    score_maximum(h, t)
                rows[h] = maxima_rows(h)
            for h in range(TURN + 1):
                if h < TURN:
                    nxt = fetch_head((h + 3) % SLOTS, (i * TURN + h + 3) % (B * H), PE.last())
                    if h + 3 < TURN:
                        landed[h + 3] = nxt
                    take_values(h)
                for j in range(TB):
                    if h < TURN:
                        exponentials(h, j, rows[h])
                    if h + 2 < TURN:
                        score_maximum(h + 2, j)
                    if h >= 1:
                        m = weigh(h - 1, (j,), done_exp[h - 1])
                    if j == 0 and 2 <= h + 1 < TURN:
                        rows[h + 1] = maxima_rows(h + 1)
                    if j == 3 and h >= 2:
                        divide(h - 2)
                if h < TURN:
                    done_exp[h] = A.last()
                if h >= 1:
                    exp_read[(h - 1) % 2] = values_read[(h - 1) % 2] = m
                    keep_sums(h - 1, m)
            divide(TURN - 1)
            fence()

        oT = prep[:, 0:2 * GRP].rearrange("p (n c) -> p n c", n=2)
        copied, y_read, oT_read = {}, [None, None], {}
        for g in range(NG + 1):
            if g < NG:
                PE.wait(copied.get(g - 2))
                for t in range(TG):
                    ins = nc.tensor.transpose(psum[:, g % 2, t * P:(t + 1) * P], attended[:, g * TG + t, :], ident[:, :])
                copied[g] = A(lambda e: e.copy(oT[:, g % 2, :], psum[:, g % 2, :]), PE.mark(ins), oT_read.get(g - 2))
            if g >= 1:
                par = (g - 1) % 2
                y = flat[:, (4 + 2 * par) * BANK:(6 + 2 * par) * BANK].rearrange("p (t d) -> p t d", t=TG)
                PE.wait(copied[g - 1], y_read[par])
                for t in range(TG):
                    ins = nc.tensor.matmul(y[:, t, :], oT[:, par, t * P:(t + 1) * P], w_up, start=True, stop=True)
                oT_read[g - 1] = PE.mark(ins)
                for t in range(TG):
                    tile = (g - 1) * TG + t
                    y_read[par] = V(lambda e: e.tensor_tensor(inner[:, tile, :], y[:, t, :], inner[:, tile, :], ALU.add),
                                    oT_read[g - 1])
                    collect(inner, tile)
        mean_square_statistics()
        x_rows, y_rows = L3_rows
        for k in range(KD):
            V(lambda e: e.tensor_scalar(w_gate[:, k, :], w_gate[:, k, :], gain[:, 1, k:k + 1], None, ALU.mult))
        row_gain = small[:, 604:606]
        load(dma_e, row_gain, a["L3_ffn_g2"].rearrange("(p k) -> p k", k=KD))
        PE.wait(V.last())
        join()
        feed_input(inner, xnT, "plain")
        p, first_, second_, left = (wide[:, n] for n in range(4))
        V(lambda e: e.tensor_reduce(top_a[:, :], logits[:, :, :], AX.X, ALU.max))
        V(lambda e: e.tensor_tensor(p, logits[:, :, :], over(top_a[:, :]), ALU.subtract))
        A(lambda e: e.activation(p, p, ACT.Exp), V.last())
        V.wait(A.last())
        first_best(first_, p, top_a[:, :], order[:, :])
        V(lambda e: e.scalar_tensor_tensor(left, first_, -2.0, p, ALU.mult, ALU.add))
        first_best(second_, left, top_b[:, :], order[:, :])
        V(lambda e: e.tensor_tensor(rank[:, :], top_a[:, :], top_b[:, :], ALU.add))
        V(lambda e: e.reciprocal(rank[:, :], rank[:, :]))
        for k, top in enumerate((top_a, top_b)):
            V(lambda e: e.tensor_tensor(gates[:, :, k], top[:, :], rank[:, :], ALU.mult))
            V(lambda e: e.tensor_scalar(gates[:, :, k], gates[:, :, k], tanh_g[:, 7:8], None, ALU.mult))
        send = shared[:, 0:NT * D].rearrange("p (t d) -> p t d", t=NT)

        def residual():
            for t in range(NT):
                V(lambda e: e.scalar_tensor_tensor(x[:, t, :], inner[:, t, :], tanh_g[:, 7:8], x[:, t, :],
                                                   ALU.mult, ALU.add))
            SP.wait(V.last())

        def store(t, mark):
            load(dma_e, out[t // TB].rearrange("(t p) d -> p t d", p=P)[:, t % TB, :], x[:, t, :], mark)

        PE.wait(V.last())
        V.wait(PE.last())
        routed(2, 4, 6, x_rows, y_rows, a["L3_ffn_w1"], a["L3_ffn_w3"], a["L3_ffn_w2"], [first_, second_], row_gain,
               lambda k, t: gates[:, t, k:k + 1], send, lambda t: normalise(send[:, t, :], inner, t), residual, store)

    latent_block()


_TYPES = {"f": F32, "i": I32}


def rotation_tables():
    freq = np.float32(1.0) / np.float32(10000.0) ** (np.arange(0, HD3, 2, dtype=np.float32) / np.float32(HD3))
    angle = freq[:, None] * np.arange(S, dtype=np.float32)[None, :]
    rows = np.tile(np.repeat(angle, 2, axis=0), (H, 1))
    return np.cos(rows).astype(np.float32), np.sin(rows).astype(np.float32)


def kernel(**inputs):
    import concourse.bacc as bacc
    from concourse.bass_utils import run_bass_kernel_spmd

    nc = bacc.Bacc("TRN2", target_bir_lowering=False, num_devices=1)
    arrays, aps = {}, {}
    for name, value in inputs.items():
        v = np.ascontiguousarray(value)
        arrays["in_" + name] = v
        aps[name] = nc.dram_tensor("in_" + name, v.shape, _TYPES[v.dtype.kind], kind="ExternalInput").ap()
    for name, table in zip(("rope_cos", "rope_sin"), rotation_tables()):
        arrays["in_" + name] = table
        aps[name] = nc.dram_tensor("in_" + name, table.shape, F32, kind="ExternalInput").ap()
    out = nc.dram_tensor("out_0", (B, S, D), F32, kind="ExternalOutput").ap()
    program(nc, aps, out)
    r = run_bass_kernel_spmd(nc, [arrays], core_ids=[0])
    return r.results[0]["out_0"]
```
